# Optimizing a Trainium2 kernel written in Bass

```python
import numpy as np
import jax
import jax.numpy as jnp

def _softmax(x, axis=-1):
    return jax.nn.softmax(x, axis=axis)

def _gelu(x):
    return jax.nn.gelu(x, approximate=True)

def _silu(x):
    return jax.nn.silu(x)

def _sigmoid(x):
    return jax.nn.sigmoid(x)

def _layernorm(x, axis=-1, eps=1e-05):
    m = jnp.mean(x, axis=axis, keepdims=True)
    v = jnp.var(x, axis=axis, keepdims=True)
    return (x - m) / jnp.sqrt(v + eps)

def _scatter_add(tgt, idx, src, axis=0):
    return tgt.at[idx].add(src)

def _segment_sum(src, seg, n):
    return jax.ops.segment_sum(src, seg, n)
kernel_name = 'mk_decoder_postln_d1_seqx_r2_dade03'

def setup_inputs(seed: int=0):
    np.random.seed(seed)
    _w = jnp.asarray

    def _rec_inputs():
        import jax
        import jax.numpy as jnp
        _rk = jax.random.key(seed)
        x = 7.22e-05 + 1 * jax.random.normal(jax.random.fold_in(_rk, 1), (8, 512, 512), jnp.float32)
        _lenS = 512 - jax.random.randint(jax.random.fold_in(_rk, 7), (8,), 0, max(1, 512 // 4) + 1, jnp.int32)
        _lenS2 = 512 - jax.random.randint(jax.random.fold_in(_rk, 8), (8,), 0, max(1, 512 // 4) + 1, jnp.int32)
        _ctx_1024P = jax.random.normal(jax.random.fold_in(_rk, 11), (8, 16, 512), jnp.float32)
        _ctx_1024c = jax.random.dirichlet(jax.random.fold_in(_rk, 511), 0.3 * jnp.ones((16,), jnp.float32), (8, 512))
        _ctx_1024t = jnp.einsum('bsk,bkd->bsd', _ctx_1024c, _ctx_1024P)
        _ctx_1024t = _ctx_1024t * jax.lax.rsqrt(jnp.mean(jnp.square(_ctx_1024t)) + 1e-12) * 0.953939
        ctx_1024 = 4.13588e-05 + 0.999923 * (_ctx_1024t + 0.3 * jax.random.normal(jax.random.fold_in(_rk, 611), (8, 512, 512), jnp.float32))
        return (x, ctx_1024)
    x, ctx_1024 = _rec_inputs()

    def _L0_attn_setup():
        import jax, jax.numpy as jnp
        import numpy as np
        H = 16
        E = 512
        D = E // H
        M = 512
        EPS = 1e-12
        key = jax.random.key(seed)
        ks = jax.random.split(key, 12)
        s = 0.02
        B, S = (8, 512)
        return {'hidden_states': jax.random.normal(ks[0], (B, S, E), jnp.float32), 'Wq': jax.random.normal(ks[1], (E, E), jnp.float32) * s, 'bq': jnp.zeros((E,), jnp.float32), 'Wk': jax.random.normal(ks[2], (E, E), jnp.float32) * s, 'bk': jnp.zeros((E,), jnp.float32), 'Wv': jax.random.normal(ks[3], (E, E), jnp.float32) * s, 'bv': jnp.zeros((E,), jnp.float32), 'dist_emb': jax.random.normal(ks[4], (2 * M - 1, D), jnp.float32) * s, 'Wo': jax.random.normal(ks[5], (E, E), jnp.float32) * s, 'bo': jnp.zeros((E,), jnp.float32), 'ln_gamma': jnp.ones((E,), jnp.float32), 'ln_beta': jnp.zeros((E,), jnp.float32)}
    _L0_attn_all = _L0_attn_setup()
    _L0_attn_in = {k: v for k, v in _L0_attn_all.items() if k in ('Wq', 'bq', 'Wk', 'bk', 'Wv', 'bv', 'dist_emb', 'Wo', 'bo', 'ln_gamma', 'ln_beta')}
    del _L0_attn_all

    def _L0_xattn_setup():
        import jax, jax.numpy as jnp
        import numpy as np
        D_MODEL, D_K, D_V, H = (512, 64, 64, 16)
        B, N = (4, 1024)
        key = jax.random.key(seed)
        ks = jax.random.split(key, 11)
        s = 0.02
        return {'Q': jax.random.normal(ks[0], (B, N, D_MODEL), jnp.float32), 'K': jax.random.normal(ks[1], (B, N, D_MODEL), jnp.float32), 'V': jax.random.normal(ks[2], (B, N, D_MODEL), jnp.float32), 'Wq': jax.random.normal(ks[3], (H, D_MODEL, D_K), jnp.float32) * s, 'bq': jax.random.normal(ks[4], (H, D_K), jnp.float32) * s, 'Wk': jax.random.normal(ks[5], (H, D_MODEL, D_K), jnp.float32) * s, 'bk': jax.random.normal(ks[6], (H, D_K), jnp.float32) * s, 'Wv': jax.random.normal(ks[7], (H, D_MODEL, D_V), jnp.float32) * s, 'bv': jax.random.normal(ks[8], (H, D_V), jnp.float32) * s, 'Wo': jax.random.normal(ks[9], (H * D_V, D_MODEL), jnp.float32) * s, 'bo': jax.random.normal(ks[10], (D_MODEL,), jnp.float32) * s, 'apply_mask': 1}
    _L0_xattn_all = _L0_xattn_setup()
    _L0_xattn_in = {k: v for k, v in _L0_xattn_all.items() if k in ('Wq', 'bq', 'Wk', 'bk', 'Wv', 'bv', 'Wo', 'bo')}
    del _L0_xattn_all

    def _L0_ffn_setup():
        import jax, jax.numpy as jnp
        import numpy as np
        B, L, D = (4, 1024, 512)
        H = 16
        E = 16
        NS = 16
        S = NS // E
        F = 2048
        EPS = 1e-05

        def _layernorm(x, g, b):
            mu = jnp.mean(x, axis=-1, keepdims=True)
            var = jnp.mean(jnp.square(x - mu), axis=-1, keepdims=True)
            return (x - mu) * jax.lax.rsqrt(var + EPS) * g + b

        def _mha(q, k, v, Wq, bq, Wk, bk, Wv, bv, Wo, bo):
            Bq, Lq, Dm = q.shape
            dh = Dm // H
            qh = (q @ Wq + bq).reshape(Bq, Lq, H, dh)
            kh = (k @ Wk + bk).reshape(Bq, -1, H, dh)
            vh = (v @ Wv + bv).reshape(Bq, -1, H, dh)
            scores = jnp.einsum('bqhd,bkhd->bhqk', qh, kh) / jnp.asarray(np.sqrt(dh), q.dtype)
            attn = jax.nn.softmax(scores, axis=-1)
            out = jnp.einsum('bhqk,bkhd->bqhd', attn, vh).reshape(Bq, Lq, Dm)
            return out @ Wo + bo
        key = jax.random.key(seed)
        ks = jax.random.split(key, 32)
        s = 0.02
        d = {}
        d['x'] = jax.random.normal(ks[0], (B, L, D), jnp.float32)
        d['slot_query'] = jax.random.normal(ks[1], (1, NS, D), jnp.float32) * 0.01
        for i, nm in enumerate(['d_Wq', 'd_Wk', 'd_Wv', 'd_Wo']):
            d[nm] = jax.random.normal(ks[2 + i], (D, D), jnp.float32) * s
        for nm in ['d_bq', 'd_bk', 'd_bv', 'd_bo']:
            d[nm] = jnp.zeros((D,), jnp.float32)
        for i, nm in enumerate(['c_Wq', 'c_Wk', 'c_Wv', 'c_Wo']):
            d[nm] = jax.random.normal(ks[6 + i], (D, D), jnp.float32) * s
        for nm in ['c_bq', 'c_bk', 'c_bv', 'c_bo']:
            d[nm] = jnp.zeros((D,), jnp.float32)
        d['e_ln_g'] = jnp.ones((E, D), jnp.float32)
        d['e_ln_b'] = jnp.zeros((E, D), jnp.float32)
        d['e_W1'] = jax.random.normal(ks[10], (E, D, F), jnp.float32) * s
        d['e_b1'] = jnp.zeros((E, F), jnp.float32)
        d['e_Wg'] = jax.random.normal(ks[11], (E, D, F), jnp.float32) * s
        d['e_bg'] = jnp.zeros((E, F), jnp.float32)
        d['e_W2'] = jax.random.normal(ks[12], (E, F, D), jnp.float32) * s
        d['e_b2'] = jnp.zeros((E, D), jnp.float32)
        return d
    _L0_ffn_all = _L0_ffn_setup()
    _L0_ffn_in = {k: v for k, v in _L0_ffn_all.items() if k in ('slot_query', 'd_Wq', 'd_Wk', 'd_Wv', 'd_Wo', 'd_bq', 'd_bk', 'd_bv', 'd_bo', 'c_Wq', 'c_Wk', 'c_Wv', 'c_Wo', 'c_bq', 'c_bk', 'c_bv', 'c_bo', 'e_ln_g', 'e_ln_b', 'e_W1', 'e_b1', 'e_Wg', 'e_bg', 'e_W2', 'e_b2')}
    del _L0_ffn_all
    return {'x': x, 'ctx_1024': ctx_1024, 'L0_attn_Wq': _L0_attn_in['Wq'], 'L0_attn_bq': _L0_attn_in['bq'], 'L0_attn_Wk': _L0_attn_in['Wk'], 'L0_attn_bk': _L0_attn_in['bk'], 'L0_attn_Wv': _L0_attn_in['Wv'], 'L0_attn_bv': _L0_attn_in['bv'], 'L0_attn_dist_emb': _L0_attn_in['dist_emb'], 'L0_attn_Wo': _L0_attn_in['Wo'], 'L0_attn_bo': _L0_attn_in['bo'], 'L0_attn_ln_gamma': _L0_attn_in['ln_gamma'], 'L0_attn_ln_beta': _L0_attn_in['ln_beta'], 'L0_xattn_Wq': _L0_xattn_in['Wq'], 'L0_xattn_bq': _L0_xattn_in['bq'], 'L0_xattn_Wk': _L0_xattn_in['Wk'], 'L0_xattn_bk': _L0_xattn_in['bk'], 'L0_xattn_Wv': _L0_xattn_in['Wv'], 'L0_xattn_bv': _L0_xattn_in['bv'], 'L0_xattn_Wo': _L0_xattn_in['Wo'], 'L0_xattn_bo': _L0_xattn_in['bo'], 'L0_ffn_slot_query': _L0_ffn_in['slot_query'], 'L0_ffn_d_Wq': _L0_ffn_in['d_Wq'], 'L0_ffn_d_Wk': _L0_ffn_in['d_Wk'], 'L0_ffn_d_Wv': _L0_ffn_in['d_Wv'], 'L0_ffn_d_Wo': _L0_ffn_in['d_Wo'], 'L0_ffn_d_bq': _L0_ffn_in['d_bq'], 'L0_ffn_d_bk': _L0_ffn_in['d_bk'], 'L0_ffn_d_bv': _L0_ffn_in['d_bv'], 'L0_ffn_d_bo': _L0_ffn_in['d_bo'], 'L0_ffn_c_Wq': _L0_ffn_in['c_Wq'], 'L0_ffn_c_Wk': _L0_ffn_in['c_Wk'], 'L0_ffn_c_Wv': _L0_ffn_in['c_Wv'], 'L0_ffn_c_Wo': _L0_ffn_in['c_Wo'], 'L0_ffn_c_bq': _L0_ffn_in['c_bq'], 'L0_ffn_c_bk': _L0_ffn_in['c_bk'], 'L0_ffn_c_bv': _L0_ffn_in['c_bv'], 'L0_ffn_c_bo': _L0_ffn_in['c_bo'], 'L0_ffn_e_ln_g': _L0_ffn_in['e_ln_g'], 'L0_ffn_e_ln_b': _L0_ffn_in['e_ln_b'], 'L0_ffn_e_W1': _L0_ffn_in['e_W1'], 'L0_ffn_e_b1': _L0_ffn_in['e_b1'], 'L0_ffn_e_Wg': _L0_ffn_in['e_Wg'], 'L0_ffn_e_bg': _L0_ffn_in['e_bg'], 'L0_ffn_e_W2': _L0_ffn_in['e_W2'], 'L0_ffn_e_b2': _L0_ffn_in['e_b2']}

def reference(x, ctx_1024, L0_attn_Wq, L0_attn_bq, L0_attn_Wk, L0_attn_bk, L0_attn_Wv, L0_attn_bv, L0_attn_dist_emb, L0_attn_Wo, L0_attn_bo, L0_attn_ln_gamma, L0_attn_ln_beta, L0_xattn_Wq, L0_xattn_bq, L0_xattn_Wk, L0_xattn_bk, L0_xattn_Wv, L0_xattn_bv, L0_xattn_Wo, L0_xattn_bo, L0_ffn_slot_query, L0_ffn_d_Wq, L0_ffn_d_Wk, L0_ffn_d_Wv, L0_ffn_d_Wo, L0_ffn_d_bq, L0_ffn_d_bk, L0_ffn_d_bv, L0_ffn_d_bo, L0_ffn_c_Wq, L0_ffn_c_Wk, L0_ffn_c_Wv, L0_ffn_c_Wo, L0_ffn_c_bq, L0_ffn_c_bk, L0_ffn_c_bv, L0_ffn_c_bo, L0_ffn_e_ln_g, L0_ffn_e_ln_b, L0_ffn_e_W1, L0_ffn_e_b1, L0_ffn_e_Wg, L0_ffn_e_bg, L0_ffn_e_W2, L0_ffn_e_b2):
    import jax
    import jax.numpy as jnp

    def _L0_attn_ref(hidden_states, Wq, bq, Wk, bk, Wv, bv, dist_emb, Wo, bo, ln_gamma, ln_beta):
        import jax, jax.numpy as jnp
        import numpy as np
        H = 16
        E = 512
        D = E // H
        M = 512
        EPS = 1e-12
        B, S, _ = hidden_states.shape

        def heads(x):
            return x.reshape(B, S, H, D).transpose(0, 2, 1, 3)
        q = heads(hidden_states @ Wq + bq)
        k = heads(hidden_states @ Wk + bk)
        v = heads(hidden_states @ Wv + bv)
        scores = jnp.einsum('bhqd,bhkd->bhqk', q, k)
        pos_l = jnp.arange(S)[:, None]
        pos_r = jnp.arange(S)[None, :]
        dist_idx = pos_l - pos_r + M - 1
        pos_emb = dist_emb[dist_idx]
        rel_q = jnp.einsum('bhld,lrd->bhlr', q, pos_emb)
        rel_k = jnp.einsum('bhrd,lrd->bhlr', k, pos_emb)
        scores = (scores + rel_q + rel_k) / jnp.sqrt(jnp.asarray(D, scores.dtype))
        probs = jax.nn.softmax(scores, axis=-1)
        ctx = jnp.einsum('bhqk,bhkd->bhqd', probs, v)
        ctx = ctx.transpose(0, 2, 1, 3).reshape(B, S, E)
        h = ctx @ Wo + bo + hidden_states
        mu = jnp.mean(h, axis=-1, keepdims=True)
        var = jnp.mean(jnp.square(h - mu), axis=-1, keepdims=True)
        out = (h - mu) * jax.lax.rsqrt(var + EPS) * ln_gamma + ln_beta
        return out

    def _L0_xattn_ref(Q, K, V, Wq, bq, Wk, bk, Wv, bv, Wo, bo, apply_mask):
        import jax, jax.numpy as jnp
        import numpy as np
        D_MODEL, D_K, D_V, H = (512, 64, 64, 16)
        B, N = (4, 1024)
        q = jnp.einsum('bnd,hdk->bhnk', Q, Wq) + bq[None, :, None, :]
        k = jnp.einsum('bnd,hdk->bhnk', K, Wk) + bk[None, :, None, :]
        v = jnp.einsum('bnd,hdv->bhnv', V, Wv) + bv[None, :, None, :]
        scores = jnp.einsum('bhnk,bhmk->bhnm', q, k) / jnp.sqrt(jnp.asarray(D_K, q.dtype))
        if apply_mask:
            n = Q.shape[1]
            causal = jnp.tril(jnp.ones((n, n), dtype=bool))
            scores = jnp.where(causal[None, None], scores, -jnp.inf)
        weights = jax.nn.softmax(scores, axis=-1)
        out = jnp.einsum('bhnm,bhmv->bhnv', weights, v)
        out = out.transpose(0, 2, 1, 3).reshape(Q.shape[0], Q.shape[1], H * D_V)
        return out @ Wo + bo

    def _L0_ffn_ref(x, slot_query, d_Wq, d_Wk, d_Wv, d_Wo, d_bq, d_bk, d_bv, d_bo, c_Wq, c_Wk, c_Wv, c_Wo, c_bq, c_bk, c_bv, c_bo, e_ln_g, e_ln_b, e_W1, e_b1, e_Wg, e_bg, e_W2, e_b2):
        import jax, jax.numpy as jnp
        import numpy as np
        B, L, D = (4, 1024, 512)
        H = 16
        E = 16
        NS = 16
        S = NS // E
        F = 2048
        EPS = 1e-05

        def _layernorm(x, g, b):
            mu = jnp.mean(x, axis=-1, keepdims=True)
            var = jnp.mean(jnp.square(x - mu), axis=-1, keepdims=True)
            return (x - mu) * jax.lax.rsqrt(var + EPS) * g + b

        def _mha(q, k, v, Wq, bq, Wk, bk, Wv, bv, Wo, bo):
            Bq, Lq, Dm = q.shape
            dh = Dm // H
            qh = (q @ Wq + bq).reshape(Bq, Lq, H, dh)
            kh = (k @ Wk + bk).reshape(Bq, -1, H, dh)
            vh = (v @ Wv + bv).reshape(Bq, -1, H, dh)
            scores = jnp.einsum('bqhd,bkhd->bhqk', qh, kh) / jnp.asarray(np.sqrt(dh), q.dtype)
            attn = jax.nn.softmax(scores, axis=-1)
            out = jnp.einsum('bhqk,bkhd->bqhd', attn, vh).reshape(Bq, Lq, Dm)
            return out @ Wo + bo
        Bx = x.shape[0]
        q = jnp.broadcast_to(slot_query, (Bx, NS, D))
        o = q + _mha(q, x, x, d_Wq, d_bq, d_Wk, d_bk, d_Wv, d_bv, d_Wo, d_bo)
        os = o.reshape(Bx, E, S, D)
        h = _layernorm(os, e_ln_g[None, :, None, :], e_ln_b[None, :, None, :])
        u = jax.nn.silu(jnp.einsum('besd,edf->besf', h, e_W1) + e_b1[None, :, None, :])
        g = jax.nn.silu(jnp.einsum('besd,edf->besf', h, e_Wg) + e_bg[None, :, None, :])
        y = jnp.einsum('besf,efd->besd', u * g, e_W2) + e_b2[None, :, None, :]
        o = o + y.reshape(Bx, NS, D)
        out = _mha(x, o, o, c_Wq, c_bq, c_Wk, c_bk, c_Wv, c_bv, c_Wo, c_bo)
        return out
    x = _layernorm(x + _L0_attn_ref(x, L0_attn_Wq, L0_attn_bq, L0_attn_Wk, L0_attn_bk, L0_attn_Wv, L0_attn_bv, L0_attn_dist_emb, L0_attn_Wo, L0_attn_bo, L0_attn_ln_gamma, L0_attn_ln_beta), axis=-1)
    x = _layernorm(x + _L0_xattn_ref(x, ctx_1024, ctx_1024, L0_xattn_Wq, L0_xattn_bq, L0_xattn_Wk, L0_xattn_bk, L0_xattn_Wv, L0_xattn_bv, L0_xattn_Wo, L0_xattn_bo, 1), axis=-1)
    x = _layernorm(x + _L0_ffn_ref(x, L0_ffn_slot_query, L0_ffn_d_Wq, L0_ffn_d_Wk, L0_ffn_d_Wv, L0_ffn_d_Wo, L0_ffn_d_bq, L0_ffn_d_bk, L0_ffn_d_bv, L0_ffn_d_bo, L0_ffn_c_Wq, L0_ffn_c_Wk, L0_ffn_c_Wv, L0_ffn_c_Wo, L0_ffn_c_bq, L0_ffn_c_bk, L0_ffn_c_bv, L0_ffn_c_bo, L0_ffn_e_ln_g, L0_ffn_e_ln_b, L0_ffn_e_W1, L0_ffn_e_b1, L0_ffn_e_Wg, L0_ffn_e_bg, L0_ffn_e_W2, L0_ffn_e_b2), axis=-1)
    return x

_drawn_inputs = setup_inputs


def setup_inputs(seed=0):
    import zlib

    import numpy as np

    out = dict(_drawn_inputs(seed))
    spreads = {'L0_attn_bq': (0.0, 0.8),
     'L0_attn_bk': (0.0, 0.8),
     'L0_attn_bv': (0.0, 0.36),
     'L0_attn_bo': (0.0, 0.1),
     'L0_attn_ln_gamma': (1.0, 0.2),
     'L0_attn_ln_beta': (0.0, 0.1),
     'L0_ffn_d_bq': (0.0, 0.8),
     'L0_ffn_d_bk': (0.0, 2.0),
     'L0_ffn_d_bv': (0.0, 0.729),
     'L0_ffn_d_bo': (0.0, 0.357),
     'L0_ffn_c_bq': (0.0, 0.8),
     'L0_ffn_c_bk': (0.0, 2.0),
     'L0_ffn_c_bv': (0.0, 2.0),
     'L0_ffn_c_bo': (0.0, 2.0),
     'L0_ffn_e_ln_g': (1.0, 0.6),
     'L0_ffn_e_ln_b': (0.0, 0.8),
     'L0_ffn_e_b1': (0.0, 0.8),
     'L0_ffn_e_bg': (0.0, 0.8),
     'L0_ffn_e_b2': (0.0, 0.8)}
    factors = {'L0_attn_Wq': 8.0,
     'L0_attn_Wk': 8.0,
     'L0_attn_Wv': 8.0,
     'L0_attn_dist_emb': 8.0,
     'L0_xattn_Wq': 5.049,
     'L0_xattn_bq': 8.0,
     'L0_xattn_Wk': 5.046,
     'L0_xattn_bk': 200.0,
     'L0_xattn_bv': 4.674,
     'L0_xattn_bo': 2.771,
     'L0_ffn_slot_query': 8.0,
     'L0_ffn_d_Wq': 8.0,
     'L0_ffn_d_Wk': 8.0,
     'L0_ffn_d_Wv': 7.597,
     'L0_ffn_d_Wo': 4.842,
     'L0_ffn_c_Wq': 8.0,
     'L0_ffn_c_Wk': 8.0,
     'L0_ffn_e_W1': 8.0,
     'L0_ffn_e_Wg': 8.0,
     'L0_ffn_e_W2': 8.0}
    for name, (base, spread) in spreads.items():
        noise = np.random.default_rng([zlib.crc32(name.encode()), seed]).standard_normal(out[name].shape)
        drawn = base * np.exp(spread * noise) if base else spread * noise
        out[name] = jnp.asarray(drawn.astype(out[name].dtype))
    for name, factor in factors.items():
        out[name] = (out[name] * factor).astype(out[name].dtype)
    return out
```

```python
import concourse.bass as bass
from concourse import mybir
from contextlib import ExitStack

F32 = mybir.dt.float32
F32R = mybir.dt.float32r
ALU = mybir.AluOpType
ACT = mybir.ActivationFunctionType
AX = mybir.AxisListType

B, S, E = 8, 512, 512
P = 128
T4 = S // P
K4 = E // P
H = 16
D = E // H
HQ = P // D
QUADS = B * (H // HQ)
NT = HQ * T4
WIN = 640
SCALE_A = float(D) ** -0.5
BIG = 3.0e38


def self_attention(nc, dr, sems):
    with ExitStack() as ctx:
        def sb(name, shape, dt=F32):
            return ctx.enter_context(nc.sbuf_tensor(name, shape, dt))

        def ps(name, shape):
            return ctx.enter_context(nc.psum_tensor(name, shape, F32))

        sem = sems
        xT = sb("a_xT", [P, K4, S])
        wq, wk, wv = (sb(f"a_w{n}", [P, K4, P]) for n in "qkv")
        bqk = sb("a_bqk", [P, 2])
        bv = sb("a_bv", [P, P])
        split_q = sb("a_split_q", [P, 2, S], F32R)
        split_k = sb("a_split_k", [P, 2, S], F32R)
        qs = [sb(f"a_qs{i}", [P, HQ, S], F32R) for i in range(2)]
        ks = [sb(f"a_ks{i}", [P, HQ, S], F32R) for i in range(2)]
        eq = sb("a_eq", [P, 1024], F32R)
        ek = sb("a_ek", [P, 1024], F32R)
        emask = sb("a_emask", [P, 2])
        stage_q = [sb(f"a_stage_q{i}", [P, 2, WIN]) for i in range(2)]
        stage_k = [sb(f"a_stage_k{i}", [P, 2, WIN]) for i in range(2)]
        rq = [sb(f"a_rq{i}", [P, 2, S]) for i in range(4)]
        rk = [sb(f"a_rk{i}", [P, T4, S]) for i in range(4)]
        sc = [sb(f"a_sc{i}", [P, S]) for i in range(4)]
        mx = sb("a_mx", [P, 4])
        sm = sb("a_sm", [P, 4])
        inv = sb("a_inv", [P, 4])
        pt = sb("a_pt", [P, HQ, T4, S])
        v = [sb(f"a_v{i}", [P, T4, P]) for i in range(2)]
        cx = [sb(f"a_cx{i}", [P, S]) for i in range(2)]
        ident = sb("a_ident", [P, P])

        ps_q = ps("a_ps_q", [P, 2, 512])
        ps_k = ps("a_ps_k", [P, 2, 512])
        ps_s = [ps(f"a_ps_s{i}", [P, 512]) for i in range(2)]
        ps_t = ps("a_ps_t", [P, 512])
        ps_c = ps("a_ps_c", [P, 512])

        def band(i):
            return 384 - P * (i % T4)

        per_step = {3 + n: c for n, c in enumerate([1, 1, 2, 1, 2, 1, 2, 1, 2, 1, 2])}
        bands_at, nxt = {}, 0
        for t in range(NT - 2):
            c = per_step.get(t, 0)
            bands_at[t] = list(range(nxt, nxt + c))
            nxt += c
        assert nxt == NT

        block = ctx.enter_context(nc.Block())

        @block.sync
        def _(sp):
            sp.dma_start(ident[:, :], dr["ident"]).then_inc(sem["a_const_in"], 16)
            sp.dma_start(emask[:, :], dr["emask"]).then_inc(sem["a_const_in"], 16)
            for i, n in enumerate(["dist_rev", "dist_fwd"]):
                sp.dma_start(pt[:, i, 0:2, :].rearrange("p a b -> p (a b)"), dr[n]).then_inc(sem["a_const_in"], 16)

            def settle():
                sp.sem_inc(sem["a_sp_waited"], 1)

            def load(q):
                if not (isinstance(q, int) and q == 0):
                    sp.wait_ge(sem["a_qk_lo"], 2 * q)
                    settle()
                    sp.wait_ge(sem["a_v_out"], q)
                    settle()
                sp.dma_start(xT[:, :, :], dr["xT"](q)).then_inc(sem["a_in"], 16)
                for w, n in ((wq, "a_wq"), (wk, "a_wk"), (wv, "a_wv")):
                    sp.dma_start(w[:, :, :], dr[n](q)).then_inc(sem["a_in"], 16)
                sp.dma_start(bqk[:, :], dr["a_bqk"](q)).then_inc(sem["a_in"], 16)
                sp.dma_start(bv[:, :], dr["a_bv"](q)).then_inc(sem["a_in"], 16)

            def restack(q, par):
                sp.wait_ge(sem["a_qk_lo"], 2 * q + 2)
                settle()
                d = dr["a_split"]
                sq, sk = split_q[:, :, :].bitcast(F32), split_k[:, :, :].bitcast(F32)
                sp.dma_start(d[0].rearrange("(p a) n -> p a n", a=2), sq).then_inc(sem["a_split_out"], 16)
                sp.dma_start(d[1].rearrange("(p a) n -> p a n", a=2), sk).then_inc(sem["a_split_out"], 16)
                dk = d[2].rearrange("(p a) n -> p a n", a=2)
                sp.dma_start(dk[:, 0, :], sk[:, 1, :]).then_inc(sem["a_split_out"], 16)
                sp.dma_start(dk[:, 1, :], sk[:, 0, :]).then_inc(sem["a_split_out"], 16)
                sp.wait_ge(sem["a_split_out"], 64 * q + 64)
                settle()
                if not (isinstance(q, int) and q < 2):
                    sp.wait_ge(sem["a_summed"], NT * (q - 1))
                    settle()
                for dst, src, row in ((qs, 0, 0), (qs, 0, 64), (ks, 1, 0), (ks, 2, 64)):
                    sp.dma_start(dst[par][row:row + 64, :, :].bitcast(F32),
                                 d[src].rearrange("(h p) n -> p h n", p=64)).then_inc(sem[f"a_stack{par}"], 16)

            def write_pair(q, par, n):
                for kind, st in (("q", stage_q), ("k", stage_k)):
                    sp.wait_ge(sem[f"a_{kind}_staged"], NT * q + 2 * n + 2)
                    settle()
                    sp.dma_start(dr[f"a_band_{kind}"][par, 2 * n:2 * n + 2, :].rearrange("t (p n) -> p t n", p=P),
                                 st[n % 2][:, :, :]).then_inc(sem[f"a_{kind}_written{n % 2}"], 16)

            def shear(kind, par, t0, nt):
                h = dr[f"a_band_{kind}"]
                base = (par * NT + t0) * P * WIN + P - 1
                return bass.AP(tensor=h.tensor, offset=base, ap=[[WIN - 1, P], [P * WIN, nt], [1, S]])

            def read_k(q, par, j):
                i = HQ * q + j
                for n in range(2):
                    sp.wait_ge(sem[f"a_k_written{n}"], 16 * (i + 1))
                    settle()
                if not (isinstance(q, int) and q == 0):
                    sp.wait_ge(sem["a_summed"], T4 * (i - 3))
                    settle()
                sp.dma_start(rk[j][:, :, :], shear("k", par, T4 * j, T4)).then_inc(sem[f"a_rk{j}"], 16)

            def read_q(q, par, j, half):
                i = HQ * q + j
                sp.wait_ge(sem[f"a_q_written{half}"], 16 * (i + 1))
                settle()
                if not (isinstance(q, int) and q == 0 and j < 2):
                    sp.wait_ge(sem["a_summed"], T4 * (i - 2) + 2 * half + 2)
                    settle()
                slot = 2 * (j % 2) + half
                sp.dma_start(rq[slot][:, :, :], shear("q", par, T4 * j + 2 * half, 2)).then_inc(sem[f"a_rq{slot}"], 16)

            def store(q, par):
                sp.wait_ge(sem["a_cx_out"], q + 1)
                settle()
                sp.dma_start(dr["a_ctxT"](q), cx[par][:, :]).then_inc(sem[f"a_stored{par}"], 16)

            def sp_quad(g, par, first=False, last=False, loads=True):
                nx, np_ = g + 1, 1 - par
                read_k(g, par, 3)
                read_q(g, par, 1, 0)
                read_q(g, par, 1, 1)
                if not last:
                    restack(nx, np_)
                if not first:
                    store(g - 1, np_)
                if loads:
                    load(nx + 1)
                read_q(g, par, 2, 0)
                read_q(g, par, 2, 1)
                if last:
                    read_q(g, par, 3, 0)
                    read_q(g, par, 3, 1)
                    return
                write_pair(nx, np_, 0)
                write_pair(nx, np_, 1)
                read_k(nx, np_, 0)
                read_q(g, par, 3, 0)
                write_pair(nx, np_, 2)
                read_q(g, par, 3, 1)
                write_pair(nx, np_, 3)
                read_k(nx, np_, 1)
                write_pair(nx, np_, 4)
                write_pair(nx, np_, 5)
                read_q(nx, np_, 0, 0)
                write_pair(nx, np_, 6)
                read_k(nx, np_, 2)
                read_q(nx, np_, 0, 1)
                write_pair(nx, np_, 7)

            sp.sem_inc(sem["a_stored0"], 16)
            sp.sem_inc(sem["a_stored1"], 16)
            load(0)
            restack(0, 0)
            load(1)
            for n in range(NT // 2):
                write_pair(0, 0, n)
            for j in range(3):
                read_k(0, 0, j)
            read_q(0, 0, 0, 0)
            read_q(0, 0, 0, 1)
            sp_quad(0, 0, first=True)
            with sp.Fori(1, QUADS - 3, 2) as g:
                sp_quad(g, 1)
                sp_quad(g + 1, 0)
            sp_quad(QUADS - 3, 1)
            sp_quad(QUADS - 2, 0, loads=False)
            sp_quad(QUADS - 1, 1, last=True, loads=False)
            store(QUADS - 1, 1)
            sp.wait_ge(sem["a_stored0"], 16 * (QUADS // 2) + 16)
            sp.wait_ge(sem["a_stored1"], 16 * (QUADS // 2) + 16)

        @block.tensor
        def _(pe):
            def project(q, par):
                pe.wait_ge(sem["a_in"], 96 * q + 96)
                if not (isinstance(q, int) and q == 0):
                    pe.wait_ge(sem["a_q_staged"], NT * q)
                    pe.wait_ge(sem["a_k_staged"], NT * q)
                for i, w in enumerate((wq, wk)):
                    for k in range(K4):
                        mm = pe.matmul(ps_q[:, i, :], w[:, k, :], xT[:, k, :], start=(k == 0), stop=(k == K4 - 1))
                    mm.then_inc(sem["a_qk_ready"], 1)
                for t in range(T4):
                    for k in range(K4):
                        mm = pe.matmul(ps_k[:, 0, t * P:(t + 1) * P], xT[:, k, t * P:(t + 1) * P], wv[:, k, :],
                                       start=(k == 0), stop=(k == K4 - 1))
                mm.then_inc(sem["a_v_ready"], 1)

            def bands(q, par, i):
                h, t = i // T4, i % T4
                if i == 0:
                    pe.wait_ge(sem[f"a_stack{par}"], (q - par) * 32 + 64)
                w = band(i)
                for kind, src, table, out in (("q", qs, eq, ps_q), ("k", ks, ek, ps_k)):
                    if i:
                        pe.wait_ge(sem[f"a_{kind}_staged"], NT * q + i)
                    else:
                        pe.wait_ge(*((sem["a_qk_lo"], 2 * q + 2) if kind == "q" else (sem["a_v_out"], q + 1)))
                    for n in range(2):
                        mm = pe.matmul(out[:, n, 0:WIN // 2], src[par][:, h, t * P:(t + 1) * P],
                                       table[:, w + n * (WIN // 2):w + (n + 1) * (WIN // 2)], start=True, stop=True)
                    mm.then_inc(sem[f"a_{kind}_band"], 1)

            def score(q, par, i):
                h, t = i // T4, i % T4
                if t == 0:
                    pe.wait_ge(sem[f"a_rk{h}"], 16 * q + 16)
                if not (isinstance(q, int) and q == 0 and i < 2):
                    pe.wait_ge(sem["a_summed"], NT * q + i - 1)
                out = ps_s[i % 2]
                pe.matmul(out[:, :], qs[par][:, h, t * P:(t + 1) * P], ks[par][:, h, :], start=True, stop=False)
                for r in range(T4):
                    mm = pe.matmul(out[:, r * P:(r + 1) * P], rk[h][:, r, t * P:(t + 1) * P], ident[:, :],
                                   is_transpose=True, start=False, stop=(r == T4 - 1))
                mm.then_inc(sem["a_score"], 1)

            def turn(q, i):
                pe.wait_ge(sem["a_normed"], NT * q + i + 1)
                if not (isinstance(q, int) and q == 0 and i == 0):
                    pe.wait_ge(sem["a_pt_out"], NT * q + i)
                for r in range(T4):
                    mm = pe.transpose(ps_t[:, r * P:(r + 1) * P], sc[i % 4][:, r * P:(r + 1) * P], ident[:, :])
                mm.then_inc(sem["a_turned"], 1)

            def context(q, par):
                pe.wait_ge(sem["a_pt_out"], NT * q + NT)
                for r in range(T4):
                    for h in range(HQ):
                        mm = pe.matmul(ps_c[D * h:D * (h + 1), :], v[par][:, r, D * h:D * (h + 1)], pt[:, h, r, :],
                                       start=(r == 0), stop=(r == T4 - 1))
                mm.then_inc(sem["a_cx_ready"], 1)

            def pe_quad(g, par, first=False, last=False):
                if not last:
                    project(g + 1, 1 - par)
                if not first:
                    turn(g - 1, NT - 2)
                    turn(g - 1, NT - 1)
                score(g, par, 0)
                score(g, par, 1)
                if not first:
                    context(g - 1, 1 - par)
                for t in range(NT - 2):
                    score(g, par, t + 2)
                    if not last:
                        for i in bands_at[t]:
                            bands(g + 1, 1 - par, i)
                    turn(g, t)

            pe.wait_ge(sem["a_const_in"], 64)
            pe.wait_ge(sem["a_tables"], 2)
            project(0, 0)
            for i in range(NT):
                bands(0, 0, i)
            pe_quad(0, 0, first=True)
            with pe.Fori(1, QUADS - 1, 2) as g:
                pe_quad(g, 1)
                pe_quad(g + 1, 0)
            pe_quad(QUADS - 1, 1, last=True)
            turn(QUADS - 1, NT - 2)
            turn(QUADS - 1, NT - 1)
            context(QUADS - 1, 1)

        @block.scalar
        def _(act):
            def halves(q):
                if not (isinstance(q, int) and q == 0):
                    act.wait_ge(sem["a_split_out"], 64 * q)
                for i, dst in enumerate((split_q, split_k)):
                    act.wait_ge(sem["a_qk_ready"], 2 * q + i + 1)
                    act.activation(dst[:, 0, :], ps_q[:, i, :], ACT.Identity, bias=bqk[:, i:i + 1])\
                       .then_inc(sem["a_qk_hi"], 1)

            def stage(q, i):
                n = i // 2
                for kind, src, st in (("q", ps_q, stage_q), ("k", ps_k, stage_k)):
                    act.wait_ge(sem[f"a_{kind}_band"], NT * q + i + 1)
                    if not (isinstance(q, int) and q == 0 and n < 2):
                        act.wait_ge(sem[f"a_{kind}_written{n % 2}"], 16 * (HQ * q + n // 2))
                    act.activation(st[n % 2][:, i % 2, :].rearrange("p (a n) -> p a n", a=2),
                                   src[:, :, 0:WIN // 2], ACT.Copy).then_inc(sem[f"a_{kind}_staged"], 1)

            def softexp(q, i):
                act.wait_ge(sem["a_summed"], NT * q + i + 1)
                act.activation(sc[i % 4][:, :], sc[i % 4][:, :], ACT.Exp, bias=mx[:, i % 4:i % 4 + 1], scale=-1.0,
                               accum_out=sm[:, i % 4:i % 4 + 1]).then_inc(sem["a_exped"], 1)

            def act_quad(g, last=False):
                if not last:
                    halves(g + 1)
                softexp(g, 0)
                for t in range(NT - 2):
                    softexp(g, t + 1)
                    if not last:
                        for i in bands_at[t]:
                            stage(g + 1, i)
                softexp(g, NT - 1)

            halves(0)
            for i in range(NT):
                stage(0, i)
            act_quad(0)
            with act.Fori(1, QUADS - 1, 2) as g:
                act_quad(g)
                act_quad(g + 1)
            act_quad(QUADS - 1, last=True)

        @block.vector
        def _(dve):
            def tables():
                dve.wait_ge(sem["a_const_in"], 64)
                hi = qs[1][:, 0:2, :].rearrange("p a b -> p (a b)")
                n = 0
                for i, dst in enumerate((eq, ek)):
                    x = pt[:, i, 0:2, :].rearrange("p a b -> p (a b)")
                    lo = pt[:, i, 2:4, :].rearrange("p a b -> p (a b)")
                    mask = emask[:, i:i + 1]
                    dve.tensor_copy(hi, x).then_inc(sem["a_tab"], 1)
                    dve.wait_ge(sem["a_tab"], n + 1)
                    dve.tensor_tensor(lo, x, hi.bitcast(F32), ALU.subtract).then_inc(sem["a_tab"], 1)
                    dve.wait_ge(sem["a_tab"], n + 2)
                    dve.tensor_scalar(x, hi.bitcast(F32), mask, None, ALU.mult).then_inc(sem["a_tab"], 1)
                    dve.wait_ge(sem["a_tab"], n + 3)
                    dve.tensor_scalar(pt[:, 2 + i, 0:2, :].rearrange("p a b -> p (a b)"), lo, mask, None, ALU.mult)\
                       .then_inc(sem["a_tab"], 1)
                    dve.wait_ge(sem["a_tab"], n + 4)
                    dve.tensor_tensor(lo, lo, pt[:, 2 + i, 0:2, :].rearrange("p a b -> p (a b)"), ALU.subtract)\
                       .then_inc(sem["a_tab"], 1)
                    dve.wait_ge(sem["a_tab"], n + 5)
                    dve.tensor_tensor(dst[:, :], x, lo, ALU.add).then_inc(sem["a_tables"], 1)
                    n += 5

            def low_halves(q):
                for i, dst in enumerate((split_q, split_k)):
                    dve.wait_ge(sem["a_qk_hi"], 2 * q + i + 1)
                    ins = dve.scalar_tensor_tensor(dst[:, 1, :], ps_q[:, i, :], bqk[:, i:i + 1],
                                                   dst[:, 0, :].bitcast(F32), ALU.add, ALU.subtract)
                    ins.then_inc(sem["a_qk_lo"], 1)

            def v_out(q, par):
                dve.wait_ge(sem["a_v_ready"], q + 1)
                if not (isinstance(q, int) and q < 2):
                    dve.wait_ge(sem["a_cx_ready"], q - 1)
                for t in range(T4):
                    ins = dve.tensor_tensor(v[par][:, t, :], ps_k[:, 0, t * P:(t + 1) * P], bv[:, :], ALU.add)
                ins.then_inc(sem["a_v_out"], 1)

            def add_max(q, i):
                j, half = i // T4, (i // 2) % 2
                slot = 2 * (j % 2) + half
                dve.wait_ge(sem["a_score"], NT * q + i + 1)
                dve.wait_ge(sem[f"a_rq{slot}"], 16 * (2 * q + j // 2 + 1))
                if not (isinstance(q, int) and q == 0 and i < 4):
                    dve.wait_ge(sem["a_turned"], NT * q + i - 3)
                dve.sem_inc(sem["a_dve_waited"], 1)
                dve.tensor_tensor_reduce(out=sc[i % 4][:, :], in0=ps_s[i % 2][:, :], in1=rq[slot][:, i % 2, :],
                                         scale=-SCALE_A, scalar=BIG, op0=ALU.add, op1=ALU.min,
                                         accum_out=mx[:, i % 4:i % 4 + 1]).then_inc(sem["a_summed"], 1)

            def invert(q, i):
                dve.wait_ge(sem["a_exped"], NT * q + i + 1)
                dve.reciprocal(inv[:, i % 4:i % 4 + 1], sm[:, i % 4:i % 4 + 1]).then_inc(sem["a_inverse"], 1)

            def pt_out(q, i):
                h, t = i // T4, i % T4
                dve.wait_ge(sem["a_turned"], NT * q + i + 1)
                if i == 0 and not (isinstance(q, int) and q == 0):
                    dve.wait_ge(sem["a_cx_ready"], q)
                dve.tensor_copy(pt[:, h, :, t * P:(t + 1) * P],
                                ps_t[:, :].rearrange("p (r n) -> p r n", r=T4)).then_inc(sem["a_pt_out"], 1)

            def cx_out(q, par):
                dve.wait_ge(sem["a_cx_ready"], q + 1)
                dve.wait_ge(sem[f"a_stored{par}"], (q - par) * 8 + 16)
                dve.tensor_copy(cx[par][:, :], ps_c[:, :]).then_inc(sem["a_cx_out"], 1)

            def dve_quad(g, par, first=False, last=False):
                if not last:
                    low_halves(g + 1)
                if not first:
                    pt_out(g - 1, NT - 2)
                    pt_out(g - 1, NT - 1)
                add_max(g, 0)
                add_max(g, 1)
                if not first:
                    cx_out(g - 1, 1 - par)
                if not last:
                    v_out(g + 1, 1 - par)
                invert(g, 0)
                for t in range(NT - 2):
                    add_max(g, t + 2)
                    pt_out(g, t)
                    invert(g, t + 1)
                invert(g, NT - 1)

            tables()
            low_halves(0)
            v_out(0, 0)
            dve_quad(0, 0, first=True)
            with dve.Fori(1, QUADS - 1, 2) as g:
                dve_quad(g, 1)
                dve_quad(g + 1, 0)
            dve_quad(QUADS - 1, 1, last=True)
            pt_out(QUADS - 1, NT - 2)
            pt_out(QUADS - 1, NT - 1)
            cx_out(QUADS - 1, 1)

        @block.gpsimd
        def _(pool):
            def quad_norm(g):
                for i in range(NT):
                    pool.wait_ge(sem["a_inverse"], NT * g + i + 1)
                    pool.sem_inc(sem["a_pool_waited"], 1)
                    pool.tensor_scalar(sc[i % 4][:, :], sc[i % 4][:, :], inv[:, i % 4:i % 4 + 1], None, ALU.mult)\
                        .then_inc(sem["a_normed"], 1)

            with pool.Fori(0, QUADS) as g:
                quad_norm(g)


A_SEMS = (["a_dve_waited", "a_pool_waited", "a_sp_waited", "a_const_in", "a_in", "a_split_out", "a_stack0", "a_stack1", "a_q_staged", "a_k_staged",
           "a_q_written0", "a_q_written1", "a_k_written0", "a_k_written1", "a_cx_out", "a_stored0",
           "a_stored1", "a_qk_ready", "a_v_ready", "a_q_band", "a_k_band", "a_summed",
           "a_score", "a_normed", "a_pt_out", "a_turned", "a_cx_ready", "a_tables", "a_tab", "a_qk_hi", "a_qk_lo",
           "a_exped", "a_inverse", "a_v_out"] + [f"a_rk{i}" for i in range(4)] + [f"a_rq{i}" for i in range(4)])

UNITS = B * T4
EPS_ATTN, EPS = 1e-12, 1e-5


def project_norm(nc, dr, sem, z, chunks, affine):
    with ExitStack() as ctx:
        def sb(name, shape, dt=F32):
            return ctx.enter_context(nc.sbuf_tensor(z + name, shape, dt))

        def ps(name, shape):
            return ctx.enter_context(nc.psum_tensor(z + name, shape, F32))

        R = 4
        wo = sb("wo", [P, chunks, E])
        cT = [sb(f"cT{i}", [P, chunks, P]) for i in range(R)]
        x = [sb(f"x{i}", [P, E]) for i in range(R)]
        xb = [sb(f"xb{i}", [P, E]) for i in range(R)]
        xg = [sb(f"xg{i}", [P, E]) for i in range(R)] if affine else None
        h = [sb(f"h{i}", [P, E]) for i in range(R)]
        y = [sb(f"y{i}", [P, E]) for i in range(R)]
        yT = [sb(f"yT{i}", [P, K4, P]) for i in range(R)]
        st = [sb(f"st{i}", [P, 2, 16]) for i in range(R)]
        bo = sb("bo", [P, E])
        gamma = sb("gamma", [P, E]) if affine else None
        beta = sb("beta", [P, E]) if affine else None
        eps = sb("eps", [P, 2])
        ident = sb("ident", [P, P])
        ps_o = [ps(f"ps_o{i}", [P, 512]) for i in range(R)]
        ps_y = [ps(f"ps_y{i}", [P, 512]) for i in range(2)]

        const_in = 16 * (5 if affine else 3)
        rounds = (0, 1) if affine else (1,)

        def steps(e, step):
            for s in range(R):
                step(s, s)
            with e.Fori(R, UNITS - R, R) as s:
                for j in range(R):
                    step(s + j, j)
            for s in range(UNITS - R, UNITS + 3):
                step(s, s % R)

        def has(s, lag):
            return not isinstance(s, int) or 0 <= s - lag < UNITS

        def early(s, n):
            return isinstance(s, int) and s < n

        block = ctx.enter_context(nc.Block())

        @block.sync
        def _(sp):
            def settle():
                sp.sem_inc(sem[z + "sp_waited"], 1)

            def load(u, j):
                if not early(u, R):
                    sp.wait_ge(sem[z + "projected"], u - R + 1)
                    settle()
                    sp.wait_ge(sem[z + "biased"], u - R + 1)
                    settle()
                sp.dma_start(cT[j][:, :, :], dr[z + "cT"](u)).then_inc(sem[f"{z}in{j}"], 16)
                sp.dma_start(x[j][:, :], dr[z + "x"](u)).then_inc(sem[f"{z}in{j}"], 16)

            def store(u, j):
                sp.wait_ge(sem[z + "y"], u + 1)
                settle()
                sp.dma_start(dr[z + "y"](u), y[j][:, :]).then_inc(sem[f"{z}stored{j}"], 16)
                sp.wait_ge(sem[z + "yT"], u + 1)
                settle()
                sp.dma_start(dr[z + "yT"](u), yT[j][:, :, :]).then_inc(sem[f"{z}stored{j}"], 16)

            def step(s, j):
                if has(s, 0):
                    load(s, j)
                if has(s, 2):
                    store(s - 2, (j - 2) % R)

            for j in range(R):
                sp.sem_inc(sem[f"{z}stored{j}"], 32)
            c = sem[z + "const_in"]
            sp.dma_start(wo[:, :, :], dr[z + "wo"]).then_inc(c, 16)
            sp.dma_start(bo[:, :], dr[z + "bo"]).then_inc(c, 16)
            sp.dma_start(ident[:, :], dr["ident"]).then_inc(c, 16)
            if affine:
                sp.dma_start(gamma[:, :], dr["gamma"]).then_inc(c, 16)
                sp.dma_start(beta[:, :], dr["beta"]).then_inc(c, 16)
            steps(sp, step)
            for j in range(R):
                sp.wait_ge(sem[f"{z}stored{j}"], 32 * (UNITS // R) + 32)

        @block.tensor
        def _(pe):
            def project(u, j):
                pe.wait_ge(sem[f"{z}in{j}"], (u - j) * 8 + 32)
                if not early(u, R):
                    pe.wait_ge(sem[z + "summed"], u - R + 1)
                for k in range(chunks):
                    mm = pe.matmul(ps_o[j][:, :], cT[j][:, k, :], wo[:, k, :], start=(k == 0), stop=(k == chunks - 1))
                mm.then_inc(sem[z + "projected"], 1)

            def turn(u, j):
                pe.wait_ge(sem[z + "y"], u + 1)
                if not early(u, 2):
                    pe.wait_ge(sem[z + "yT"], u - 1)
                for k in range(K4):
                    mm = pe.transpose(ps_y[j % 2][:, k * P:(k + 1) * P], y[j][:, k * P:(k + 1) * P], ident[:, :])
                mm.then_inc(sem[z + "turned"], 1)

            def step(s, j):
                if has(s, 0):
                    project(s, j)
                if has(s, 2):
                    turn(s - 2, (j - 2) % R)

            pe.wait_ge(sem[z + "const_in"], const_in)
            steps(pe, step)

        @block.gpsimd
        def _(pool):
            def step(s, j):
                if not has(s, 0):
                    return
                pool.wait_ge(sem[f"{z}in{j}"], (s - j) * 8 + 32)
                if not early(s, R):
                    pool.wait_ge(sem[z + "summed"], s - R + 1)
                    if affine:
                        pool.wait_ge(sem[z + "shifted"], s - R + 1)
                pool.sem_inc(sem[z + "pool_waited"], 1)
                ins = pool.tensor_tensor(xb[j][:, :], x[j][:, :], bo[:, :], ALU.add)
                if affine:
                    ins.then_inc(sem[z + "biased_h"], 1)
                    ins = pool.tensor_tensor(xg[j][:, :], x[j][:, :], beta[:, :], ALU.add)
                ins.then_inc(sem[z + "biased"], 1)

            pool.wait_ge(sem[z + "const_in"], const_in)
            steps(pool, step)

        @block.vector
        def _(dve):
            def stats(u, j, r):
                dve.wait_ge(sem[z + ("shifted" if affine and r else "summed")], u + 1)
                dve.bn_stats(st[j][:, r, 0:6], h[j][:, :]).then_inc(sem[f"{z}bn{r}"], 1)
                dve.wait_ge(sem[f"{z}bn{r}"], u + 1)
                dve.sem_inc(sem[z + "dve_waited"], 1)
                dve.bn_aggr(st[j][:, r, 6:8], st[j][:, r, 0:6]).then_inc(sem[f"{z}var{r}"], 1)

            def scales(u, j, r):
                s_ = st[j]
                dve.wait_ge(sem[f"{z}std{r}"], u + 1)
                dve.reciprocal(s_[:, r, 9:10], s_[:, r, 8:9]).then_inc(sem[f"{z}inv{r}"], 1)
                dve.wait_ge(sem[f"{z}inv{r}"], u + 1)
                dve.scalar_tensor_tensor(s_[:, r, 10:11], s_[:, r, 6:7], -1.0, s_[:, r, 9:10], ALU.mult, ALU.mult)\
                   .then_inc(sem[f"{z}scales{r}"], 1)

            def add(u, j):
                dve.wait_ge(sem[z + "projected"], u + 1)
                dve.wait_ge(sem[z + ("biased_h" if affine else "biased")], u + 1)
                if not early(u, R):
                    dve.wait_ge(sem[z + "y"], u - R + 1)
                ins = dve.tensor_tensor(h[j][:, :], ps_o[j][:, :], xb[j][:, :], ALU.add)
                ins.then_inc(sem[z + "summed"], 1)

            def shift(u, j):
                dve.wait_ge(sem[z + "normed"], u + 1)
                dve.tensor_tensor(h[j][:, :], h[j][:, :], gamma[:, :], ALU.mult).then_inc(sem[z + "scaled"], 1)
                dve.wait_ge(sem[z + "biased"], u + 1)
                dve.wait_ge(sem[z + "scaled"], u + 1)
                dve.tensor_tensor(h[j][:, :], h[j][:, :], xg[j][:, :], ALU.add).then_inc(sem[z + "shifted"], 1)

            def turned_out(u, j):
                dve.wait_ge(sem[z + "turned"], u + 1)
                dve.wait_ge(sem[f"{z}stored{j}"], (u - j) * 8 + 32)
                dve.tensor_copy(yT[j][:, :, :], ps_y[j % 2][:, :].rearrange("p (k n) -> p k n", k=K4))\
                   .then_inc(sem[z + "yT"], 1)

            def step(s, j):
                i = (j - 1) % R
                if affine:
                    if has(s, 1):
                        shift(s - 1, i)
                        stats(s - 1, i, 1)
                    if has(s, 0):
                        add(s, j)
                        stats(s, j, 0)
                    if has(s, 1):
                        scales(s - 1, i, 1)
                    if has(s, 0):
                        scales(s, j, 0)
                else:
                    if has(s, 0):
                        add(s, j)
                        stats(s, j, 1)
                    if has(s, 1):
                        scales(s - 1, i, 1)
                if has(s, 2):
                    turned_out(s - 2, (j - 2) % R)

            for r in range(2):
                dve.memset(eps[:, r:r + 1], (EPS_ATTN, EPS)[r]).then_inc(sem[z + "eps"], 1)
            dve.wait_ge(sem[z + "const_in"], const_in)
            steps(dve, step)

        @block.scalar
        def _(act):
            def std(u, j, r):
                act.wait_ge(sem[f"{z}var{r}"], u + 1)
                act.activation(st[j][:, r, 8:9], st[j][:, r, 7:8], ACT.Sqrt, bias=eps[:, r:r + 1])\
                   .then_inc(sem[f"{z}std{r}"], 1)

            def norm(u, j, r):
                act.wait_ge(sem[f"{z}scales{r}"], u + 1)
                dst, done = (h[j], "normed") if r == 0 else (y[j], "y")
                if r == 1:
                    act.wait_ge(sem[f"{z}stored{j}"], (u - j) * 8 + 32)
                act.activation(dst[:, :], h[j][:, :], ACT.Identity, bias=st[j][:, r, 10:11],
                               scale=st[j][:, r, 9:10]).then_inc(sem[z + done], 1)

            def step(s, j):
                i = (j - 1) % R
                if has(s, 1):
                    if affine:
                        std(s - 1, i, 1)
                if has(s, 0):
                    std(s, j, rounds[0])
                if has(s, 1):
                    norm(s - 1, i, 1)
                if has(s, 0) and affine:
                    norm(s, j, 0)

            act.wait_ge(sem[z + "eps"], 2)
            steps(act, step)


def norm_sems(z):
    return [z + n for n in ["sp_waited", "pool_waited", "dve_waited", "const_in", "projected", "biased", "biased_h", "y", "yT",
                            "summed", "turned", "shifted", "scaled", "normed", "eps", "bn0", "bn1",
                            "var0", "var1", "std0", "std1", "inv0", "inv1", "scales0", "scales1"]
            + [f"in{j}" for j in range(4)] + [f"stored{j}" for j in range(4)]]

KD = 64
XH = 16
XW = XH * KD
PAIRS = B * (XH // 2)
NP = 2 * T4
XP = XH // 2
SCALE_B = float(KD) ** -0.5


def cross_attention(nc, dr, sem):
    with ExitStack() as ctx:
        def sb(name, shape, dt=F32):
            return ctx.enter_context(nc.sbuf_tensor(name, shape, dt))

        def ps(name, shape):
            return ctx.enter_context(nc.psum_tensor(name, shape, F32))

        xT = [sb(f"b_xT{i}", [P, K4, S]) for i in range(2)]
        cT = [sb(f"b_cT{i}", [P, K4, S]) for i in range(2)]
        w = {n: [sb(f"b_w{n}{i}", [P, K4, P]) for i in range(2)] for n in "qkv"}
        bqk = [sb(f"b_bqk{i}", [P, 2]) for i in range(2)]
        bv = [sb(f"b_bv{i}", [P, P]) for i in range(2)]
        qz = [sb(f"b_qz{i}", [P, 2, S]) for i in range(2)]
        kT = [sb(f"b_kT{i}", [P, S]) for i in range(2)]
        v = [sb(f"b_v{i}", [P, T4, P]) for i in range(2)]
        sc = [sb(f"b_sc{i}", [P, S]) for i in range(4)]
        mx = sb("b_mx", [P, 4])
        sm = sb("b_sm", [P, 4])
        inv = sb("b_inv", [P, 4])
        pt = [sb(f"b_pt{i}", [P, 2, T4, S]) for i in range(2)]
        cx = [sb(f"b_cx{i}", [P, S]) for i in range(2)]
        mask = sb("b_mask", [P, S])
        ident = sb("b_ident", [P, P])

        ps_p = ps("b_ps_p", [P, 2, 512])
        ps_v = ps("b_ps_v", [P, 512])
        ps_s = [ps(f"b_ps_s{i}", [P, 512]) for i in range(2)]
        ps_t = [ps(f"b_ps_t{i}", [P, 512]) for i in range(2)]
        ps_c = ps("b_ps_c", [P, 512])

        def width(i):
            return (i % T4 + 1) * P

        block = ctx.enter_context(nc.Block())

        @block.sync
        def _(sp):
            def settle():
                sp.sem_inc(sem["b_sp_waited"], 1)

            def load(n, par, first=False):
                if not first:
                    sp.wait_ge(sem["b_v_ready"], n - 1)
                    settle()
                    sp.wait_ge(sem["b_v_out"], n - 1)
                    settle()
                    sp.wait_ge(sem["b_qk_out"], 3 * (n - 1))
                    settle()
                s = sem[f"b_in{par}"]
                sp.dma_start(w["q"][par][:, :, :], dr["b_wq"](n)).then_inc(s, 16)
                sp.dma_start(xT[par][:, :, :], dr["x1T"](n)).then_inc(s, 16)
                sp.dma_start(w["k"][par][:, :, :], dr["b_wk"](n)).then_inc(s, 16)
                sp.dma_start(cT[par][:, :, :], dr["ctxT"](n)).then_inc(s, 16)
                sp.dma_start(w["v"][par][:, :, :], dr["b_wv"](n)).then_inc(s, 16)
                sp.dma_start(bqk[par][:, :], dr["b_bqk"](n)).then_inc(s, 16)
                sp.dma_start(bv[par][:, :], dr["b_bv"](n)).then_inc(s, 16)

            def store(n, par):
                sp.wait_ge(sem["b_cx_out"], n + 1)
                settle()
                sp.dma_start(dr["b_cxT"](n), cx[par][:, :]).then_inc(sem[f"b_stored{par}"], 16)

            for i in range(2):
                sp.sem_inc(sem[f"b_stored{i}"], 16)
            sp.dma_start(ident[:, :], dr["ident"]).then_inc(sem["b_const_in"], 16)
            sp.dma_start(mask[:, :], dr["mask"]).then_inc(sem["b_const_in"], 16)
            load(0, 0, first=True)
            load(1, 1, first=True)
            load(2, 0)
            load(3, 1)
            store(0, 0)
            with sp.Fori(4, PAIRS - 1, 2) as n:
                load(n, 0)
                store(n - 3, 1)
                load(n + 1, 1)
                store(n - 2, 0)
            store(PAIRS - 3, 1)
            store(PAIRS - 2, 0)
            store(PAIRS - 1, 1)
            for i in range(2):
                sp.wait_ge(sem[f"b_stored{i}"], 16 * (PAIRS // 2) + 16)

        @block.tensor
        def _(pe):
            def unit(n, par, u):
                if u == 0:
                    pe.wait_ge(sem[f"b_in{par}"], (n - par) * 56 + 112)
                if u in (0, 2):
                    if not (isinstance(n, int) and n == 0):
                        pe.wait_ge(sem["b_qk_out"], 3 * n - (1 if u == 0 else 0))
                if u == 4 and not (isinstance(n, int) and n == 0):
                    pe.wait_ge(sem["b_v_out"], n)
                if u < 4:
                    i, name, src = (0, "q", xT) if u < 2 else (1, "k", cT)
                    for k in (2 * (u % 2), 2 * (u % 2) + 1):
                        mm = pe.matmul(ps_p[:, i, :], w[name][par][:, k, :], src[par][:, k, :],
                                       start=(k == 0), stop=(k == K4 - 1))
                    if u % 2:
                        mm.then_inc(sem[f"b_{name}_ready"], 1)
                else:
                    for t in (2 * (u % 2), 2 * (u % 2) + 1):
                        for k in range(K4):
                            mm = pe.matmul(ps_v[:, t * P:(t + 1) * P], cT[par][:, k, t * P:(t + 1) * P],
                                           w["v"][par][:, k, :], start=(k == 0), stop=(k == K4 - 1))
                    if u == 5:
                        mm.then_inc(sem["b_v_ready"], 1)

            def score(n, par, i):
                h, t = i // T4, i % T4
                if i == 0:
                    pe.wait_ge(sem["b_qk_out"], 3 * n + 3)
                if not (isinstance(n, int) and n == 0 and i < 2):
                    pe.wait_ge(sem["b_summed"], NP * n + i - 1)
                pe.matmul(ps_s[i % 2][:, 0:width(i)], qz[par][:, h, t * P:(t + 1) * P], kT[par][:, 0:width(i)],
                          start=True, stop=True).then_inc(sem["b_score"], 1)

            def turn(n, i):
                pe.wait_ge(sem["b_normed"], NP * n + i + 1)
                if not (isinstance(n, int) and n == 0 and i < 2):
                    pe.wait_ge(sem["b_pt_out"], NP * n + i - 1)
                for r in range(i % T4 + 1):
                    mm = pe.transpose(ps_t[i % 2][:, r * P:(r + 1) * P], sc[i % 4][:, r * P:(r + 1) * P], ident[:, :])
                mm.then_inc(sem["b_turned"], 1)

            def context(n, par):
                pe.wait_ge(sem["b_pt_out"], NP * n + NP)
                for r in range(T4):
                    for h in range(2):
                        mm = pe.matmul(ps_c[KD * h:KD * (h + 1), r * P:S], v[par][:, r, KD * h:KD * (h + 1)],
                                       pt[par][:, h, r, r * P:S], start=(r == 0), stop=(r == T4 - 1))
                mm.then_inc(sem["b_cx_ready"], 1)

            def pe_pair(n, par, first=False, last=False):
                if not first:
                    turn(n - 1, NP - 2)
                    turn(n - 1, NP - 1)
                score(n, par, 0)
                score(n, par, 1)
                if not first:
                    context(n - 1, 1 - par)
                for t in range(NP - 2):
                    score(n, par, t + 2)
                    if not last:
                        unit(n + 1, 1 - par, t)
                    turn(n, t)

            pe.wait_ge(sem["b_const_in"], 32)
            for u in range(6):
                unit(0, 0, u)
            pe_pair(0, 0, first=True)
            with pe.Fori(1, PAIRS - 1, 2) as n:
                pe_pair(n, 1)
                pe_pair(n + 1, 0)
            pe_pair(PAIRS - 1, 1, last=True)
            turn(PAIRS - 1, NP - 2)
            turn(PAIRS - 1, NP - 1)
            context(PAIRS - 1, 1)

        @block.scalar
        def _(act):
            def q_out(n, par):
                act.wait_ge(sem["b_q_ready"], n + 1)
                for h in range(2):
                    r = slice(KD * h, KD * (h + 1))
                    act.activation(qz[par][r, h, :], ps_p[r, 0, :], ACT.Identity, bias=bqk[par][r, 0:1])\
                       .then_inc(sem["b_qk_out"], 1)

            def k_out(n, par):
                act.wait_ge(sem["b_k_ready"], n + 1)
                act.activation(kT[par][:, :], ps_p[:, 1, :], ACT.Identity, bias=bqk[par][:, 1:2])\
                   .then_inc(sem["b_qk_out"], 1)

            def softexp(n, i):
                act.wait_ge(sem["b_summed"], NP * n + i + 1)
                act.activation(sc[i % 4][:, 0:width(i)], sc[i % 4][:, 0:width(i)], ACT.Exp,
                               bias=mx[:, i % 4:i % 4 + 1], scale=-1.0,
                               accum_out=sm[:, i % 4:i % 4 + 1]).then_inc(sem["b_exped"], 1)

            def act_pair(n, par, last=False):
                softexp(n, 0)
                for t in range(NP - 2):
                    softexp(n, t + 1)
                    if not last and t == 2:
                        q_out(n + 1, 1 - par)
                    if not last and t == 4:
                        k_out(n + 1, 1 - par)
                softexp(n, NP - 1)

            act.wait_ge(sem["b_zeroed"], 2)
            q_out(0, 0)
            k_out(0, 0)
            act_pair(0, 0)
            with act.Fori(1, PAIRS - 1, 2) as n:
                act_pair(n, 1)
                act_pair(n + 1, 0)
            act_pair(PAIRS - 1, 1, last=True)

        @block.vector
        def _(dve):
            def v_out(n, par):
                dve.wait_ge(sem["b_v_ready"], n + 1)
                for t in range(T4):
                    ins = dve.tensor_tensor(v[par][:, t, :], ps_v[:, t * P:(t + 1) * P], bv[par][:, :], ALU.add)
                ins.then_inc(sem["b_v_out"], 1)

            def add_max(n, i):
                c = S - width(i)
                dve.wait_ge(sem["b_score"], NP * n + i + 1)
                if not (isinstance(n, int) and n == 0 and i < 4):
                    dve.wait_ge(sem["b_turned"], NP * n + i - 3)
                dve.sem_inc(sem["b_dve_waited"], 1)
                dve.tensor_tensor_reduce(out=sc[i % 4][:, 0:width(i)], in0=ps_s[i % 2][:, 0:width(i)],
                                         in1=mask[:, c:S], scale=-SCALE_B, scalar=BIG, op0=ALU.add, op1=ALU.min,
                                         accum_out=mx[:, i % 4:i % 4 + 1]).then_inc(sem["b_summed"], 1)

            def invert(n, i):
                dve.wait_ge(sem["b_exped"], NP * n + i + 1)
                dve.reciprocal(inv[:, i % 4:i % 4 + 1], sm[:, i % 4:i % 4 + 1]).then_inc(sem["b_inverse"], 1)

            def pt_out(n, par, i):
                h, t = i // T4, i % T4
                dve.wait_ge(sem["b_turned"], NP * n + i + 1)
                dve.tensor_copy(pt[par][:, h, 0:t + 1, t * P:(t + 1) * P],
                                ps_t[i % 2][:, 0:width(i)].rearrange("p (r n) -> p r n", n=P))\
                   .then_inc(sem["b_pt_out"], 1)

            def cx_out(n, par):
                dve.wait_ge(sem["b_cx_ready"], n + 1)
                dve.wait_ge(sem[f"b_stored{par}"], (n - par) * 8 + 16)
                dve.tensor_copy(cx[par][:, :], ps_c[:, :]).then_inc(sem["b_cx_out"], 1)

            def dve_pair(n, par, first=False, last=False):
                if not first:
                    pt_out(n - 1, 1 - par, NP - 2)
                    pt_out(n - 1, 1 - par, NP - 1)
                add_max(n, 0)
                add_max(n, 1)
                if not first:
                    cx_out(n - 1, 1 - par)
                invert(n, 0)
                for t in range(NP - 2):
                    add_max(n, t + 2)
                    pt_out(n, par, t)
                    invert(n, t + 1)
                if not last:
                    v_out(n + 1, 1 - par)
                invert(n, NP - 1)

            for i in range(2):
                dve.memset(qz[i][:, :, :], 0.0).then_inc(sem["b_zeroed"], 1)
            dve.wait_ge(sem["b_const_in"], 32)
            v_out(0, 0)
            dve_pair(0, 0, first=True)
            with dve.Fori(1, PAIRS - 1, 2) as n:
                dve_pair(n, 1)
                dve_pair(n + 1, 0)
            dve_pair(PAIRS - 1, 1, last=True)
            pt_out(PAIRS - 1, 1, NP - 2)
            pt_out(PAIRS - 1, 1, NP - 1)
            cx_out(PAIRS - 1, 1)

        @block.gpsimd
        def _(pool):
            def norm(n, i):
                pool.wait_ge(sem["b_inverse"], NP * n + i + 1)
                pool.sem_inc(sem["b_pool_waited"], 1)
                pool.tensor_scalar(sc[i % 4][:, 0:width(i)], sc[i % 4][:, 0:width(i)], inv[:, i % 4:i % 4 + 1], None,
                                   ALU.mult).then_inc(sem["b_normed"], 1)

            with pool.Fori(0, PAIRS) as n:
                for i in range(NP):
                    norm(n, i)


B_SEMS = (["b_dve_waited", "b_pool_waited", "b_sp_waited", "b_const_in", "b_in0", "b_in1", "b_v_ready", "b_q_ready",
           "b_k_ready", "b_qk_out", "b_v_out", "b_cx_out", "b_stored0", "b_stored1", "b_score", "b_summed", "b_exped",
           "b_inverse", "b_normed", "b_turned", "b_pt_out", "b_cx_ready", "b_zeroed"])

NS = 16
HS = H * NS
SB = NS * B
SCALE_F = float(D) ** -0.5


def loop(e, n, step, lag):
    for s in range(2):
        step(s, s)
    with e.Fori(2, n - 2, 2) as s:
        for j in range(2):
            step(s + j, j)
    for s in range(n - 2, n + lag):
        step(s, s % 2)


def inside(s, lag, n):
    return not isinstance(s, int) or 0 <= s - lag < n


def early(s, n):
    return isinstance(s, int) and s < n


def slot_attention(nc, dr, sem):
    with ExitStack() as ctx:
        def sb(name, shape, dt=F32):
            return ctx.enter_context(nc.sbuf_tensor("c_" + name, shape, dt))

        def ps(name, shape):
            return ctx.enter_context(nc.psum_tensor("c_" + name, shape, F32))

        wq, wkT, wv, wo = (sb(n, [P, K4, E]) for n in ("wq", "wkT", "wv", "wo"))
        sqT = sb("sqT", [P, K4, NS])
        cols = sb("cols", [P, 3, K4])
        slots = sb("slots", [P, E])
        bo, gamma, beta = (sb(n, [P, E]) for n in ("bo", "gamma", "beta"))
        ident = sb("ident", [P, P])
        qd = sb("qd", [P, K4, HQ, NS])
        a = sb("a", [P, K4, HS])
        cb = sb("cb", [P, 2])
        xT = [sb(f"xT{i}", [P, K4, S]) for i in range(2)]
        x = [sb(f"x{i}", [P, T4, E]) for i in range(2)]
        sc = [sb(f"sc{i}", [P, 2, S]) for i in range(2)]
        st = [sb(f"st{i}", [P, 2, 3]) for i in range(2)]
        pt = sb("pt", [P, T4, HS])
        yT = sb("yT", [P, B, K4, HS])
        cx = sb("cx", [P, K4, SB])
        o = sb("o", [P, E])
        h = sb("h", [P, E])
        hT = sb("hT", [P, K4, SB])
        ns = sb("ns", [P, 16])
        eps = sb("eps", [P, 1])

        ps_s = ps("ps_s", [P, 2, 512])
        ps_t = ps("ps_t", [P, 2, 512])
        ps_y = ps("ps_y", [P, 2, 512])
        ps_a = ps("ps_a", [P, 2, 512])

        block = ctx.enter_context(nc.Block())

        @block.sync
        def _(sp):
            def settle():
                sp.sem_inc(sem["c_sp_waited"], 1)

            def load(b, j):
                if not early(b, 2):
                    sp.wait_ge(sem["c_mixed"], b - 1)
                    settle()
                sp.dma_start(xT[j][:, :, :], dr["x2T"](b)).then_inc(sem[f"c_in{j}"], 16)
                sp.dma_start(x[j][:, :, :], dr["x2"](b)).then_inc(sem[f"c_in{j}"], 16)

            for tile, n in ((wq[:, :, :], "d_wq"), (sqT[:, :, :], "sqT"), (cols[:, :, :], "d_cols"),
                            (wkT[:, :, :], "d_wkT"), (wv[:, :, :], "d_wv"), (wo[:, :, :], "d_wo"),
                            (slots[:, :], "slots"), (bo[:, :], "d_bo"), (gamma[:, :], "e_g"), (beta[:, :], "e_b"),
                            (ident[:, :], "ident")):
                sp.dma_start(tile, dr[n]).then_inc(sem["c_const_in"], 16)
            loop(sp, B, lambda s, j: load(s, j) if inside(s, 0, B) else None, 0)
            sp.wait_ge(sem["c_o"], 2)
            sp.dma_start(dr["o1"], o[:, :]).then_inc(sem["c_stored"], 16)
            sp.wait_ge(sem["c_hT"], 1)
            sp.dma_start(dr["hT"], hT[:, :, :]).then_inc(sem["c_stored"], 16)
            sp.wait_ge(sem["c_stored"], 32)

        @block.tensor
        def _(pe):
            def scores(b, j):
                pe.wait_ge(sem[f"c_in{j}"], (b - j) * 16 + 32)
                if not early(b, 1):
                    pe.wait_ge(sem["c_scaled"], 2 * b)
                for t in range(2):
                    for k in range(K4):
                        mm = pe.matmul(ps_s[:, t, :], a[:, k, t * P:(t + 1) * P], xT[j][:, k, :],
                                       start=(k == 0), stop=(k == K4 - 1))
                    mm.then_inc(sem["c_scored"], 1)

            def mix(b, j):
                pe.wait_ge(sem["c_probs"], 2 * b + 2)
                if not early(b, 1):
                    pe.wait_ge(sem["c_pt"], 2 * b)
                for t in range(2):
                    for r in range(T4):
                        mm = pe.transpose(ps_t[:, t, r * P:(r + 1) * P], sc[j][:, t, r * P:(r + 1) * P], ident[:, :])
                    mm.then_inc(sem["c_turned"], 1)
                pe.wait_ge(sem["c_pt"], 2 * b + 2)
                if not early(b, 1):
                    pe.wait_ge(sem["c_yT"], b)
                for k in range(K4):
                    for r in range(T4):
                        mm = pe.matmul(ps_y[:, k // 2, (k % 2) * HS:(k % 2 + 1) * HS], x[j][:, r, k * P:(k + 1) * P],
                                       pt[:, r, :], start=(r == 0), stop=(r == T4 - 1))
                mm.then_inc(sem["c_mixed"], 1)

            pe.wait_ge(sem["c_const_in"], 16 * 11)
            for m in range(K4):
                for k in range(K4):
                    mm = pe.matmul(ps_a[:, 0, m * NS:(m + 1) * NS], wq[:, k, m * P:(m + 1) * P], sqT[:, k, :],
                                   start=(k == 0), stop=(k == K4 - 1))
            mm.then_inc(sem["c_q_ready"], 1)
            pe.wait_ge(sem["c_qd"], 17)
            for m in range(K4):
                mm = pe.matmul(ps_a[64 * (m % 2):64 * (m % 2) + 64, 1, m // 2:m // 2 + 1],
                               qd[:, m, :, :].rearrange("p h s -> p (h s)"), cols[:, 1, m:m + 1], start=True, stop=True)
            mm.then_inc(sem["c_cb_ready"], 1)
            for k in range(K4):
                for m in range(K4):
                    mm = pe.matmul(ps_t[:, k // 2, (k % 2) * HS + m * 64:(k % 2) * HS + (m + 1) * 64],
                                   wkT[:, m, k * P:(k + 1) * P], qd[:, m, :, :].rearrange("p h s -> p (h s)"),
                                   start=True, stop=True)
            mm.then_inc(sem["c_a_ready"], 1)
            pe.wait_ge(sem["c_a"], 1)

            def step(s, j):
                if inside(s, 0, B):
                    scores(s, j)
                if inside(s, 1, B):
                    mix(s - 1, 1 - j)

            loop(pe, B, step, 1)
            pe.wait_ge(sem["c_yT"], B)
            for m in range(K4):
                for k in range(K4):
                    for hh in range(HQ):
                        c = HQ * m + hh
                        mm = pe.matmul(ps_a[D * hh:D * (hh + 1), 0, m * SB:(m + 1) * SB], wv[:, k, c * D:(c + 1) * D],
                                       yT[:, :, k, c * NS:(c + 1) * NS].rearrange("p b s -> p s b"),
                                       start=(k == 0), stop=(k == K4 - 1))
            mm.then_inc(sem["c_cx_ready"], 1)
            pe.wait_ge(sem["c_cx"], 1)
            for m in range(K4):
                mm = pe.matmul(ps_a[:, 1, :], cx[:, m, :], wo[:, m, :], start=(m == 0), stop=(m == K4 - 1))
            mm.then_inc(sem["c_o_ready"], 1)
            pe.wait_ge(sem["c_h"], 3)
            for k in range(K4):
                mm = pe.transpose(ps_s[:, 0, k * P:(k + 1) * P], h[:, k * P:(k + 1) * P], ident[:, :])
            mm.then_inc(sem["c_hT_ready"], 1)

        @block.vector
        def _(dve):
            chain = [0]

            def link(ins):
                chain[0] += 1
                ins.then_inc(sem["c_chain"], 1)
                dve.wait_ge(sem["c_chain"], chain[0])

            dve.memset(qd[:, :, :, :], 0.0).then_inc(sem["c_qd"], 1)
            dve.memset(eps[:, :], EPS).then_inc(sem["c_eps"], 1)
            dve.wait_ge(sem["c_const_in"], 16 * 11)
            dve.wait_ge(sem["c_qd"], 1)
            dve.wait_ge(sem["c_q_ready"], 1)
            for m in range(K4):
                for hh in range(HQ):
                    r = slice(D * hh, D * (hh + 1))
                    dve.tensor_scalar(qd[r, m, hh, :], ps_a[r, 0, m * NS:(m + 1) * NS], cols[r, 0, m:m + 1], None,
                                      ALU.add).then_inc(sem["c_qd"], 1)
            dve.wait_ge(sem["c_cb_ready"], 1)
            dve.tensor_copy(cb[:, :], ps_a[:, 1, 0:2])
            dve.wait_ge(sem["c_a_ready"], 1)
            link(dve.tensor_copy(a[:, :, :].rearrange("p (u k) n -> p u (k n)", u=2), ps_t[:, :, :]))
            dve.sem_inc(sem["c_a"], 1)

            def soft(b, j):
                for t in range(2):
                    dve.wait_ge(sem["c_scored"], 2 * b + t + 1)
                    if not early(b, 2):
                        dve.wait_ge(sem["c_turned"], 2 * (b - 1))
                    dve.tensor_scalar(sc[j][:, t, :], ps_s[:, t, :], cb[:, t:t + 1], -SCALE_F, ALU.add, ALU.mult)\
                       .then_inc(sem["c_scaled"], 1)
                for t in range(2):
                    dve.wait_ge(sem["c_scaled"], 2 * b + t + 1)
                    dve.tensor_reduce(st[j][:, t, 0:1], sc[j][:, t, :], AX.X, ALU.min).then_inc(sem["c_max"], 1)
                for t in range(2):
                    dve.wait_ge(sem["c_exped"], 2 * b + t + 1)
                    dve.reciprocal(st[j][:, t, 2:3], st[j][:, t, 1:2]).then_inc(sem["c_inv"], 1)
                for t in range(2):
                    dve.wait_ge(sem["c_inv"], 2 * b + t + 1)
                    dve.tensor_scalar(sc[j][:, t, :], sc[j][:, t, :], st[j][:, t, 2:3], None, ALU.mult)\
                       .then_inc(sem["c_probs"], 1)

            def out(b, j):
                for t in range(2):
                    dve.wait_ge(sem["c_turned"], 2 * b + t + 1)
                    if not early(b, 1):
                        dve.wait_ge(sem["c_mixed"], b)
                    dve.tensor_copy(pt[:, :, t * P:(t + 1) * P], ps_t[:, t, :].rearrange("p (r n) -> p r n", r=T4))\
                       .then_inc(sem["c_pt"], 1)
                dve.wait_ge(sem["c_mixed"], b + 1)
                dve.tensor_copy(yT[:, b, :, :].rearrange("p (u k) n -> p u (k n)", u=2), ps_y[:, :, :])\
                   .then_inc(sem["c_yT"], 1)

            def step(s, j):
                if inside(s, 0, B):
                    soft(s, j)
                if inside(s, 1, B):
                    out(s - 1, 1 - j)

            loop(dve, B, step, 1)
            dve.wait_ge(sem["c_cx_ready"], 1)
            for m in range(K4):
                ins = dve.tensor_scalar(cx[:, m, :], ps_a[:, 0, m * SB:(m + 1) * SB], cols[:, 2, m:m + 1], None, ALU.add)
            ins.then_inc(sem["c_cx"], 1)
            link(dve.tensor_tensor(slots[:, :], slots[:, :], bo[:, :], ALU.add))
            dve.wait_ge(sem["c_o_ready"], 1)
            dve.tensor_tensor(o[:, :], ps_a[:, 1, :], slots[:, :], ALU.add).then_inc(sem["c_o"], 1)
            dve.wait_ge(sem["c_o"], 1)
            link(dve.bn_stats(ns[:, 0:6], o[:, :]))
            dve.bn_aggr(ns[:, 6:8], ns[:, 0:6]).then_inc(sem["c_o"], 1)
            dve.wait_ge(sem["c_std"], 1)
            link(dve.reciprocal(ns[:, 9:10], ns[:, 8:9]))
            dve.tensor_scalar(h[:, :], o[:, :], ns[:, 6:7], ns[:, 9:10], ALU.subtract, ALU.mult).then_inc(sem["c_h"], 1)
            dve.wait_ge(sem["c_h"], 1)
            dve.tensor_tensor(h[:, :], h[:, :], gamma[:, :], ALU.mult).then_inc(sem["c_h"], 1)
            dve.wait_ge(sem["c_h"], 2)
            dve.tensor_tensor(h[:, :], h[:, :], beta[:, :], ALU.add).then_inc(sem["c_h"], 1)
            dve.wait_ge(sem["c_hT_ready"], 1)
            dve.tensor_copy(hT[:, :, :].rearrange("p k n -> p (k n)"), ps_s[:, 0, :]).then_inc(sem["c_hT"], 1)

        @block.scalar
        def _(act):
            def step(b, j):
                for t in range(2):
                    act.wait_ge(sem["c_max"], 2 * b + t + 1)
                    act.activation(sc[j][:, t, :], sc[j][:, t, :], ACT.Exp, bias=st[j][:, t, 0:1], scale=-1.0,
                                   accum_out=st[j][:, t, 1:2]).then_inc(sem["c_exped"], 1)

            loop(act, B, step, 0)
            act.wait_ge(sem["c_eps"], 1)
            act.wait_ge(sem["c_o"], 2)
            act.activation(ns[:, 8:9], ns[:, 7:8], ACT.Sqrt, bias=eps[:, :]).then_inc(sem["c_std"], 1)


C_SEMS = ["c_" + n for n in ["sp_waited", "mixed", "const_in", "in0", "in1", "o", "stored", "hT", "scaled", "scored",
                             "probs", "pt", "turned", "yT", "q_ready", "qd", "cb_ready", "a_ready", "a", "cx_ready",
                             "cx", "o_ready", "h", "hT_ready", "chain", "eps", "max", "exped", "inv", "std"]]

F = 2048
FC = F // P
FQ = F // 512


def experts(nc, dr, sem):
    with ExitStack() as ctx:
        def sb(name, shape, dt=F32):
            return ctx.enter_context(nc.sbuf_tensor("d_" + name, shape, dt))

        def ps(name, shape):
            return ctx.enter_context(nc.psum_tensor("d_" + name, shape, F32))

        w1 = [sb(f"w1{i}", [P, K4, F]) for i in range(2)]
        wg = [sb(f"wg{i}", [P, K4, F]) for i in range(2)]
        w2 = [sb(f"w2{i}", [P, FC, E]) for i in range(2)]
        hT = sb("hT", [P, K4, SB + 24])
        hs = sb("hs", [P, K4, 32])
        bias = sb("bias", [P, NS, 2, FC])
        ident = sb("ident", [P, P])
        pre = sb("pre", [P, 2, 512])
        act_in = sb("act_in", [P, 2, FC, B])
        act_e = sb("act_e", [P, 2, FC, B])
        prod = sb("prod", [P, FC, B])
        y = sb("y", [32 + B, E])

        ps_u = ps("ps_u", [P, 2, 512])
        ps_t = ps("ps_t", [P, 2, 512])
        ps_y = ps("ps_y", [B, 512])

        block = ctx.enter_context(nc.Block())

        @block.sync
        def _(sp):
            def settle():
                sp.sem_inc(sem["d_sp_waited"], 1)

            def step(e, j):
                if not early(e, 2):
                    sp.wait_ge(sem["d_wide"], 2 * e - 3)
                    settle()
                sp.dma_start(w1[j][:, :, :], dr["w1"](e)).then_inc(sem[f"d_w1_in{j}"], 16)
                if not early(e, 2):
                    sp.wait_ge(sem["d_wide"], 2 * e - 2)
                    settle()
                sp.dma_start(wg[j][:, :, :], dr["wg"](e)).then_inc(sem[f"d_wg_in{j}"], 16)
                if not early(e, 2):
                    sp.wait_ge(sem["d_narrow"], e - 1)
                    settle()
                sp.dma_start(w2[j][:, :, :], dr["w2"](e)).then_inc(sem[f"d_w2_in{j}"], 16)

            sp.dma_start(hT[:, :, 0:SB], dr["hT"]).then_inc(sem["d_const_in"], 16)
            sp.dma_start(bias[:, :, :, :], dr["e_bias"]).then_inc(sem["d_const_in"], 16)
            sp.dma_start(ident[:, :], dr["ident"]).then_inc(sem["d_const_in"], 16)
            loop(sp, NS, step, 0)

        @block.tensor
        def _(pe):
            def step(e, j):
                pe.wait_ge(sem["d_hs"], e + 1)
                for i, w in enumerate((w1, wg)):
                    pe.wait_ge(sem[f"d_w{'1g'[i]}_in{j}"], (e - j) * 8 + 16)
                    if not early(e, 1):
                        pe.wait_ge(sem[("d_pre", "d_pre_g")[i]], e)
                    for k in range(K4):
                        for f in range(FQ):
                            mm = pe.matmul(ps_u[32 * f:32 * f + 32, i, :], hs[:, k, :],
                                           w[j][:, k, f * 512:(f + 1) * 512], start=(k == 0), stop=(k == K4 - 1))
                    mm.then_inc(sem["d_wide"], 1)
                for i in range(2):
                    pe.wait_ge(sem[("d_pre", "d_pre_g")[i]], e + 1)
                    if not early(e, 1):
                        pe.wait_ge(sem["d_in"], 2 * e - 1 + i)
                    for c in range(4):
                        mm = pe.transpose(ps_t[:, i, c * P:(c + 1) * P], pre[:, i, c * P:(c + 1) * P], ident[:, :])
                    mm.then_inc(sem["d_turned"], 1)
                pe.wait_ge(sem[f"d_w2_in{j}"], (e - j) * 8 + 16)
                pe.wait_ge(sem["d_prod"], e + 1)
                if not early(e, 1):
                    pe.wait_ge(sem["d_y"], e)
                for n in range(FC):
                    c, f = n // FQ, n % FQ
                    mm = pe.matmul(ps_y[:, :], prod[:, n, :], w2[j][:, 4 * f + c, :], start=(n == 0), stop=(n == FC - 1))
                mm.then_inc(sem["d_narrow"], 1)

            pe.wait_ge(sem["d_const_in"], 48)
            loop(pe, NS, step, 0)

        @block.vector
        def _(dve):
            def step(e, j):
                if not early(e, 1):
                    dve.wait_ge(sem["d_wide"], 2 * e)
                dve.tensor_copy(hs[:, :, :], hT[:, :, bass.ds(e * B, 32)]).then_inc(sem["d_hs"], 1)
                dve.wait_ge(sem["d_wide"], 2 * e + 2)
                if not early(e, 1):
                    dve.wait_ge(sem["d_turned"], 2 * e)
                dve.tensor_copy(pre[:, 1, :], ps_u[:, 1, :]).then_inc(sem["d_pre_g"], 1)
                for i in range(2):
                    dve.wait_ge(sem["d_turned"], 2 * e + i + 1)
                    dve.tensor_tensor(act_in[:, i, :, :],
                                      ps_t[:, i, :].rearrange("p (n r) -> p n r", r=32)[:, :, 0:B],
                                      bias[:, e, i, :].unsqueeze(2).to_broadcast([P, FC, B]), ALU.add)\
                       .then_inc(sem["d_in"], 1)
                dve.wait_ge(sem["d_exp"], e + 1)
                dve.tensor_scalar(act_e[:, :, :, :], act_e[:, :, :, :], 1.0, None, ALU.add).then_inc(sem["d_one"], 1)
                dve.wait_ge(sem["d_one"], e + 1)
                dve.reciprocal(act_e[:, :, :, :], act_e[:, :, :, :]).then_inc(sem["d_inv"], 1)
                dve.wait_ge(sem["d_inv"], e + 1)
                dve.tensor_tensor(act_e[:, :, :, :], act_e[:, :, :, :], act_in[:, :, :, :], ALU.mult)\
                   .then_inc(sem["d_silu"], 1)
                dve.wait_ge(sem["d_silu"], e + 1)
                if not early(e, 1):
                    dve.wait_ge(sem["d_narrow"], e)
                dve.tensor_tensor(prod[:, :, :], act_e[:, 0, :, :], act_e[:, 1, :, :], ALU.mult)\
                   .then_inc(sem["d_prod"], 1)
                dve.wait_ge(sem["d_narrow"], e + 1)
                if not early(e, 2):
                    dve.wait_ge(sem[f"d_stored{j}"], (e - j) * 8)
                dve.tensor_copy(y[32 * j:32 * j + B, :], ps_y[:, :]).then_inc(sem["d_y"], 1)

            dve.memset(hT[:, :, SB:SB + 24], 0.0).then_inc(sem["d_pad"], 1)
            dve.wait_ge(sem["d_pad"], 1)
            dve.wait_ge(sem["d_const_in"], 48)
            loop(dve, NS, step, 0)

        @block.scalar
        def _(act):
            def step(e, j):
                act.wait_ge(sem["d_wide"], 2 * e + 1)
                if not early(e, 1):
                    act.wait_ge(sem["d_turned"], 2 * e)
                act.activation(pre[:, 0, :], ps_u[:, 0, :], ACT.Copy).then_inc(sem["d_pre"], 1)
                act.wait_ge(sem["d_in"], 2 * e + 2)
                if not early(e, 1):
                    act.wait_ge(sem["d_prod"], e)
                act.activation(act_e[:, :, :, :], act_in[:, :, :, :], ACT.Exp, scale=-1.0).then_inc(sem["d_exp"], 1)

            loop(act, NS, step, 0)

        @block.gpsimd
        def _(pool):
            def step(e, j):
                pool.wait_ge(sem["d_y"], e + 1)
                pool.sem_inc(sem["d_pool_waited"], 1)
                pool.dma_start(dr["y"](e), y[32 * j:32 * j + B, :]).then_inc(sem[f"d_stored{j}"], 16)

            loop(pool, NS, step, 0)
            for j in range(2):
                pool.wait_ge(sem[f"d_stored{j}"], 8 * NS)


D_SEMS = ["d_" + n for n in ["sp_waited", "pool_waited", "wide", "narrow", "w1_in0", "w1_in1", "wg_in0", "wg_in1",
                             "w2_in0", "w2_in1", "const_in", "hs", "pre", "pre_g", "in", "turned", "prod", "y", "exp",
                             "one", "inv", "silu", "stored0", "stored1", "pad"]]


def slots_to_tokens(nc, dr, sem):
    with ExitStack() as ctx:
        def sb(name, shape, dt=F32):
            return ctx.enter_context(nc.sbuf_tensor("e_" + name, shape, dt))

        def ps(name, shape):
            return ctx.enter_context(nc.psum_tensor("e_" + name, shape, F32))

        wqT, wk, wv, wo = (sb(n, [P, K4, E]) for n in ("wqT", "wk", "wv", "wo"))
        cols = sb("cols", [P, 3, K4])
        bo = sb("bo", [P, E])
        ident = sb("ident", [P, P])
        o, y, b2 = (sb(n, [P, E]) for n in ("o", "y", "b2"))
        oT = sb("oT", [P, K4, SB])
        kd, vd = (sb(n, [P, K4, B, HQ, NS]) for n in ("kd", "vd"))
        bq = sb("bq", [P, K4, P])
        a = sb("a", [P, K4, B, K4, HQ * NS])
        cb = sb("cb", [P, B, K4, HQ * NS])
        vo = sb("vo", [P, B, 2, E])
        xT = [sb(f"xT{i}", [P, K4, S]) for i in range(2)]
        x = [sb(f"x{i}", [P, T4, E]) for i in range(2)]
        h = [sb(f"h{i}", [P, T4, E]) for i in range(2)]
        sc = [sb(f"sc{i}", [P, T4, HS]) for i in range(2)]
        mx, sm, inv = (sb(n, [P, T4 * H]) for n in ("mx", "sm", "inv"))
        pt = sb("pt", [P, 2, S])
        st = [sb(f"st{i}", [P, T4, 16]) for i in range(2)]
        eps = sb("eps", [P, 1])

        ps_s = ps("ps_s", [P, 2, 512])
        ps_t = ps("ps_t", [P, 2, 512])
        ps_o = [ps(f"ps_o{i}", [P, 2, 512]) for i in range(2)]

        const_in = 16 * 10
        block = ctx.enter_context(nc.Block())

        @block.sync
        def _(sp):
            def settle():
                sp.sem_inc(sem["e_sp_waited"], 1)

            def load(b, j):
                if not early(b, 2):
                    sp.wait_ge(sem["e_scored"], b - 1)
                    settle()
                    sp.wait_ge(sem["e_xb"], b - 1)
                    settle()
                sp.dma_start(xT[j][:, :, :], dr["x2T"](b)).then_inc(sem[f"e_in{j}"], 16)
                sp.dma_start(x[j][:, :, :], dr["x2"](b)).then_inc(sem[f"e_in{j}"], 16)

            def store(b, j):
                sp.wait_ge(sem["e_normed"], b + 1)
                settle()
                sp.dma_start(dr["out"](b), h[j][:, :, :]).then_inc(sem[f"e_stored{j}"], 16)

            def step(s, j):
                if inside(s, 0, B):
                    load(s, j)
                if inside(s, 1, B):
                    store(s - 1, 1 - j)

            for j in range(2):
                sp.sem_inc(sem[f"e_stored{j}"], 16)
            for tile, n in ((o[:, :], "o1"), (y[:, :], "y_all"), (b2[:, :], "e_b2"), (ident[:, :], "ident"),
                            (wk[:, :, :], "c_wk"), (wv[:, :, :], "c_wv"), (cols[:, :, :], "c_cols"),
                            (wqT[:, :, :], "c_wqT"), (wo[:, :, :], "c_wo"), (bo[:, :], "c_bo")):
                sp.dma_start(tile, dr[n]).then_inc(sem["e_const_in"], 16)
            loop(sp, B, step, 1)
            for j in range(2):
                sp.wait_ge(sem[f"e_stored{j}"], 8 * B + 16)

        rounds = [("a", k, m) for k in range(K4) for m in (0, 2)] + [("cb", 0, m) for m in (0, 2)]\
            + [("vo", b, 0) for b in range(B)]

        @block.tensor
        def _(pe):
            pe.wait_ge(sem["e_const_in"], const_in)
            pe.wait_ge(sem["e_o"], 2)
            for k in range(K4):
                mm = pe.transpose(ps_t[:, 0, k * P:(k + 1) * P], o[:, k * P:(k + 1) * P], ident[:, :])
            mm.then_inc(sem["e_oT_ready"], 1)
            pe.wait_ge(sem["e_oT"], 1)
            for i, w in enumerate((wk, wv)):
                for m in range(K4):
                    for k in range(K4):
                        mm = pe.matmul(ps_s[:, i, m * SB:(m + 1) * SB], w[:, k, m * P:(m + 1) * P], oT[:, k, :],
                                       start=(k == 0), stop=(k == K4 - 1))
                mm.then_inc(sem["e_kv_ready"], 1)
            for r, (kind, n, m) in enumerate(rounds):
                if r == 0:
                    pe.wait_ge(sem["e_kd"], 2 + HQ * K4)
                elif kind == "cb":
                    pe.wait_ge(sem["e_bq"], K4)
                elif kind == "vo" and n == 0:
                    pe.wait_ge(sem["e_kd"], 2 + 2 * HQ * K4)
                if r >= 2:
                    pe.wait_ge(sem[f"e_folded{r % 2}"], r // 2)
                for i in range(2):
                    if kind == "a":
                        mm = pe.matmul(ps_o[r % 2][:, i, :], wqT[:, m + i, n * P:(n + 1) * P],
                                       kd[:, m + i, :, :, :].rearrange("p b h s -> p (b h s)"), start=True, stop=True)
                    elif kind == "cb":
                        mm = pe.matmul(ps_o[r % 2][:, i, :], bq[:, m + i, :],
                                       kd[:, m + i, :, :, :].rearrange("p b h s -> p (b h s)"), start=True, stop=True)
                    else:
                        for c in range(2):
                            mm = pe.matmul(ps_o[r % 2][64 * c:64 * c + 64, i, :],
                                           vd[:, 2 * i + c, n, :, :].rearrange("p h s -> p (h s)"),
                                           wo[:, 2 * i + c, :], start=True, stop=True)
                mm.then_inc(sem["e_fold"], 1)

            def scores(b, j):
                pe.wait_ge(sem[f"e_in{j}"], (b - j) * 16 + 32)
                if not early(b, 1):
                    pe.wait_ge(sem["e_biased"], b)
                for t in range(T4):
                    for k in range(K4):
                        mm = pe.matmul(ps_s[:, t // 2, (t % 2) * HS:(t % 2 + 1) * HS], xT[j][:, k, t * P:(t + 1) * P],
                                       a[:, k, b, :, :].rearrange("p m n -> p (m n)"),
                                       start=(k == 0), stop=(k == K4 - 1))
                mm.then_inc(sem["e_scored"], 1)

            def turn(b, j):
                pe.wait_ge(sem["e_probs"], b + 1)
                if not early(b, 1):
                    pe.wait_ge(sem["e_pt"], b)
                for i in range(2):
                    for t in range(T4):
                        mm = pe.transpose(ps_t[:, i, t * P:(t + 1) * P], sc[j][:, t, i * P:(i + 1) * P], ident[:, :])
                mm.then_inc(sem["e_turned"], 1)

            def mix(b, j):
                pe.wait_ge(sem["e_pt"], b + 1)
                if not early(b, 1):
                    pe.wait_ge(sem["e_summed"], b)
                for t in range(T4):
                    for i in range(2):
                        mm = pe.matmul(ps_o[t // 2][:, t % 2, :], pt[:, i, t * P:(t + 1) * P], vo[:, b, i, :],
                                       start=(i == 0), stop=(i == 1))
                mm.then_inc(sem["e_mixed"], 1)

            def step(s, j):
                if inside(s, 1, B):
                    turn(s - 1, 1 - j)
                if inside(s, 0, B):
                    scores(s, j)
                if inside(s, 1, B):
                    mix(s - 1, 1 - j)

            for j in range(2):
                pe.wait_ge(sem[f"e_folded{j}"], len(rounds) // 2)
            loop(pe, B, step, 1)

        def fold_out(e, parity, copy):
            for r, (kind, n, m) in enumerate(rounds):
                if r % 2 != parity:
                    continue
                e.wait_ge(sem["e_fold"], r + 1)
                src = ps_o[parity][:, :, :]
                if kind == "vo":
                    ins = copy(vo[:, n, :, :], src)
                else:
                    dst = a[:, n, :, m:m + 2, :] if kind == "a" else cb[:, :, m:m + 2, :]
                    for i in range(2):
                        ins = copy(dst[:, :, i, :], src[:, i, :].rearrange("p (b n) -> p b n", b=B))
                ins.then_inc(sem[f"e_folded{parity}"], 1)

        @block.vector
        def _(dve):
            dve.memset(kd[:, :, :, :, :].rearrange("p m b h s -> p (m b h s)"), 0.0).then_inc(sem["e_kd"], 1)
            dve.memset(vd[:, :, :, :, :].rearrange("p m b h s -> p (m b h s)"), 0.0).then_inc(sem["e_kd"], 1)
            dve.memset(eps[:, :], EPS).then_inc(sem["e_eps"], 1)
            dve.wait_ge(sem["e_const_in"], const_in)
            dve.tensor_tensor(o[:, :], o[:, :], y[:, :], ALU.add).then_inc(sem["e_o"], 1)
            dve.wait_ge(sem["e_o"], 1)
            dve.tensor_tensor(o[:, :], o[:, :], b2[:, :], ALU.add).then_inc(sem["e_o"], 1)
            for m in range(K4):
                dve.tensor_copy(bq[:, m, :], cols[:, 0, m:m + 1].to_broadcast([P, P])).then_inc(sem["e_bq"], 1)
            dve.wait_ge(sem["e_oT_ready"], 1)
            dve.tensor_copy(oT[:, :, :].rearrange("p k n -> p (k n)"), ps_t[:, 0, :]).then_inc(sem["e_oT"], 1)
            dve.wait_ge(sem["e_kd"], 2)
            for i, dst in enumerate((kd, vd)):
                dve.wait_ge(sem["e_kv_ready"], i + 1)
                for m in range(K4):
                    for hh in range(HQ):
                        r = slice(D * hh, D * (hh + 1))
                        dve.tensor_scalar(dst[r, m, :, hh, :],
                                          ps_s[r, i, m * SB:(m + 1) * SB].rearrange("p (s b) -> p b s", b=B),
                                          cols[r, 1 + i, m:m + 1], None, ALU.add).then_inc(sem["e_kd"], 1)
            fold_out(dve, 0, lambda d, s: dve.tensor_copy(d, s))

            def groups(j):
                return sc[j][:, :, :].rearrange("p t (h s) -> p (t h) s", s=NS)

            def soft_in(b, j):
                dve.wait_ge(sem["e_scored"], b + 1)
                if not early(b, 2):
                    dve.wait_ge(sem["e_turned"], b - 1)
                for u in range(2):
                    ins = dve.tensor_tensor(sc[j][:, 2 * u:2 * u + 2, :],
                                            ps_s[:, u, :].rearrange("p (t n) -> p t n", t=2),
                                            cb[:, b, :, :].rearrange("p m n -> p (m n)").unsqueeze(1)
                                            .to_broadcast([P, 2, HS]), ALU.add)
                ins.then_inc(sem["e_biased"], 1)
                dve.wait_ge(sem["e_biased"], b + 1)
                dve.tensor_reduce(mx[:, :], groups(j), AX.X, ALU.max).then_inc(sem["e_max"], 1)
                dve.wait_ge(sem["e_max"], b + 1)
                dve.tensor_tensor(groups(j), groups(j), mx[:, :].unsqueeze(2).to_broadcast([P, T4 * H, NS]),
                                  ALU.subtract).then_inc(sem["e_shifted"], 1)

            def soft_out(b, j):
                dve.wait_ge(sem["e_exped"], b + 1)
                dve.tensor_reduce(sm[:, :], groups(j), AX.X, ALU.add).then_inc(sem["e_sum"], 1)
                dve.wait_ge(sem["e_sum"], b + 1)
                dve.reciprocal(inv[:, :], sm[:, :]).then_inc(sem["e_inv"], 1)
                dve.wait_ge(sem["e_inv"], b + 1)
                dve.tensor_tensor(groups(j), groups(j), inv[:, :].unsqueeze(2).to_broadcast([P, T4 * H, NS]),
                                  ALU.mult).then_inc(sem["e_probs"], 1)

            def norm_in(b, j):
                dve.wait_ge(sem["e_mixed"], b + 1)
                dve.wait_ge(sem["e_xb"], b + 1)
                for u in range(2):
                    ins = dve.tensor_tensor(h[j][:, 2 * u:2 * u + 2, :], ps_o[u][:, :, :],
                                            h[j][:, 2 * u:2 * u + 2, :], ALU.add)
                ins.then_inc(sem["e_summed"], 1)
                dve.wait_ge(sem["e_summed"], b + 1)
                for t in range(T4):
                    ins = dve.bn_stats(st[j][:, t, 0:6], h[j][:, t, :])
                ins.then_inc(sem["e_bn"], 1)

            def norm_scales(b, j):
                dve.wait_ge(sem["e_bn"], b + 1)
                dve.sem_inc(sem["e_dve_waited"], 1)
                for t in range(T4):
                    ins = dve.bn_aggr(st[j][:, t, 6:8], st[j][:, t, 0:6])
                ins.then_inc(sem["e_var"], 1)

            def norm_out(b, j):
                s_ = st[j]
                dve.wait_ge(sem["e_std"], b + 1)
                dve.reciprocal(s_[:, :, 9:10], s_[:, :, 8:9]).then_inc(sem["e_rstd"], 1)
                dve.wait_ge(sem["e_rstd"], b + 1)
                for t in range(T4):
                    ins = dve.scalar_tensor_tensor(s_[:, t, 10:11], s_[:, t, 6:7], -1.0, s_[:, t, 9:10],
                                                   ALU.mult, ALU.mult)
                ins.then_inc(sem["e_scales"], 1)

            def step(s, j):
                if inside(s, 0, B):
                    soft_in(s, j)
                if inside(s, 1, B):
                    norm_in(s - 1, 1 - j)
                    norm_scales(s - 1, 1 - j)
                if inside(s, 0, B):
                    soft_out(s, j)
                if inside(s, 1, B):
                    norm_out(s - 1, 1 - j)

            loop(dve, B, step, 1)

        @block.gpsimd
        def _(pool):
            def step(b, j):
                pool.wait_ge(sem[f"e_in{j}"], (b - j) * 16 + 32)
                pool.wait_ge(sem[f"e_stored{j}"], (b - j) * 8 + 16)
                for t in range(T4):
                    ins = pool.tensor_tensor(h[j][:, t, :], x[j][:, t, :], bo[:, :], ALU.add)
                ins.then_inc(sem["e_xb"], 1)

            pool.wait_ge(sem["e_const_in"], const_in)
            loop(pool, B, step, 0)

        @block.scalar
        def _(act):
            fold_out(act, 1, lambda d, s: act.activation(d, s, ACT.Copy))

            def step(s, j):
                b, i = s - 1, 1 - j
                if inside(s, 1, B):
                    act.wait_ge(sem["e_turned"], b + 1)
                    if not early(b, 1):
                        act.wait_ge(sem["e_mixed"], b)
                    act.activation(pt[:, :, :], ps_t[:, :, :], ACT.Copy).then_inc(sem["e_pt"], 1)
                if inside(s, 0, B):
                    act.wait_ge(sem["e_shifted"], s + 1)
                    act.activation(sc[j][:, :, :], sc[j][:, :, :], ACT.Exp, scale=SCALE_F).then_inc(sem["e_exped"], 1)
                if inside(s, 1, B):
                    act.wait_ge(sem["e_var"], b + 1)
                    act.activation(st[i][:, :, 8:9], st[i][:, :, 7:8], ACT.Sqrt, bias=eps[:, :])\
                       .then_inc(sem["e_std"], 1)
                    act.wait_ge(sem["e_scales"], b + 1)
                    for t in range(T4):
                        ins = act.activation(h[i][:, t, :], h[i][:, t, :], ACT.Identity, bias=st[i][:, t, 10:11],
                                             scale=st[i][:, t, 9:10])
                    ins.then_inc(sem["e_normed"], 1)

            act.wait_ge(sem["e_eps"], 1)
            loop(act, B, step, 1)


E_SEMS = ["e_" + n for n in ["sp_waited", "dve_waited", "scored", "xb", "in0", "in1", "normed", "stored0", "stored1",
                             "const_in", "o", "oT_ready", "oT", "kv_ready", "kd", "bq", "folded0", "folded1", "fold",
                             "biased", "probs", "pt", "turned", "summed", "mixed", "eps", "max", "shifted", "exped",
                             "sum", "inv", "bn", "var", "std", "rstd", "scales"]]


def ffn_views(nc, t, x2, x2T, out):
    w = lambda n: t[n].rearrange("(k p) n -> p k n", p=P)
    rows = lambda n: bass.AP(tensor=t[n].tensor, offset=0, ap=[[E, NS], [0, B], [1, E]])
    o1 = nc.dram_tensor("o1", (SB, E), F32).ap()
    hT = nc.dram_tensor("hT", (P, K4, SB), F32).ap()
    y = nc.dram_tensor("y", (NS, B, E), F32).ap()
    bc = lambda n: t[n].partition_broadcast(P)
    return {
        "ident": t["ident"], "d_wq": w("d_Wq"), "d_wkT": w("d_WkT"), "d_wv": w("d_Wv"), "d_wo": w("d_Wo"),
        "sqT": t["sqT"].rearrange("(k p) s -> p k s", p=P), "d_cols": t["d_cols"], "slots": rows("slots"),
        "d_bo": bc("d_bo"), "e_g": rows("e_ln_g"), "e_b": rows("e_ln_b"),
        "x2T": lambda b: x2T[b].rearrange("(k p) s -> p k s", p=P),
        "x2": lambda b: x2[b].rearrange("(t p) e -> p t e", p=P),
        "o1": o1, "hT": hT, "e_bias": t["e_bias"],
        "w1": lambda e: t["e_W1"][e].rearrange("(k p) f -> p k f", p=P),
        "wg": lambda e: t["e_Wg"][e].rearrange("(k p) f -> p k f", p=P),
        "w2": lambda e: t["e_W2"][e].rearrange("(c p) n -> p c n", p=P),
        "y": lambda e: y[e], "y_all": y.rearrange("s b e -> (s b) e"), "e_b2": rows("e_b2"),
        "c_wqT": w("c_WqT"), "c_wk": w("c_Wk"), "c_wv": w("c_Wv"), "c_wo": w("c_Wo"), "c_cols": t["c_cols"],
        "c_bo": bc("c_bo"), "out": lambda b: out[b].rearrange("(t p) e -> p t e", p=P),
    }

def attention_views(nc, t, x1T):
    chunks = lambda ap: ap.rearrange("(k p) n -> p k n", p=P)
    group = lambda n, per: (lambda q: chunks(t[n][q % per]))
    batch = lambda ap, per: (lambda q: chunks(ap[q // per]))
    scratch = lambda name, shape: nc.dram_tensor(name, shape, F32).ap()
    col = lambda ap: (lambda u: ap[u // T4].rearrange("(k p) (t n) -> t p k n", p=P, n=P)[u % T4])
    tok = lambda ap: (lambda u: ap.rearrange("b (t p) e -> (b t) p e", p=P)[u])
    bc = lambda ap: ap.partition_broadcast(P)
    ctx1, ctx2 = scratch("ctx1", (QUADS, P, S)), scratch("ctx2", (PAIRS, P, S))
    x1, x2, x2T = (scratch(n, (B, S, E)) for n in ("x1", "x2", "x2T"))
    whole = lambda ap: ap.rearrange("(b m) p s -> b (m p) s", b=B)
    dr = {
        "ident": t["ident"], "emask": t["emask"], "dist_rev": t["dist_rev"], "dist_fwd": t["dist_fwd"],
        "xT": batch(t["xT"], QUADS // B), "a_bqk": lambda q: t["a_bqk"][q % (QUADS // B)],
        "a_bv": lambda q: bc(t["a_bv"][q % (QUADS // B)]),
        "a_split": scratch("split", (3, 2 * P, S)), "a_band_q": scratch("band_q", (2, NT, P * WIN)),
        "a_band_k": scratch("band_k", (2, NT, P * WIN)), "a_ctxT": lambda q: ctx1[q],
        "na_wo": chunks(t["attn_Wo"]), "na_bo": bc(t["attn_bo"]), "gamma": bc(t["attn_ln_gamma"]),
        "beta": bc(t["attn_ln_beta"]), "na_cT": col(whole(ctx1)), "na_x": tok(t["x"]), "na_y": tok(x1),
        "na_yT": col(x1T),
        "mask": t["mask"], "x1T": batch(x1T, PAIRS // B), "ctxT": batch(t["ctxT"], PAIRS // B),
        "b_bqk": lambda q: t["b_bqk"][q % (PAIRS // B)], "b_bv": lambda q: bc(t["b_bv"][q % (PAIRS // B)]),
        "b_cxT": lambda q: ctx2[q],
        "nb_wo": chunks(t["xattn_Wo"]), "nb_bo": bc(t["xattn_bo"]), "nb_cT": col(whole(ctx2)), "nb_x": tok(x1),
        "nb_y": tok(x2), "nb_yT": col(x2T),
    }
    for n in "qkv":
        dr["a_w" + n] = group("a_w" + n, QUADS // B)
        dr["b_w" + n] = group("b_w" + n, PAIRS // B)
    return dr, x2, x2T


def program(nc, t, out):
    def run(phase, names, *more):
        sems = {n: nc.alloc_semaphore(n) for n in names}
        phase(nc, dr, sems, *more)
        nc.clear_and_free_semaphores(list(sems.values()))
        nc.all_engine_barrier()

    x1T = nc.dram_tensor("x1T", (B, E, S), F32).ap()
    dr, x2, x2T = attention_views(nc, t, x1T)
    dr.update(ffn_views(nc, t, x2, x2T, out))
    run(self_attention, A_SEMS)
    run(project_norm, norm_sems("na_"), "na_", K4, True)
    run(cross_attention, B_SEMS)
    run(project_norm, norm_sems("nb_"), "nb_", 2 * K4, False)
    run(slot_attention, C_SEMS)
    run(experts, D_SEMS)
    run(slots_to_tokens, E_SEMS)


def kernel(**inputs):
    import numpy as np
    import concourse.bacc as _bacc
    from concourse.bass_utils import run_bass_kernel_spmd as _run
    nc = _bacc.Bacc("TRN2", target_bir_lowering=False, num_devices=1)
    a = {}
    c = np.ascontiguousarray
    i = {k: np.asarray(v) for k, v in inputs.items()}
    a["x"] = i["x"]
    a["xT"] = c(i["x"].transpose(0, 2, 1))
    a["ctxT"] = c(i["ctx_1024"].transpose(0, 2, 1))
    for n in "qkv":
        a[f"a_w{n}"] = c(i[f"L0_attn_W{n}"].reshape(E, E // P, P).transpose(1, 0, 2))
        a[f"b_w{n}"] = c(i[f"L0_xattn_W{n}"].reshape(-1, 2, E, KD).transpose(0, 2, 1, 3).reshape(-1, E, P))
    for z, layer in (("a", "attn"), ("b", "xattn")):
        a[z + "_bqk"] = c(np.stack([i[f"L0_{layer}_b{n}"].reshape(-1, P) for n in "qk"], axis=2))
        a[z + "_bv"] = c(i[f"L0_{layer}_bv"].reshape(-1, P))
    for n in ("attn_Wo", "attn_bo", "attn_ln_gamma", "attn_ln_beta", "xattn_Wo", "xattn_bo"):
        a[n] = i["L0_" + n]
    table = i["L0_attn_dist_emb"]
    for n, rows in (("dist_fwd", table), ("dist_rev", table[::-1])):
        d = np.zeros((1024, D), np.float32)
        d[:1023] = rows
        a[n] = c(np.tile(np.repeat(d.T, 2, axis=0), (2, 1)))
    part, rep = np.arange(P) % 2, np.arange(P) // 64
    a["emask"] = c(np.stack([part == rep, part == 0], axis=1).astype(np.float32))
    a["ident"] = np.eye(P, dtype=np.float32)
    mask = np.zeros((P, S), np.float32)
    mask[:, S - P:] = np.where(np.tril(np.ones((P, P), bool)), 0.0, -1e30)
    a["mask"] = mask
    for n in ("d_Wq", "d_Wv", "d_Wo", "c_Wk", "c_Wv", "c_Wo"):
        a[n] = i["L0_ffn_" + n]
    for n in ("d_Wk", "c_Wq"):
        a[n + "T"] = c(i["L0_ffn_" + n].T)
    for z in "dc":
        a[z + "_cols"] = c(np.stack([i[f"L0_ffn_{z}_b{n}"].reshape(4, P) for n in "qkv"]).transpose(2, 0, 1))
        a[z + "_bo"] = i[f"L0_ffn_{z}_bo"]
    a["slots"] = c(i["L0_ffn_slot_query"][0])
    a["sqT"] = c(i["L0_ffn_slot_query"][0].T)
    for n in ("e_ln_g", "e_ln_b", "e_b2", "e_W1", "e_Wg", "e_W2"):
        a[n] = i["L0_ffn_" + n]
    a["e_bias"] = c(np.stack([i["L0_ffn_e_b1"], i["L0_ffn_e_bg"]], axis=1)
                    .reshape(NS, 2, FQ, 4, P).transpose(4, 0, 1, 3, 2).reshape(P, NS, 2, FC))
    t = {n: nc.dram_tensor(f"in_{n}", x.shape, mybir.dt.from_np(x.dtype), kind="ExternalInput").ap() for n, x in a.items()}
    out = nc.dram_tensor("out0", (B, S, E), F32, kind="ExternalOutput").ap()
    program(nc, t, out)
    r = _run(nc, [{f"in_{n}": x for n, x in a.items()}], core_ids=[0])
    return r.results[0]["out0"]
```

```python
import concourse.bass as bass
from concourse import mybir
from contextlib import ExitStack

F32 = mybir.dt.float32
F32R = mybir.dt.float32r
ALU = mybir.AluOpType
ACT = mybir.ActivationFunctionType
AX = mybir.AxisListType

B, S, E = 8, 512, 512
P = 128
T4 = S // P
K4 = E // P
H = 16
D = E // H
HQ = P // D
QUADS = B * (H // HQ)
NT = HQ * T4
SC = 8
LAG_A = 3
WIN = 640
SCALE_A = float(D) ** -0.5
BIG = 3.0e38


def self_attention(nc, dr, sem):
    with ExitStack() as ctx:
        def sb(name, shape, dt=F32):
            return ctx.enter_context(nc.sbuf_tensor(name, shape, dt))

        def ps(name, shape):
            return ctx.enter_context(nc.psum_tensor(name, shape, F32))

        xT = sb("a_xT", [P, K4, S])
        wq, wk, wv = (sb(f"a_w{n}", [P, K4, P]) for n in "qkv")
        bqk = sb("a_bqk", [P, 2])
        bv = sb("a_bv", [P, P])
        hi_q = sb("a_hi_q", [P, S], F32R)
        hi_k = sb("a_hi_k", [P, S], F32R)
        qs = [sb(f"a_qs{i}", [P, HQ, S], F32R) for i in range(2)]
        ks = [sb(f"a_ks{i}", [P, HQ, S], F32R) for i in range(2)]
        eq = sb("a_eq", [P, 1024], F32R)
        ek = sb("a_ek", [P, 1024], F32R)
        emask = sb("a_emask", [P, 2])
        stage_q = [sb(f"a_stage_q{i}", [P, 2, WIN]) for i in range(4)]
        stage_k = [sb(f"a_stage_k{i}", [P, 2, WIN]) for i in range(4)]
        rq = [sb(f"a_rq{i}", [P, 2, S]) for i in range(4)]
        rk = [sb(f"a_rk{i}", [P, T4, S]) for i in range(4)]
        sc = [sb(f"a_sc{i}", [P, S]) for i in range(SC)]
        mx, sm, inv = (sb(f"a_{n}", [P, SC]) for n in ("mx", "sm", "inv"))
        pt = sb("a_pt", [P, HQ, T4, S])
        v = [sb(f"a_v{i}", [P, T4, P]) for i in range(2)]
        cx = [sb(f"a_cx{i}", [P, S]) for i in range(2)]
        ident = sb("a_ident", [P, P])

        ps_q = ps("a_ps_q", [P, 2, 512])
        ps_k = ps("a_ps_k", [P, 2, 512])
        ps_s = [ps(f"a_ps_s{i}", [P, 512]) for i in range(2)]
        ps_t = ps("a_ps_t", [P, 512])
        ps_c = ps("a_ps_c", [P, 512])

        def band(i):
            return 384 - P * (i % T4)

        bands_at, nxt = {}, 0
        for t, c in enumerate([0, 0, 0, 1, 1, 1, 1, 1, 2, 1, 1, 2, 1, 1, 2, 1]):
            bands_at[t] = list(range(nxt, nxt + c))
            nxt += c
        assert nxt == NT

        block = ctx.enter_context(nc.Block())

        @block.sync
        def _(sp):
            sp.dma_start(ident[:, :], dr["ident"]).then_inc(sem["a_const_in"], 16)
            sp.dma_start(emask[:, :], dr["emask"]).then_inc(sem["a_const_in"], 16)
            for i, n in enumerate(["dist_rev", "dist_fwd"]):
                sp.dma_start(pt[:, i, 0:2, :].rearrange("p a b -> p (a b)"), dr[n]).then_inc(sem["a_const_in"], 16)

            def settle():
                sp.sem_inc(sem["a_sp_waited"], 1)

            def load(q, new_batch=False):
                if not (isinstance(q, int) and q == 0):
                    sp.wait_ge(sem["a_lo_stacked"], HQ * q)
                    settle()
                    sp.wait_ge(sem["a_v_out"], q)
                    settle()
                if new_batch:
                    sp.dma_start(xT[:, :, :], dr["xT"](q)).then_inc(sem["a_x_in"], 16)
                for w, n in ((wq, "a_wq"), (wk, "a_wk"), (wv, "a_wv")):
                    sp.dma_start(w[:, :, :], dr[n](q)).then_inc(sem["a_in"], 16)
                sp.dma_start(bqk[:, :], dr["a_bqk"](q)).then_inc(sem["a_in"], 16)
                sp.dma_start(bv[:, :], dr["a_bv"](q)).then_inc(sem["a_in"], 16)

            def write_pair(q, par, n):
                for kind, st in (("q", stage_q), ("k", stage_k)):
                    sp.wait_ge(sem[f"a_{kind}_staged"], NT * q + 2 * n + 2)
                    settle()
                    out = dr[f"a_band_{kind}"][par, 2 * n:2 * n + 2, :].rearrange("t (p n) -> p t n", p=P)
                    for r in (0, 64):
                        cols = slice(64 - r, 64 - r + S + 64)
                        sp.dma_start(out[r:r + 64, :, cols], st[n % 4][r:r + 64, :, cols])\
                          .then_inc(sem[f"a_{kind}_written{n % 4}"], 16)

            def shear(kind, par, t0, nt):
                h = dr[f"a_band_{kind}"]
                base = (par * NT + t0) * P * WIN + P - 1
                return bass.AP(tensor=h.tensor, offset=base, ap=[[WIN - 1, P], [P * WIN, nt], [1, S]])

            def read_k(q, par, j):
                i = HQ * q + j
                for n in (2 * j, 2 * j + 1):
                    sp.wait_ge(sem[f"a_k_written{n % 4}"], 32 * (2 * q + n // 4 + 1))
                    settle()
                if not (isinstance(q, int) and q == 0):
                    sp.wait_ge(sem["a_summed"], T4 * (i - 3))
                    settle()
                sp.dma_start(rk[j][:, :, :], shear("k", par, T4 * j, T4)).then_inc(sem[f"a_rk{j}"], 16)

            def read_q(q, par, j, half):
                i = HQ * q + j
                n = 2 * j + half
                sp.wait_ge(sem[f"a_q_written{n % 4}"], 32 * (2 * q + n // 4 + 1))
                settle()
                if not (isinstance(q, int) and q == 0 and j < 2):
                    sp.wait_ge(sem["a_summed"], T4 * (i - 2) + 2 * half + 2)
                    settle()
                slot = 2 * (j % 2) + half
                sp.dma_start(rq[slot][:, :, :], shear("q", par, T4 * j + 2 * half, 2)).then_inc(sem[f"a_rq{slot}"], 16)

            def store(q, par):
                sp.wait_ge(sem["a_cx_out"], q + 1)
                settle()
                sp.dma_start(dr["a_ctxT"](q), cx[par][:, :]).then_inc(sem[f"a_stored{par}"], 16)

            def sp_quad(g, par, first=False, last=False, loads=True, new_batch=False):
                nx, np_ = g + 1, 1 - par
                read_k(g, par, 3)
                read_q(g, par, 1, 1)
                read_q(g, par, 2, 0)
                read_q(g, par, 2, 1)
                if not first:
                    store(g - 1, np_)
                if loads:
                    load(nx + 1, new_batch)
                if last:
                    read_q(g, par, 3, 0)
                    read_q(g, par, 3, 1)
                    return
                write_pair(nx, np_, 0)
                read_q(g, par, 3, 0)
                write_pair(nx, np_, 1)
                read_k(nx, np_, 0)
                read_q(g, par, 3, 1)
                write_pair(nx, np_, 2)
                write_pair(nx, np_, 3)
                read_k(nx, np_, 1)
                read_q(nx, np_, 0, 0)
                write_pair(nx, np_, 4)
                read_q(nx, np_, 0, 1)
                write_pair(nx, np_, 5)
                read_k(nx, np_, 2)
                write_pair(nx, np_, 6)
                read_q(nx, np_, 1, 0)
                write_pair(nx, np_, 7)

            sp.sem_inc(sem["a_stored0"], 16)
            sp.sem_inc(sem["a_stored1"], 16)
            load(0, new_batch=True)
            load(1)
            for n in range(NT // 2):
                write_pair(0, 0, n)
            for j in range(3):
                read_k(0, 0, j)
            read_q(0, 0, 0, 0)
            read_q(0, 0, 0, 1)
            read_q(0, 0, 1, 0)
            sp_quad(0, 0, first=True)
            with sp.Fori(1, QUADS - 3, 4) as g:
                for j in range(4):
                    sp_quad(g + j, (1 + j) % 2, new_batch=(j == 1))
            sp_quad(QUADS - 3, 1)
            sp_quad(QUADS - 2, 0, loads=False)
            sp_quad(QUADS - 1, 1, last=True, loads=False)
            store(QUADS - 1, 1)
            sp.wait_ge(sem["a_stored0"], 16 * (QUADS // 2) + 16)
            sp.wait_ge(sem["a_stored1"], 16 * (QUADS // 2) + 16)

        @block.tensor
        def _(pe):
            def project(q, which):
                if which == 0:
                    pe.wait_ge(sem["a_in"], 80 * q + 80)
                    pe.wait_ge(sem["a_x_in"], 16 * (q // HQ) + 16)
                if not (isinstance(q, int) and q == 0):
                    pe.wait_ge(sem["a_q_staged" if which < 2 else "a_k_staged"], NT * q)
                if which < 2:
                    w = (wq, wk)[which]
                    for k in range(K4):
                        mm = pe.matmul(ps_q[:, which, :], w[:, k, :], xT[:, k, :], start=(k == 0), stop=(k == K4 - 1))
                    mm.then_inc(sem["a_qk_ready"], 1)
                    return
                for t in range(T4):
                    for k in range(K4):
                        mm = pe.matmul(ps_k[:, 0, t * P:(t + 1) * P], xT[:, k, t * P:(t + 1) * P], wv[:, k, :],
                                       start=(k == 0), stop=(k == K4 - 1))
                mm.then_inc(sem["a_v_ready"], 1)

            def bands(q, par, i):
                h, t = i // T4, i % T4
                if i == 0:
                    pe.wait_ge(sem["a_lo_stacked"], HQ * q + HQ)
                    pe.wait_ge(sem["a_v_out"], q + 1)
                w = band(i)
                for kind, src, table, out in (("q", qs, eq, ps_q), ("k", ks, ek, ps_k)):
                    if i:
                        pe.wait_ge(sem[f"a_{kind}_staged"], NT * q + i)
                    for n in range(2):
                        mm = pe.matmul(out[:, n, 0:WIN // 2], src[par][:, h, t * P:(t + 1) * P],
                                       table[:, w + n * (WIN // 2):w + (n + 1) * (WIN // 2)], start=True, stop=True)
                    mm.then_inc(sem[f"a_{kind}_band"], 1)

            def score(q, par, i):
                h, t = i // T4, i % T4
                if t == 0:
                    pe.wait_ge(sem[f"a_rk{h}"], 16 * q + 16)
                if not (isinstance(q, int) and q == 0 and i < 2):
                    pe.wait_ge(sem["a_summed"], NT * q + i - 1)
                out = ps_s[i % 2]
                pe.matmul(out[:, :], qs[par][:, h, t * P:(t + 1) * P], ks[par][:, h, :], start=True, stop=False)
                for r in range(T4):
                    mm = pe.matmul(out[:, r * P:(r + 1) * P], rk[h][:, r, t * P:(t + 1) * P], ident[:, :],
                                   is_transpose=True, start=False, stop=(r == T4 - 1))
                mm.then_inc(sem["a_score"], 1)

            def turn(q, i):
                pe.wait_ge(sem["a_normed"], NT * q + i + 1)
                if not (isinstance(q, int) and q == 0 and i == 0):
                    pe.wait_ge(sem["a_pt_out"], NT * q + i)
                for r in range(T4):
                    mm = pe.transpose(ps_t[:, r * P:(r + 1) * P], sc[i % SC][:, r * P:(r + 1) * P], ident[:, :])
                mm.then_inc(sem["a_turned"], 1)

            def context(q, par):
                pe.wait_ge(sem["a_pt_out"], NT * q + NT)
                for r in range(T4):
                    for h in range(HQ):
                        mm = pe.matmul(ps_c[D * h:D * (h + 1), :], v[par][:, r, D * h:D * (h + 1)], pt[:, h, r, :],
                                       start=(r == 0), stop=(r == T4 - 1))
                mm.then_inc(sem["a_cx_ready"], 1)

            def pe_quad(g, par, first=False, last=False):
                for i in range(NT):
                    score(g, par, i)
                    if i == LAG_A and not first:
                        context(g - 1, 1 - par)
                    if i >= LAG_A:
                        turn(g, i - LAG_A)
                    elif not first:
                        turn(g - 1, NT + i - LAG_A)
                    if not last:
                        for n in bands_at[i]:
                            bands(g + 1, 1 - par, n)
                    if i < 3 and not last:
                        project(g + 1, i)

            pe.wait_ge(sem["a_const_in"], 64)
            pe.wait_ge(sem["a_tables"], 2)
            for i in range(3):
                project(0, i)
            for i in range(NT):
                bands(0, 0, i)
            pe_quad(0, 0, first=True)
            with pe.Fori(1, QUADS - 1, 2) as g:
                pe_quad(g, 1)
                pe_quad(g + 1, 0)
            pe_quad(QUADS - 1, 1, last=True)
            for i in range(NT - LAG_A, NT):
                turn(QUADS - 1, i)
            context(QUADS - 1, 1)

        @block.scalar
        def _(act):
            def halves(q):
                if not (isinstance(q, int) and q == 0):
                    act.wait_ge(sem["a_lo_stacked"], HQ * q)
                for i, dst in enumerate((hi_q, hi_k)):
                    act.wait_ge(sem["a_qk_ready"], 2 * q + i + 1)
                    act.activation(dst[:, :], ps_q[:, i, :], ACT.Identity, bias=bqk[:, i:i + 1])\
                       .then_inc(sem["a_qk_hi"], 1)

            def stack_hi(q, par, h):
                r = slice(D * h, D * (h + 1))
                if h == 0:
                    act.wait_ge(sem["a_qk_hi"], 2 * q + 2)
                for dst, hi, block in ((qs, hi_q, 0), (ks, hi_k, 0), (ks, hi_k, 1)):
                    ins = act.activation(dst[par][D * block:D * (block + 1), h, :], hi[r, :].bitcast(F32), ACT.Copy)
                ins.then_inc(sem["a_hi_stacked"], 1)

            def stage(q, i):
                n = i // 2
                for kind, src, st in (("q", ps_q, stage_q), ("k", ps_k, stage_k)):
                    act.wait_ge(sem[f"a_{kind}_band"], NT * q + i + 1)
                    if not (isinstance(q, int) and q == 0 and n < 4):
                        act.wait_ge(sem[f"a_{kind}_written{n % 4}"], 32 * (2 * q + n // 4))
                    act.activation(st[n % 4][:, i % 2, :].rearrange("p (a n) -> p a n", a=2),
                                   src[:, :, 0:WIN // 2], ACT.Copy).then_inc(sem[f"a_{kind}_staged"], 1)

            def softexp(q, i):
                act.wait_ge(sem["a_summed"], NT * q + i + 1)
                act.activation(sc[i % SC][:, :], sc[i % SC][:, :], ACT.Exp, bias=mx[:, i % SC:i % SC + 1], scale=-1.0,
                               accum_out=sm[:, i % SC:i % SC + 1]).then_inc(sem["a_exped"], 1)

            def act_quad(g, par, last=False):
                for i in range(NT):
                    softexp(g, i)
                    if last:
                        continue
                    if i == 1:
                        halves(g + 1)
                    if i in (2, 3):
                        stack_hi(g + 1, 1 - par, 2 * i - 4)
                        stack_hi(g + 1, 1 - par, 2 * i - 3)
                    for n in bands_at[i]:
                        stage(g + 1, n)

            halves(0)
            act.wait_ge(sem["a_tables"], 2)
            for h in range(HQ):
                stack_hi(0, 0, h)
            for i in range(NT):
                stage(0, i)
            act_quad(0, 0)
            with act.Fori(1, QUADS - 1, 2) as g:
                act_quad(g, 1)
                act_quad(g + 1, 0)
            act_quad(QUADS - 1, 1, last=True)

        @block.vector
        def _(dve):
            def tables():
                dve.wait_ge(sem["a_const_in"], 64)
                hi = qs[1][:, 0:2, :].rearrange("p a b -> p (a b)")
                n = 0
                for i, dst in enumerate((eq, ek)):
                    x = pt[:, i, 0:2, :].rearrange("p a b -> p (a b)")
                    lo = pt[:, i, 2:4, :].rearrange("p a b -> p (a b)")
                    mask = emask[:, i:i + 1]
                    dve.tensor_copy(hi, x).then_inc(sem["a_tab"], 1)
                    dve.wait_ge(sem["a_tab"], n + 1)
                    dve.tensor_tensor(lo, x, hi.bitcast(F32), ALU.subtract).then_inc(sem["a_tab"], 1)
                    dve.wait_ge(sem["a_tab"], n + 2)
                    dve.tensor_scalar(x, hi.bitcast(F32), mask, None, ALU.mult).then_inc(sem["a_tab"], 1)
                    dve.wait_ge(sem["a_tab"], n + 3)
                    dve.tensor_scalar(pt[:, 2 + i, 0:2, :].rearrange("p a b -> p (a b)"), lo, mask, None, ALU.mult)\
                       .then_inc(sem["a_tab"], 1)
                    dve.wait_ge(sem["a_tab"], n + 4)
                    dve.tensor_tensor(lo, lo, pt[:, 2 + i, 0:2, :].rearrange("p a b -> p (a b)"), ALU.subtract)\
                       .then_inc(sem["a_tab"], 1)
                    dve.wait_ge(sem["a_tab"], n + 5)
                    dve.tensor_tensor(dst[:, :], x, lo, ALU.add).then_inc(sem["a_tables"], 1)
                    n += 5

            def stack_lo(q, par, h):
                if h == 0:
                    dve.wait_ge(sem["a_qk_hi"], 2 * q + 2)
                r = slice(D * h, D * (h + 1))
                for i, dst, hi, block in ((0, qs, hi_q, 1), (1, ks, hi_k, 2), (1, ks, hi_k, 3)):
                    ins = dve.scalar_tensor_tensor(dst[par][D * block:D * (block + 1), h, :], ps_q[r, i, :],
                                                   bqk[r, i:i + 1], hi[r, :].bitcast(F32), ALU.add, ALU.subtract)
                    if i == 0:
                        ins.then_inc(sem["a_q_lo"], 1)
                dve.wait_ge(sem["a_q_lo"], HQ * q + h + 1)
                dve.wait_ge(sem["a_hi_stacked"], HQ * q + h + 1)
                dve.tensor_copy(qs[par][64:P, h, :], qs[par][0:64, h, :]).then_inc(sem["a_lo_stacked"], 1)

            def v_out(q, par):
                dve.wait_ge(sem["a_v_ready"], q + 1)
                if not (isinstance(q, int) and q < 2):
                    dve.wait_ge(sem["a_cx_ready"], q - 1)
                for t in range(T4):
                    ins = dve.tensor_tensor(v[par][:, t, :], ps_k[:, 0, t * P:(t + 1) * P], bv[:, :], ALU.add)
                ins.then_inc(sem["a_v_out"], 1)

            def add_max(q, i):
                j, half = i // T4, (i // 2) % 2
                slot = 2 * (j % 2) + half
                dve.wait_ge(sem["a_score"], NT * q + i + 1)
                dve.wait_ge(sem[f"a_rq{slot}"], 16 * (2 * q + j // 2 + 1))
                if not (isinstance(q, int) and q == 0 and i < SC):
                    dve.wait_ge(sem["a_turned"], NT * q + i + 1 - SC)
                dve.sem_inc(sem["a_dve_waited"], 1)
                dve.tensor_tensor_reduce(out=sc[i % SC][:, :], in0=ps_s[i % 2][:, :], in1=rq[slot][:, i % 2, :],
                                         scale=-SCALE_A, scalar=BIG, op0=ALU.add, op1=ALU.min,
                                         accum_out=mx[:, i % SC:i % SC + 1]).then_inc(sem["a_summed"], 1)

            def invert(q, i):
                dve.wait_ge(sem["a_exped"], NT * q + i + 1)
                dve.reciprocal(inv[:, i % SC:i % SC + 1], sm[:, i % SC:i % SC + 1]).then_inc(sem["a_inverse"], 1)

            def pt_out(q, i):
                h, t = i // T4, i % T4
                dve.wait_ge(sem["a_turned"], NT * q + i + 1)
                if i == 0 and not (isinstance(q, int) and q == 0):
                    dve.wait_ge(sem["a_cx_ready"], q)
                dve.tensor_copy(pt[:, h, :, t * P:(t + 1) * P],
                                ps_t[:, :].rearrange("p (r n) -> p r n", r=T4)).then_inc(sem["a_pt_out"], 1)

            def cx_out(q, par):
                dve.wait_ge(sem["a_cx_ready"], q + 1)
                dve.wait_ge(sem[f"a_stored{par}"], (q - par) * 8 + 16)
                dve.tensor_copy(cx[par][:, :], ps_c[:, :]).then_inc(sem["a_cx_out"], 1)

            def dve_quad(g, par, first=False, last=False):
                for i in range(NT):
                    add_max(g, i)
                    if i:
                        invert(g, i - 1)
                    if i in (2, 3) and not last:
                        stack_lo(g + 1, 1 - par, 2 * i - 4)
                        stack_lo(g + 1, 1 - par, 2 * i - 3)
                    if i >= LAG_A:
                        pt_out(g, i - LAG_A)
                    elif not first:
                        pt_out(g - 1, NT + i - LAG_A)
                    if i == LAG_A and not last:
                        v_out(g + 1, 1 - par)
                    if i == LAG_A and not first:
                        cx_out(g - 1, 1 - par)
                invert(g, NT - 1)

            tables()
            for h in range(HQ):
                stack_lo(0, 0, h)
            v_out(0, 0)
            dve_quad(0, 0, first=True)
            with dve.Fori(1, QUADS - 1, 2) as g:
                dve_quad(g, 1)
                dve_quad(g + 1, 0)
            dve_quad(QUADS - 1, 1, last=True)
            for i in range(NT - LAG_A, NT):
                pt_out(QUADS - 1, i)
            cx_out(QUADS - 1, 1)

        @block.gpsimd
        def _(pool):
            def quad_norm(g):
                for i in range(NT):
                    pool.wait_ge(sem["a_inverse"], NT * g + i + 1)
                    pool.sem_inc(sem["a_pool_waited"], 1)
                    pool.tensor_scalar(sc[i % SC][:, :], sc[i % SC][:, :], inv[:, i % SC:i % SC + 1], None, ALU.mult)\
                        .then_inc(sem["a_normed"], 1)

            with pool.Fori(0, QUADS) as g:
                quad_norm(g)


A_SEMS = (["a_dve_waited", "a_pool_waited", "a_sp_waited", "a_const_in", "a_in", "a_x_in", "a_hi_stacked", "a_lo_stacked", "a_q_lo", "a_q_staged", "a_k_staged",
           "a_cx_out", "a_stored0",
           "a_stored1", "a_qk_ready", "a_v_ready", "a_q_band", "a_k_band", "a_summed",
           "a_score", "a_normed", "a_pt_out", "a_turned", "a_cx_ready", "a_tables", "a_tab", "a_qk_hi",
           "a_exped", "a_inverse", "a_v_out"] + [f"a_rk{i}" for i in range(4)] + [f"a_rq{i}" for i in range(4)]
          + [f"a_{kind}_written{i}" for kind in "qk" for i in range(4)])

UNITS = B * T4
EPS_ATTN, EPS = 1e-12, 1e-5


def project_norm(nc, dr, sem, z, chunks, affine):
    with ExitStack() as ctx:
        def sb(name, shape, dt=F32):
            return ctx.enter_context(nc.sbuf_tensor(z + name, shape, dt))

        def ps(name, shape):
            return ctx.enter_context(nc.psum_tensor(z + name, shape, F32))

        R = 8
        SCALES0, SHIFT, SCALES1, TURN, OUT = (1, 2, 3, 4, 5) if affine else (None, 0, 1, 2, 3)
        wo = sb("wo", [P, chunks, E])
        cT = [sb(f"cT{i}", [P, chunks, P]) for i in range(R)]
        x = [sb(f"x{i}", [P, E]) for i in range(R)]
        xb = [sb(f"xb{i}", [P, E]) for i in range(R)]
        xg = [sb(f"xg{i}", [P, E]) for i in range(R)] if affine else None
        h = [sb(f"h{i}", [P, E]) for i in range(R)]
        y = [sb(f"y{i}", [P, E]) for i in range(R)]
        yT = [sb(f"yT{i}", [P, K4, P]) for i in range(R)]
        st = [sb(f"st{i}", [P, 2, 16]) for i in range(R)]
        bo = sb("bo", [P, E])
        gamma = sb("gamma", [P, E]) if affine else None
        beta = sb("beta", [P, E]) if affine else None
        eps = sb("eps", [P, 2])
        ident = sb("ident", [P, P])
        ps_o = [ps(f"ps_o{i}", [P, 512]) for i in range(4)]
        ps_y = [ps(f"ps_y{i}", [P, 512]) for i in range(2)]

        const_in = 16 * (5 if affine else 3)
        rounds = (0, 1) if affine else (1,)

        def steps(e, step):
            for s in range(R):
                step(s, s)
            with e.Fori(R, UNITS - R, R) as s:
                for j in range(R):
                    step(s + j, j)
            for s in range(UNITS - R, UNITS + R):
                step(s, s % R)

        def has(s, lag):
            return not isinstance(s, int) or 0 <= s - lag < UNITS

        def early(s, n):
            return isinstance(s, int) and s < n

        block = ctx.enter_context(nc.Block())

        @block.sync
        def _(sp):
            def settle():
                sp.sem_inc(sem[z + "sp_waited"], 1)

            def load(u, j):
                if not early(u, R):
                    sp.wait_ge(sem[z + "projected"], u - R + 1)
                    settle()
                    sp.wait_ge(sem[z + "biased"], u - R + 1)
                    settle()
                sp.dma_start(cT[j][:, :, :], dr[z + "cT"](u)).then_inc(sem[f"{z}in{j}"], 16)
                sp.dma_start(x[j][:, :], dr[z + "x"](u)).then_inc(sem[f"{z}in{j}"], 16)

            def store(u, j):
                sp.wait_ge(sem[z + "y"], u + 1)
                settle()
                sp.dma_start(dr[z + "y"](u), y[j][:, :]).then_inc(sem[f"{z}stored{j}"], 16)
                sp.wait_ge(sem[z + "yT"], u + 1)
                settle()
                sp.dma_start(dr[z + "yT"](u), yT[j][:, :, :]).then_inc(sem[f"{z}stored{j}"], 16)

            def step(s, j):
                if has(s, 0):
                    load(s, j)
                if has(s, R - 1):
                    store(s - (R - 1), (j + 1) % R)

            for j in range(R):
                sp.sem_inc(sem[f"{z}stored{j}"], 32)
            c = sem[z + "const_in"]
            sp.dma_start(wo[:, :, :], dr[z + "wo"]).then_inc(c, 16)
            sp.dma_start(bo[:, :], dr[z + "bo"]).then_inc(c, 16)
            sp.dma_start(ident[:, :], dr["ident"]).then_inc(c, 16)
            if affine:
                sp.dma_start(gamma[:, :], dr["gamma"]).then_inc(c, 16)
                sp.dma_start(beta[:, :], dr["beta"]).then_inc(c, 16)
            steps(sp, step)
            for j in range(R):
                sp.wait_ge(sem[f"{z}stored{j}"], 32 * (UNITS // R) + 32)

        @block.tensor
        def _(pe):
            def project(u, j):
                pe.wait_ge(sem[f"{z}in{j}"], (u - j) * (32 // R) + 32)
                if not early(u, 4):
                    pe.wait_ge(sem[z + "summed"], u - 3)
                for k in range(chunks):
                    mm = pe.matmul(ps_o[j % 4][:, :], cT[j][:, k, :], wo[:, k, :], start=(k == 0), stop=(k == chunks - 1))
                mm.then_inc(sem[z + "projected"], 1)

            def turn(u, j):
                pe.wait_ge(sem[z + "y"], u + 1)
                if not early(u, 2):
                    pe.wait_ge(sem[z + "yT"], u - 1)
                for k in range(K4):
                    mm = pe.transpose(ps_y[j % 2][:, k * P:(k + 1) * P], y[j][:, k * P:(k + 1) * P], ident[:, :])
                mm.then_inc(sem[z + "turned"], 1)

            def step(s, j):
                if has(s, 0):
                    project(s, j)
                if has(s, TURN):
                    turn(s - TURN, (j - TURN) % R)

            pe.wait_ge(sem[z + "const_in"], const_in)
            steps(pe, step)

        @block.gpsimd
        def _(pool):
            def step(s, j):
                if not has(s, 0):
                    return
                pool.wait_ge(sem[f"{z}in{j}"], (s - j) * (32 // R) + 32)
                if not early(s, R):
                    pool.wait_ge(sem[z + "summed"], s - R + 1)
                    if affine:
                        pool.wait_ge(sem[z + "shifted"], s - R + 1)
                pool.sem_inc(sem[z + "pool_waited"], 1)
                ins = pool.tensor_tensor(xb[j][:, :], x[j][:, :], bo[:, :], ALU.add)
                if affine:
                    ins.then_inc(sem[z + "biased_h"], 1)
                    ins = pool.tensor_tensor(xg[j][:, :], x[j][:, :], beta[:, :], ALU.add)
                ins.then_inc(sem[z + "biased"], 1)

            pool.wait_ge(sem[z + "const_in"], const_in)
            steps(pool, step)

        @block.vector
        def _(dve):
            def stats(u, j, r):
                dve.wait_ge(sem[z + ("shifted" if affine and r else "summed")], u + 1)
                dve.bn_stats(st[j][:, r, 0:6], h[j][:, :]).then_inc(sem[f"{z}bn{r}"], 1)
                dve.wait_ge(sem[f"{z}bn{r}"], u + 1)
                dve.sem_inc(sem[z + "dve_waited"], 1)
                dve.bn_aggr(st[j][:, r, 6:8], st[j][:, r, 0:6]).then_inc(sem[f"{z}var{r}"], 1)

            def scales(u, j, r):
                s_ = st[j]
                dve.wait_ge(sem[f"{z}std{r}"], u + 1)
                dve.reciprocal(s_[:, r, 9:10], s_[:, r, 8:9]).then_inc(sem[f"{z}inv{r}"], 1)
                dve.wait_ge(sem[f"{z}inv{r}"], u + 1)
                dve.scalar_tensor_tensor(s_[:, r, 10:11], s_[:, r, 6:7], -1.0, s_[:, r, 9:10], ALU.mult, ALU.mult)\
                   .then_inc(sem[f"{z}scales{r}"], 1)

            def add(u, j):
                dve.wait_ge(sem[z + "projected"], u + 1)
                dve.wait_ge(sem[z + ("biased_h" if affine else "biased")], u + 1)
                if not early(u, R):
                    dve.wait_ge(sem[z + "y"], u - R + 1)
                ins = dve.tensor_tensor(h[j][:, :], ps_o[j % 4][:, :], xb[j][:, :], ALU.add)
                ins.then_inc(sem[z + "summed"], 1)

            def shift(u, j):
                dve.wait_ge(sem[z + "normed"], u + 1)
                dve.tensor_tensor(h[j][:, :], h[j][:, :], gamma[:, :], ALU.mult).then_inc(sem[z + "scaled"], 1)
                dve.wait_ge(sem[z + "biased"], u + 1)
                dve.wait_ge(sem[z + "scaled"], u + 1)
                dve.tensor_tensor(h[j][:, :], h[j][:, :], xg[j][:, :], ALU.add).then_inc(sem[z + "shifted"], 1)

            def turned_out(u, j):
                dve.wait_ge(sem[z + "turned"], u + 1)
                dve.wait_ge(sem[f"{z}stored{j}"], (u - j) * (32 // R) + 32)
                dve.tensor_copy(yT[j][:, :, :], ps_y[j % 2][:, :].rearrange("p (k n) -> p k n", k=K4))\
                   .then_inc(sem[z + "yT"], 1)

            def step(s, j):
                if has(s, 0):
                    add(s, j)
                    stats(s, j, rounds[0])
                if affine and has(s, SCALES0):
                    scales(s - SCALES0, (j - SCALES0) % R, 0)
                if affine and has(s, SHIFT):
                    shift(s - SHIFT, (j - SHIFT) % R)
                    stats(s - SHIFT, (j - SHIFT) % R, 1)
                if has(s, SCALES1):
                    scales(s - SCALES1, (j - SCALES1) % R, 1)
                if has(s, OUT):
                    turned_out(s - OUT, (j - OUT) % R)

            for r in range(2):
                dve.memset(eps[:, r:r + 1], (EPS_ATTN, EPS)[r]).then_inc(sem[z + "eps"], 1)
            dve.wait_ge(sem[z + "const_in"], const_in)
            steps(dve, step)

        @block.scalar
        def _(act):
            def std(u, j, r):
                act.wait_ge(sem[f"{z}var{r}"], u + 1)
                act.activation(st[j][:, r, 8:9], st[j][:, r, 7:8], ACT.Sqrt, bias=eps[:, r:r + 1])\
                   .then_inc(sem[f"{z}std{r}"], 1)

            def norm(u, j, r):
                act.wait_ge(sem[f"{z}scales{r}"], u + 1)
                dst, done = (h[j], "normed") if r == 0 else (y[j], "y")
                if r == 1:
                    act.wait_ge(sem[f"{z}stored{j}"], (u - j) * (32 // R) + 32)
                act.activation(dst[:, :], h[j][:, :], ACT.Identity, bias=st[j][:, r, 10:11],
                               scale=st[j][:, r, 9:10]).then_inc(sem[z + done], 1)

            def step(s, j):
                if has(s, 0):
                    std(s, j, rounds[0])
                if affine and has(s, SCALES0):
                    norm(s - SCALES0, (j - SCALES0) % R, 0)
                if affine and has(s, SHIFT):
                    std(s - SHIFT, (j - SHIFT) % R, 1)
                if has(s, SCALES1):
                    norm(s - SCALES1, (j - SCALES1) % R, 1)

            act.wait_ge(sem[z + "eps"], 2)
            steps(act, step)


def norm_sems(z):
    return [z + n for n in ["sp_waited", "pool_waited", "dve_waited", "const_in", "projected", "biased", "biased_h", "y", "yT",
                            "summed", "turned", "shifted", "scaled", "normed", "eps", "bn0", "bn1",
                            "var0", "var1", "std0", "std1", "inv0", "inv1", "scales0", "scales1"]
            + [f"in{j}" for j in range(8)] + [f"stored{j}" for j in range(8)]]

KD = 64
XH = 16
XW = XH * KD
PAIRS = B * (XH // 2)
NP = 2 * T4
LAG = 4
XP = XH // 2
SCALE_B = float(KD) ** -0.5


def cross_attention(nc, dr, sem):
    with ExitStack() as ctx:
        def sb(name, shape, dt=F32):
            return ctx.enter_context(nc.sbuf_tensor(name, shape, dt))

        def ps(name, shape):
            return ctx.enter_context(nc.psum_tensor(name, shape, F32))

        xT = [sb(f"b_xT{i}", [P, K4, S]) for i in range(2)]
        cT = [sb(f"b_cT{i}", [P, K4, S]) for i in range(2)]
        w = {n: [sb(f"b_w{n}{i}", [P, K4, P]) for i in range(2)] for n in "qkv"}
        bqk = [sb(f"b_bqk{i}", [P, 2]) for i in range(2)]
        bv = [sb(f"b_bv{i}", [P, P]) for i in range(2)]
        qz = [sb(f"b_qz{i}", [P, 2, S]) for i in range(2)]
        kT = [sb(f"b_kT{i}", [P, S]) for i in range(2)]
        v = [sb(f"b_v{i}", [P, T4, P]) for i in range(2)]
        sc = [sb(f"b_sc{i}", [P, S]) for i in range(NP)]
        mx = sb("b_mx", [P, NP])
        sm = sb("b_sm", [P, NP])
        inv = sb("b_inv", [P, NP])
        pt = [sb(f"b_pt{i}", [P, 2, T4, S]) for i in range(2)]
        cx = [sb(f"b_cx{i}", [P, S]) for i in range(2)]
        mask = sb("b_mask", [P, S])
        ident = sb("b_ident", [P, P])

        ps_p = ps("b_ps_p", [P, 2, 512])
        ps_v = ps("b_ps_v", [P, 512])
        ps_s = [ps(f"b_ps_s{i}", [P, 512]) for i in range(2)]
        ps_t = [ps(f"b_ps_t{i}", [P, 512]) for i in range(2)]
        ps_c = ps("b_ps_c", [P, 512])

        def width(i):
            return (i % T4 + 1) * P

        block = ctx.enter_context(nc.Block())

        @block.sync
        def _(sp):
            def settle():
                sp.sem_inc(sem["b_sp_waited"], 1)

            def load(n, par, first=False):
                if not first:
                    sp.wait_ge(sem["b_v_ready"], n - 1)
                    settle()
                    sp.wait_ge(sem["b_v_out"], n - 1)
                    settle()
                    sp.wait_ge(sem["b_qk_out"], 3 * (n - 1))
                    settle()
                s = sem[f"b_in{par}"]
                sp.dma_start(w["q"][par][:, :, :], dr["b_wq"](n)).then_inc(s, 16)
                sp.dma_start(xT[par][:, :, :], dr["x1T"](n)).then_inc(s, 16)
                sp.dma_start(w["k"][par][:, :, :], dr["b_wk"](n)).then_inc(s, 16)
                sp.dma_start(cT[par][:, :, :], dr["ctxT"](n)).then_inc(s, 16)
                sp.dma_start(w["v"][par][:, :, :], dr["b_wv"](n)).then_inc(s, 16)
                sp.dma_start(bqk[par][:, :], dr["b_bqk"](n)).then_inc(s, 16)
                sp.dma_start(bv[par][:, :], dr["b_bv"](n)).then_inc(s, 16)

            def store(n, par):
                sp.wait_ge(sem["b_cx_out"], n + 1)
                settle()
                sp.dma_start(dr["b_cxT"](n), cx[par][:, :]).then_inc(sem[f"b_stored{par}"], 16)

            for i in range(2):
                sp.sem_inc(sem[f"b_stored{i}"], 16)
            sp.dma_start(ident[:, :], dr["ident"]).then_inc(sem["b_const_in"], 16)
            sp.dma_start(mask[:, :], dr["mask"]).then_inc(sem["b_const_in"], 16)
            load(0, 0, first=True)
            load(1, 1, first=True)
            load(2, 0)
            load(3, 1)
            store(0, 0)
            with sp.Fori(4, PAIRS - 1, 2) as n:
                load(n, 0)
                store(n - 3, 1)
                load(n + 1, 1)
                store(n - 2, 0)
            store(PAIRS - 3, 1)
            store(PAIRS - 2, 0)
            store(PAIRS - 1, 1)
            for i in range(2):
                sp.wait_ge(sem[f"b_stored{i}"], 16 * (PAIRS // 2) + 16)

        @block.tensor
        def _(pe):
            def unit(n, par, u):
                if u == 0:
                    pe.wait_ge(sem[f"b_in{par}"], (n - par) * 56 + 112)
                if u in (0, 2):
                    if not (isinstance(n, int) and n == 0):
                        pe.wait_ge(sem["b_qk_out"], 3 * n - (1 if u == 0 else 0))
                if u == 4 and not (isinstance(n, int) and n == 0):
                    pe.wait_ge(sem["b_v_out"], n)
                if u < 4:
                    i, name, src = (0, "q", xT) if u < 2 else (1, "k", cT)
                    for k in (2 * (u % 2), 2 * (u % 2) + 1):
                        mm = pe.matmul(ps_p[:, i, :], w[name][par][:, k, :], src[par][:, k, :],
                                       start=(k == 0), stop=(k == K4 - 1))
                    if u % 2:
                        mm.then_inc(sem[f"b_{name}_ready"], 1)
                else:
                    for t in (2 * (u % 2), 2 * (u % 2) + 1):
                        for k in range(K4):
                            mm = pe.matmul(ps_v[:, t * P:(t + 1) * P], cT[par][:, k, t * P:(t + 1) * P],
                                           w["v"][par][:, k, :], start=(k == 0), stop=(k == K4 - 1))
                    if u == 5:
                        mm.then_inc(sem["b_v_ready"], 1)

            def score(n, par, i):
                h, t = i // T4, i % T4
                if i == 0:
                    pe.wait_ge(sem["b_qk_out"], 3 * n + 3)
                if not (isinstance(n, int) and n == 0 and i < 2):
                    pe.wait_ge(sem["b_summed"], NP * n + i - 1)
                pe.matmul(ps_s[i % 2][:, 0:width(i)], qz[par][:, h, t * P:(t + 1) * P], kT[par][:, 0:width(i)],
                          start=True, stop=True).then_inc(sem["b_score"], 1)

            def turn(n, i):
                pe.wait_ge(sem["b_normed"], NP * n + i + 1)
                if not (isinstance(n, int) and n == 0 and i < 2):
                    pe.wait_ge(sem["b_pt_out"], NP * n + i - 1)
                for r in range(i % T4 + 1):
                    mm = pe.transpose(ps_t[i % 2][:, r * P:(r + 1) * P], sc[i][:, r * P:(r + 1) * P], ident[:, :])
                mm.then_inc(sem["b_turned"], 1)

            def context(n, par):
                pe.wait_ge(sem["b_pt_out"], NP * n + NP)
                for r in range(T4):
                    for h in range(2):
                        mm = pe.matmul(ps_c[KD * h:KD * (h + 1), r * P:S], v[par][:, r, KD * h:KD * (h + 1)],
                                       pt[par][:, h, r, r * P:S], start=(r == 0), stop=(r == T4 - 1))
                mm.then_inc(sem["b_cx_ready"], 1)

            def pe_pair(n, par, first=False, last=False):
                for i in range(NP):
                    score(n, par, i)
                    if i == LAG and not first:
                        context(n - 1, 1 - par)
                    if i < 6 and not last:
                        unit(n + 1, 1 - par, i)
                    if i >= LAG:
                        turn(n, i - LAG)
                    elif not first:
                        turn(n - 1, NP + i - LAG)

            pe.wait_ge(sem["b_const_in"], 32)
            for u in range(6):
                unit(0, 0, u)
            pe_pair(0, 0, first=True)
            with pe.Fori(1, PAIRS - 1, 2) as n:
                pe_pair(n, 1)
                pe_pair(n + 1, 0)
            pe_pair(PAIRS - 1, 1, last=True)
            for i in range(NP - LAG, NP):
                turn(PAIRS - 1, i)
            context(PAIRS - 1, 1)

        @block.scalar
        def _(act):
            def q_out(n, par):
                act.wait_ge(sem["b_q_ready"], n + 1)
                for h in range(2):
                    r = slice(KD * h, KD * (h + 1))
                    act.activation(qz[par][r, h, :], ps_p[r, 0, :], ACT.Identity, bias=bqk[par][r, 0:1])\
                       .then_inc(sem["b_qk_out"], 1)

            def k_out(n, par):
                act.wait_ge(sem["b_k_ready"], n + 1)
                act.activation(kT[par][:, :], ps_p[:, 1, :], ACT.Identity, bias=bqk[par][:, 1:2])\
                   .then_inc(sem["b_qk_out"], 1)

            def softexp(n, i):
                act.wait_ge(sem["b_summed"], NP * n + i + 1)
                act.activation(sc[i][:, 0:width(i)], sc[i][:, 0:width(i)], ACT.Exp,
                               bias=mx[:, i:i + 1], scale=-1.0,
                               accum_out=sm[:, i:i + 1]).then_inc(sem["b_exped"], 1)

            def act_pair(n, par, last=False):
                for i in range(NP):
                    softexp(n, i)
                    if not last and i == 2:
                        q_out(n + 1, 1 - par)
                    if not last and i == 4:
                        k_out(n + 1, 1 - par)

            act.wait_ge(sem["b_zeroed"], 2)
            q_out(0, 0)
            k_out(0, 0)
            act_pair(0, 0)
            with act.Fori(1, PAIRS - 1, 2) as n:
                act_pair(n, 1)
                act_pair(n + 1, 0)
            act_pair(PAIRS - 1, 1, last=True)

        @block.vector
        def _(dve):
            def v_out(n, par):
                dve.wait_ge(sem["b_v_ready"], n + 1)
                for t in range(T4):
                    ins = dve.tensor_tensor(v[par][:, t, :], ps_v[:, t * P:(t + 1) * P], bv[par][:, :], ALU.add)
                ins.then_inc(sem["b_v_out"], 1)

            def add_max(n, i):
                c = S - width(i)
                dve.wait_ge(sem["b_score"], NP * n + i + 1)
                if not (isinstance(n, int) and n == 0):
                    dve.wait_ge(sem["b_turned"], NP * (n - 1) + i + 1)
                dve.sem_inc(sem["b_dve_waited"], 1)
                dve.tensor_tensor_reduce(out=sc[i][:, 0:width(i)], in0=ps_s[i % 2][:, 0:width(i)],
                                         in1=mask[:, c:S], scale=-SCALE_B, scalar=BIG, op0=ALU.add, op1=ALU.min,
                                         accum_out=mx[:, i:i + 1]).then_inc(sem["b_summed"], 1)

            def invert(n, i):
                dve.wait_ge(sem["b_exped"], NP * n + i + 1)
                dve.reciprocal(inv[:, i:i + 1], sm[:, i:i + 1]).then_inc(sem["b_inverse"], 1)

            def pt_out(n, par, i):
                h, t = i // T4, i % T4
                dve.wait_ge(sem["b_turned"], NP * n + i + 1)
                dve.tensor_copy(pt[par][:, h, 0:t + 1, t * P:(t + 1) * P],
                                ps_t[i % 2][:, 0:width(i)].rearrange("p (r n) -> p r n", n=P))\
                   .then_inc(sem["b_pt_out"], 1)

            def cx_out(n, par):
                dve.wait_ge(sem["b_cx_ready"], n + 1)
                dve.wait_ge(sem[f"b_stored{par}"], (n - par) * 8 + 16)
                dve.tensor_copy(cx[par][:, :], ps_c[:, :]).then_inc(sem["b_cx_out"], 1)

            def dve_pair(n, par, first=False, last=False):
                for i in range(NP):
                    add_max(n, i)
                    if i:
                        invert(n, i - 1)
                    if i >= LAG:
                        pt_out(n, par, i - LAG)
                    elif not first:
                        pt_out(n - 1, 1 - par, NP + i - LAG)
                    if i == LAG + 1 and not first:
                        cx_out(n - 1, 1 - par)
                    if i == NP - 1 and not last:
                        v_out(n + 1, 1 - par)
                invert(n, NP - 1)

            for i in range(2):
                dve.memset(qz[i][:, :, :], 0.0).then_inc(sem["b_zeroed"], 1)
            dve.wait_ge(sem["b_const_in"], 32)
            v_out(0, 0)
            dve_pair(0, 0, first=True)
            with dve.Fori(1, PAIRS - 1, 2) as n:
                dve_pair(n, 1)
                dve_pair(n + 1, 0)
            dve_pair(PAIRS - 1, 1, last=True)
            for i in range(NP - LAG, NP):
                pt_out(PAIRS - 1, 1, i)
            cx_out(PAIRS - 1, 1)

        @block.gpsimd
        def _(pool):
            def norm(n, i):
                pool.wait_ge(sem["b_inverse"], NP * n + i + 1)
                pool.sem_inc(sem["b_pool_waited"], 1)
                pool.tensor_scalar(sc[i][:, 0:width(i)], sc[i][:, 0:width(i)], inv[:, i:i + 1], None,
                                   ALU.mult).then_inc(sem["b_normed"], 1)

            with pool.Fori(0, PAIRS) as n:
                for i in range(NP):
                    norm(n, i)


B_SEMS = (["b_dve_waited", "b_pool_waited", "b_sp_waited", "b_const_in", "b_in0", "b_in1", "b_v_ready", "b_q_ready",
           "b_k_ready", "b_qk_out", "b_v_out", "b_cx_out", "b_stored0", "b_stored1", "b_score", "b_summed", "b_exped",
           "b_inverse", "b_normed", "b_turned", "b_pt_out", "b_cx_ready", "b_zeroed"])

NS = 16
HS = H * NS
SB = NS * B
SCALE_F = float(D) ** -0.5


def loop(e, n, step, lag):
    for s in range(2):
        step(s, s)
    with e.Fori(2, n - 2, 2) as s:
        for j in range(2):
            step(s + j, j)
    for s in range(n - 2, n + lag):
        step(s, s % 2)


def inside(s, lag, n):
    return not isinstance(s, int) or 0 <= s - lag < n


def early(s, n):
    return isinstance(s, int) and s < n


def slot_attention(nc, dr, sem):
    with ExitStack() as ctx:
        def sb(name, shape, dt=F32):
            return ctx.enter_context(nc.sbuf_tensor("c_" + name, shape, dt))

        def ps(name, shape):
            return ctx.enter_context(nc.psum_tensor("c_" + name, shape, F32))

        wq, wkT, wv, wo = (sb(n, [P, K4, E]) for n in ("wq", "wkT", "wv", "wo"))
        sqT = sb("sqT", [P, K4, NS])
        cols = sb("cols", [P, 3, K4])
        slots = sb("slots", [P, E])
        bo, gamma, beta = (sb(n, [P, E]) for n in ("bo", "gamma", "beta"))
        ident = sb("ident", [P, P])
        qd = sb("qd", [P, K4, HQ, NS])
        a = sb("a", [P, K4, HS])
        cb = sb("cb", [P, 2])
        xT = [sb(f"xT{i}", [P, K4, S]) for i in range(2)]
        x = [sb(f"x{i}", [P, T4, E]) for i in range(2)]
        sc = [sb(f"sc{i}", [P, 2, S]) for i in range(2)]
        st = [sb(f"st{i}", [P, 2, 3]) for i in range(2)]
        pt = sb("pt", [P, T4, HS])
        yT = sb("yT", [P, B, K4, HS])
        cx = sb("cx", [P, K4, SB])
        o = sb("o", [P, E])
        h = sb("h", [P, E])
        hT = sb("hT", [P, K4, SB])
        ns = sb("ns", [P, 16])
        eps = sb("eps", [P, 1])

        ps_s = ps("ps_s", [P, 2, 512])
        ps_t = ps("ps_t", [P, 2, 512])
        ps_y = ps("ps_y", [P, 2, 512])
        ps_a = ps("ps_a", [P, 2, 512])

        block = ctx.enter_context(nc.Block())

        @block.sync
        def _(sp):
            def settle():
                sp.sem_inc(sem["c_sp_waited"], 1)

            def load(b, j):
                if not early(b, 2):
                    sp.wait_ge(sem["c_mixed"], b - 1)
                    settle()
                sp.dma_start(xT[j][:, :, :], dr["x2T"](b)).then_inc(sem[f"c_in{j}"], 16)
                sp.dma_start(x[j][:, :, :], dr["x2"](b)).then_inc(sem[f"c_in{j}"], 16)

            for tile, n in ((wq[:, :, :], "d_wq"), (sqT[:, :, :], "sqT"), (cols[:, :, :], "d_cols"),
                            (wkT[:, :, :], "d_wkT"), (wv[:, :, :], "d_wv"), (wo[:, :, :], "d_wo"),
                            (slots[:, :], "slots"), (bo[:, :], "d_bo"), (gamma[:, :], "e_g"), (beta[:, :], "e_b"),
                            (ident[:, :], "ident")):
                sp.dma_start(tile, dr[n]).then_inc(sem["c_const_in"], 16)
            loop(sp, B, lambda s, j: load(s, j) if inside(s, 0, B) else None, 0)
            sp.wait_ge(sem["c_o"], 2)
            sp.dma_start(dr["o1"], o[:, :]).then_inc(sem["c_stored"], 16)
            sp.wait_ge(sem["c_hT"], 1)
            sp.dma_start(dr["hT"], hT[:, :, :]).then_inc(sem["c_stored"], 16)
            sp.wait_ge(sem["c_stored"], 32)

        @block.tensor
        def _(pe):
            def scores(b, j):
                pe.wait_ge(sem[f"c_in{j}"], (b - j) * 16 + 32)
                if not early(b, 1):
                    pe.wait_ge(sem["c_scaled"], 2 * b)
                for t in range(2):
                    for k in range(K4):
                        mm = pe.matmul(ps_s[:, t, :], a[:, k, t * P:(t + 1) * P], xT[j][:, k, :],
                                       start=(k == 0), stop=(k == K4 - 1))
                    mm.then_inc(sem["c_scored"], 1)

            def turn(b, j):
                pe.wait_ge(sem["c_probs"], 2 * b + 2)
                if not early(b, 1):
                    pe.wait_ge(sem["c_pt"], 2 * b)
                for t in range(2):
                    for r in range(T4):
                        mm = pe.transpose(ps_t[:, t, r * P:(r + 1) * P], sc[j][:, t, r * P:(r + 1) * P], ident[:, :])
                    mm.then_inc(sem["c_turned"], 1)

            def mix(b, j):
                pe.wait_ge(sem["c_pt"], 2 * b + 2)
                if not early(b, 1):
                    pe.wait_ge(sem["c_yT"], b)
                for k in range(K4):
                    for r in range(T4):
                        mm = pe.matmul(ps_y[:, k // 2, (k % 2) * HS:(k % 2 + 1) * HS], x[j][:, r, k * P:(k + 1) * P],
                                       pt[:, r, :], start=(r == 0), stop=(r == T4 - 1))
                mm.then_inc(sem["c_mixed"], 1)

            pe.wait_ge(sem["c_const_in"], 16 * 11)
            for m in range(K4):
                for k in range(K4):
                    mm = pe.matmul(ps_a[:, 0, m * NS:(m + 1) * NS], wq[:, k, m * P:(m + 1) * P], sqT[:, k, :],
                                   start=(k == 0), stop=(k == K4 - 1))
            mm.then_inc(sem["c_q_ready"], 1)
            pe.wait_ge(sem["c_qd"], 17)
            for m in range(K4):
                mm = pe.matmul(ps_a[64 * (m % 2):64 * (m % 2) + 64, 1, m // 2:m // 2 + 1],
                               qd[:, m, :, :].rearrange("p h s -> p (h s)"), cols[:, 1, m:m + 1], start=True, stop=True)
            mm.then_inc(sem["c_cb_ready"], 1)
            for k in range(K4):
                for m in range(K4):
                    mm = pe.matmul(ps_t[:, k // 2, (k % 2) * HS + m * 64:(k % 2) * HS + (m + 1) * 64],
                                   wkT[:, m, k * P:(k + 1) * P], qd[:, m, :, :].rearrange("p h s -> p (h s)"),
                                   start=True, stop=True)
            mm.then_inc(sem["c_a_ready"], 1)
            pe.wait_ge(sem["c_a"], 1)

            def step(s, j):
                if inside(s, 1, B):
                    turn(s - 1, 1 - j)
                if inside(s, 0, B):
                    scores(s, j)
                if inside(s, 1, B):
                    mix(s - 1, 1 - j)

            loop(pe, B, step, 1)
            pe.wait_ge(sem["c_yT"], B)
            for m in range(K4):
                for k in range(K4):
                    for hh in range(HQ):
                        c = HQ * m + hh
                        mm = pe.matmul(ps_a[D * hh:D * (hh + 1), 0, m * SB:(m + 1) * SB], wv[:, k, c * D:(c + 1) * D],
                                       yT[:, :, k, c * NS:(c + 1) * NS].rearrange("p b s -> p s b"),
                                       start=(k == 0), stop=(k == K4 - 1))
            mm.then_inc(sem["c_cx_ready"], 1)
            pe.wait_ge(sem["c_cx"], 1)
            for m in range(K4):
                mm = pe.matmul(ps_a[:, 1, :], cx[:, m, :], wo[:, m, :], start=(m == 0), stop=(m == K4 - 1))
            mm.then_inc(sem["c_o_ready"], 1)
            pe.wait_ge(sem["c_h"], 3)
            for k in range(K4):
                mm = pe.transpose(ps_s[:, 0, k * P:(k + 1) * P], h[:, k * P:(k + 1) * P], ident[:, :])
            mm.then_inc(sem["c_hT_ready"], 1)

        @block.vector
        def _(dve):
            chain = [0]

            def link(ins):
                chain[0] += 1
                ins.then_inc(sem["c_chain"], 1)
                dve.wait_ge(sem["c_chain"], chain[0])

            dve.memset(qd[:, :, :, :], 0.0).then_inc(sem["c_qd"], 1)
            dve.memset(eps[:, :], EPS).then_inc(sem["c_eps"], 1)
            dve.wait_ge(sem["c_const_in"], 16 * 11)
            dve.wait_ge(sem["c_qd"], 1)
            dve.wait_ge(sem["c_q_ready"], 1)
            for m in range(K4):
                for hh in range(HQ):
                    r = slice(D * hh, D * (hh + 1))
                    dve.tensor_scalar(qd[r, m, hh, :], ps_a[r, 0, m * NS:(m + 1) * NS], cols[r, 0, m:m + 1], None,
                                      ALU.add).then_inc(sem["c_qd"], 1)
            dve.wait_ge(sem["c_cb_ready"], 1)
            dve.tensor_copy(cb[:, :], ps_a[:, 1, 0:2])
            dve.wait_ge(sem["c_a_ready"], 1)
            link(dve.tensor_copy(a[:, :, :].rearrange("p (u k) n -> p u (k n)", u=2), ps_t[:, :, :]))
            dve.sem_inc(sem["c_a"], 1)

            def soft(b, j):
                for t in range(2):
                    dve.wait_ge(sem["c_scored"], 2 * b + t + 1)
                    if not early(b, 2):
                        dve.wait_ge(sem["c_turned"], 2 * (b - 1))
                    dve.tensor_scalar(sc[j][:, t, :], ps_s[:, t, :], cb[:, t:t + 1], -SCALE_F, ALU.add, ALU.mult)\
                       .then_inc(sem["c_scaled"], 1)
                for t in range(2):
                    dve.wait_ge(sem["c_scaled"], 2 * b + t + 1)
                    dve.tensor_reduce(st[j][:, t, 0:1], sc[j][:, t, :], AX.X, ALU.min).then_inc(sem["c_max"], 1)
                for t in range(2):
                    dve.wait_ge(sem["c_exped"], 2 * b + t + 1)
                    dve.reciprocal(st[j][:, t, 2:3], st[j][:, t, 1:2]).then_inc(sem["c_inv"], 1)
                for t in range(2):
                    dve.wait_ge(sem["c_inv"], 2 * b + t + 1)
                    dve.tensor_scalar(sc[j][:, t, :], sc[j][:, t, :], st[j][:, t, 2:3], None, ALU.mult)\
                       .then_inc(sem["c_probs"], 1)

            def out(b, j):
                dve.wait_ge(sem["c_mixed"], b + 1)
                dve.tensor_copy(yT[:, b, :, :].rearrange("p (u k) n -> p u (k n)", u=2), ps_y[:, :, :])\
                   .then_inc(sem["c_yT"], 1)

            def step(s, j):
                if inside(s, 0, B):
                    soft(s, j)
                if inside(s, 1, B):
                    out(s - 1, 1 - j)

            loop(dve, B, step, 1)
            dve.wait_ge(sem["c_cx_ready"], 1)
            for m in range(K4):
                ins = dve.tensor_scalar(cx[:, m, :], ps_a[:, 0, m * SB:(m + 1) * SB], cols[:, 2, m:m + 1], None, ALU.add)
            ins.then_inc(sem["c_cx"], 1)
            link(dve.tensor_tensor(slots[:, :], slots[:, :], bo[:, :], ALU.add))
            dve.wait_ge(sem["c_o_ready"], 1)
            dve.tensor_tensor(o[:, :], ps_a[:, 1, :], slots[:, :], ALU.add).then_inc(sem["c_o"], 1)
            dve.wait_ge(sem["c_o"], 1)
            link(dve.bn_stats(ns[:, 0:6], o[:, :]))
            dve.bn_aggr(ns[:, 6:8], ns[:, 0:6]).then_inc(sem["c_o"], 1)
            dve.wait_ge(sem["c_std"], 1)
            link(dve.reciprocal(ns[:, 9:10], ns[:, 8:9]))
            dve.tensor_scalar(h[:, :], o[:, :], ns[:, 6:7], ns[:, 9:10], ALU.subtract, ALU.mult).then_inc(sem["c_h"], 1)
            dve.wait_ge(sem["c_h"], 1)
            dve.tensor_tensor(h[:, :], h[:, :], gamma[:, :], ALU.mult).then_inc(sem["c_h"], 1)
            dve.wait_ge(sem["c_h"], 2)
            dve.tensor_tensor(h[:, :], h[:, :], beta[:, :], ALU.add).then_inc(sem["c_h"], 1)
            dve.wait_ge(sem["c_hT_ready"], 1)
            dve.tensor_copy(hT[:, :, :].rearrange("p k n -> p (k n)"), ps_s[:, 0, :]).then_inc(sem["c_hT"], 1)

        @block.scalar
        def _(act):
            def pt_out(b):
                for t in range(2):
                    act.wait_ge(sem["c_turned"], 2 * b + t + 1)
                    if not early(b, 1):
                        act.wait_ge(sem["c_mixed"], b)
                    act.activation(pt[:, :, t * P:(t + 1) * P], ps_t[:, t, :].rearrange("p (r n) -> p r n", r=T4),
                                   ACT.Copy).then_inc(sem["c_pt"], 1)

            def step(b, j):
                if inside(b, 1, B):
                    pt_out(b - 1)
                if not inside(b, 0, B):
                    return
                for t in range(2):
                    act.wait_ge(sem["c_max"], 2 * b + t + 1)
                    act.activation(sc[j][:, t, :], sc[j][:, t, :], ACT.Exp, bias=st[j][:, t, 0:1], scale=-1.0,
                                   accum_out=st[j][:, t, 1:2]).then_inc(sem["c_exped"], 1)

            loop(act, B, step, 1)
            act.wait_ge(sem["c_eps"], 1)
            act.wait_ge(sem["c_o"], 2)
            act.activation(ns[:, 8:9], ns[:, 7:8], ACT.Sqrt, bias=eps[:, :]).then_inc(sem["c_std"], 1)


C_SEMS = ["c_" + n for n in ["sp_waited", "mixed", "const_in", "in0", "in1", "o", "stored", "hT", "scaled", "scored",
                             "probs", "pt", "turned", "yT", "q_ready", "qd", "cb_ready", "a_ready", "a", "cx_ready",
                             "cx", "o_ready", "h", "hT_ready", "chain", "eps", "max", "exped", "inv", "std"]]

F = 2048
FC = F // P
FQ = F // 512


def experts(nc, dr, sem):
    with ExitStack() as ctx:
        def sb(name, shape, dt=F32):
            return ctx.enter_context(nc.sbuf_tensor("d_" + name, shape, dt))

        def ps(name, shape):
            return ctx.enter_context(nc.psum_tensor("d_" + name, shape, F32))

        w1 = [sb(f"w1{i}", [P, K4, F]) for i in range(2)]
        wg = [sb(f"wg{i}", [P, K4, F]) for i in range(2)]
        w2 = [sb(f"w2{i}", [P, FC, E]) for i in range(2)]
        hT = sb("hT", [P, K4, SB + 24])
        hs = sb("hs", [P, K4, 32])
        bias = sb("bias", [P, NS, 2, FC])
        ident = sb("ident", [P, P])
        pre = sb("pre", [P, 2, 512])
        act_in = sb("act_in", [P, 2, FC, B])
        act_e = sb("act_e", [P, 2, FC, B])
        prod = sb("prod", [P, FC, B])
        y = sb("y", [32 + B, E])

        ps_u = ps("ps_u", [P, 2, 512])
        ps_t = ps("ps_t", [P, 2, 512])
        ps_y = ps("ps_y", [B, 512])

        block = ctx.enter_context(nc.Block())

        @block.sync
        def _(sp):
            def settle():
                sp.sem_inc(sem["d_sp_waited"], 1)

            def step(e, j):
                if not early(e, 2):
                    sp.wait_ge(sem["d_wide"], 2 * e - 3)
                    settle()
                sp.dma_start(w1[j][:, :, :], dr["w1"](e)).then_inc(sem[f"d_w1_in{j}"], 16)
                if not early(e, 2):
                    sp.wait_ge(sem["d_wide"], 2 * e - 2)
                    settle()
                sp.dma_start(wg[j][:, :, :], dr["wg"](e)).then_inc(sem[f"d_wg_in{j}"], 16)
                if not early(e, 2):
                    sp.wait_ge(sem["d_narrow"], e - 1)
                    settle()
                sp.dma_start(w2[j][:, :, :], dr["w2"](e)).then_inc(sem[f"d_w2_in{j}"], 16)

            sp.dma_start(hT[:, :, 0:SB], dr["hT"]).then_inc(sem["d_const_in"], 16)
            sp.dma_start(bias[:, :, :, :], dr["e_bias"]).then_inc(sem["d_const_in"], 16)
            sp.dma_start(ident[:, :], dr["ident"]).then_inc(sem["d_const_in"], 16)
            loop(sp, NS, step, 0)

        @block.tensor
        def _(pe):
            def step(e, j):
                pe.wait_ge(sem["d_hs"], e + 1)
                for i, w in enumerate((w1, wg)):
                    pe.wait_ge(sem[f"d_w{'1g'[i]}_in{j}"], (e - j) * 8 + 16)
                    if not early(e, 1):
                        pe.wait_ge(sem[("d_pre", "d_pre_g")[i]], e)
                    for k in range(K4):
                        for f in range(FQ):
                            mm = pe.matmul(ps_u[32 * f:32 * f + 32, i, :], hs[:, k, :],
                                           w[j][:, k, f * 512:(f + 1) * 512], start=(k == 0), stop=(k == K4 - 1))
                    mm.then_inc(sem["d_wide"], 1)
                for i in range(2):
                    pe.wait_ge(sem[("d_pre", "d_pre_g")[i]], e + 1)
                    if not early(e, 1):
                        pe.wait_ge(sem["d_in"], 2 * e - 1 + i)
                    for c in range(4):
                        mm = pe.transpose(ps_t[:, i, c * P:(c + 1) * P], pre[:, i, c * P:(c + 1) * P], ident[:, :])
                    mm.then_inc(sem["d_turned"], 1)
                pe.wait_ge(sem[f"d_w2_in{j}"], (e - j) * 8 + 16)
                pe.wait_ge(sem["d_prod"], e + 1)
                if not early(e, 1):
                    pe.wait_ge(sem["d_y"], e)
                for n in range(FC):
                    c, f = n // FQ, n % FQ
                    mm = pe.matmul(ps_y[:, :], prod[:, n, :], w2[j][:, 4 * f + c, :], start=(n == 0), stop=(n == FC - 1))
                mm.then_inc(sem["d_narrow"], 1)

            pe.wait_ge(sem["d_const_in"], 48)
            loop(pe, NS, step, 0)

        @block.vector
        def _(dve):
            def step(e, j):
                if not early(e, 1):
                    dve.wait_ge(sem["d_wide"], 2 * e)
                dve.tensor_copy(hs[:, :, :], hT[:, :, bass.ds(e * B, 32)]).then_inc(sem["d_hs"], 1)
                dve.wait_ge(sem["d_wide"], 2 * e + 2)
                if not early(e, 1):
                    dve.wait_ge(sem["d_turned"], 2 * e)
                dve.tensor_copy(pre[:, 1, :], ps_u[:, 1, :]).then_inc(sem["d_pre_g"], 1)
                for i in range(2):
                    dve.wait_ge(sem["d_turned"], 2 * e + i + 1)
                    dve.tensor_tensor(act_in[:, i, :, :],
                                      ps_t[:, i, :].rearrange("p (n r) -> p n r", r=32)[:, :, 0:B],
                                      bias[:, e, i, :].unsqueeze(2).to_broadcast([P, FC, B]), ALU.add)\
                       .then_inc(sem["d_in"], 1)
                dve.wait_ge(sem["d_exp"], e + 1)
                dve.tensor_scalar(act_e[:, :, :, :], act_e[:, :, :, :], 1.0, None, ALU.add).then_inc(sem["d_one"], 1)
                dve.wait_ge(sem["d_one"], e + 1)
                dve.reciprocal(act_e[:, :, :, :], act_e[:, :, :, :]).then_inc(sem["d_inv"], 1)
                dve.wait_ge(sem["d_inv"], e + 1)
                dve.tensor_tensor(act_e[:, :, :, :], act_e[:, :, :, :], act_in[:, :, :, :], ALU.mult)\
                   .then_inc(sem["d_silu"], 1)
                dve.wait_ge(sem["d_silu"], e + 1)
                if not early(e, 1):
                    dve.wait_ge(sem["d_narrow"], e)
                dve.tensor_tensor(prod[:, :, :], act_e[:, 0, :, :], act_e[:, 1, :, :], ALU.mult)\
                   .then_inc(sem["d_prod"], 1)
                dve.wait_ge(sem["d_narrow"], e + 1)
                if not early(e, 2):
                    dve.wait_ge(sem[f"d_stored{j}"], (e - j) * 8)
                dve.tensor_copy(y[32 * j:32 * j + B, :], ps_y[:, :]).then_inc(sem["d_y"], 1)

            dve.memset(hT[:, :, SB:SB + 24], 0.0).then_inc(sem["d_pad"], 1)
            dve.wait_ge(sem["d_pad"], 1)
            dve.wait_ge(sem["d_const_in"], 48)
            loop(dve, NS, step, 0)

        @block.scalar
        def _(act):
            def step(e, j):
                act.wait_ge(sem["d_wide"], 2 * e + 1)
                if not early(e, 1):
                    act.wait_ge(sem["d_turned"], 2 * e)
                act.activation(pre[:, 0, :], ps_u[:, 0, :], ACT.Copy).then_inc(sem["d_pre"], 1)
                act.wait_ge(sem["d_in"], 2 * e + 2)
                if not early(e, 1):
                    act.wait_ge(sem["d_prod"], e)
                act.activation(act_e[:, :, :, :], act_in[:, :, :, :], ACT.Exp, scale=-1.0).then_inc(sem["d_exp"], 1)

            loop(act, NS, step, 0)

        @block.gpsimd
        def _(pool):
            def step(e, j):
                pool.wait_ge(sem["d_y"], e + 1)
                pool.sem_inc(sem["d_pool_waited"], 1)
                pool.dma_start(dr["y"](e), y[32 * j:32 * j + B, :]).then_inc(sem[f"d_stored{j}"], 16)

            loop(pool, NS, step, 0)
            for j in range(2):
                pool.wait_ge(sem[f"d_stored{j}"], 8 * NS)


D_SEMS = ["d_" + n for n in ["sp_waited", "pool_waited", "wide", "narrow", "w1_in0", "w1_in1", "wg_in0", "wg_in1",
                             "w2_in0", "w2_in1", "const_in", "hs", "pre", "pre_g", "in", "turned", "prod", "y", "exp",
                             "one", "inv", "silu", "stored0", "stored1", "pad"]]


def slots_to_tokens(nc, dr, sem):
    with ExitStack() as ctx:
        def sb(name, shape, dt=F32):
            return ctx.enter_context(nc.sbuf_tensor("e_" + name, shape, dt))

        def ps(name, shape):
            return ctx.enter_context(nc.psum_tensor("e_" + name, shape, F32))

        wqT, wk, wv, wo = (sb(n, [P, K4, E]) for n in ("wqT", "wk", "wv", "wo"))
        cols = sb("cols", [P, 3, K4])
        bo = sb("bo", [P, E])
        ident = sb("ident", [P, P])
        o, y, b2 = (sb(n, [P, E]) for n in ("o", "y", "b2"))
        oT = sb("oT", [P, K4, SB])
        kd, vd = (sb(n, [P, K4, B, HQ, NS]) for n in ("kd", "vd"))
        bq = sb("bq", [P, K4, P])
        a = sb("a", [P, K4, B, K4, HQ * NS])
        cb = sb("cb", [P, B, K4, HQ * NS])
        vo = sb("vo", [P, B, 2, E])
        xT = [sb(f"xT{i}", [P, K4, S]) for i in range(2)]
        x = [sb(f"x{i}", [P, T4, E]) for i in range(2)]
        h = [sb(f"h{i}", [P, T4, E]) for i in range(2)]
        sc = [sb(f"sc{i}", [P, T4, HS]) for i in range(2)]
        mx, sm, inv = (sb(n, [P, T4 * H]) for n in ("mx", "sm", "inv"))
        pt = sb("pt", [P, 2, S])
        st = [sb(f"st{i}", [P, T4, 16]) for i in range(2)]
        eps = sb("eps", [P, 1])

        ps_s = ps("ps_s", [P, 2, 512])
        ps_t = ps("ps_t", [P, 2, 512])
        ps_o = [ps(f"ps_o{i}", [P, 2, 512]) for i in range(2)]

        const_in = 16 * 10
        block = ctx.enter_context(nc.Block())

        @block.sync
        def _(sp):
            def settle():
                sp.sem_inc(sem["e_sp_waited"], 1)

            def load(b, j):
                if not early(b, 2):
                    sp.wait_ge(sem["e_scored"], b - 1)
                    settle()
                    sp.wait_ge(sem["e_xb"], b - 1)
                    settle()
                sp.dma_start(xT[j][:, :, :], dr["x2T"](b)).then_inc(sem[f"e_in{j}"], 16)
                sp.dma_start(x[j][:, :, :], dr["x2"](b)).then_inc(sem[f"e_in{j}"], 16)

            def store(b, j):
                sp.wait_ge(sem["e_normed"], b + 1)
                settle()
                sp.dma_start(dr["out"](b), h[j][:, :, :]).then_inc(sem[f"e_stored{j}"], 16)

            def step(s, j):
                if inside(s, -1, B):
                    load(s + 1, 1 - j)
                if inside(s, 1, B):
                    store(s - 1, 1 - j)

            for j in range(2):
                sp.sem_inc(sem[f"e_stored{j}"], 16)
            for tile, n in ((o[:, :], "o1"), (y[:, :], "y_all"), (b2[:, :], "e_b2"), (ident[:, :], "ident"),
                            (wk[:, :, :], "c_wk"), (wv[:, :, :], "c_wv"), (cols[:, :, :], "c_cols"),
                            (wqT[:, :, :], "c_wqT"), (wo[:, :, :], "c_wo"), (bo[:, :], "c_bo")):
                sp.dma_start(tile, dr[n]).then_inc(sem["e_const_in"], 16)
            load(0, 0)
            loop(sp, B, step, 1)
            for j in range(2):
                sp.wait_ge(sem[f"e_stored{j}"], 8 * B + 16)

        rounds = [("a", k, m) for k in range(K4) for m in (0, 2)] + [("cb", 0, m) for m in (0, 2)]\
            + [("vo", b, 0) for b in range(B)]

        @block.tensor
        def _(pe):
            pe.wait_ge(sem["e_const_in"], const_in)
            pe.wait_ge(sem["e_o"], 2)
            for k in range(K4):
                mm = pe.transpose(ps_t[:, 0, k * P:(k + 1) * P], o[:, k * P:(k + 1) * P], ident[:, :])
            mm.then_inc(sem["e_oT_ready"], 1)
            pe.wait_ge(sem["e_oT"], 1)
            for i, w in enumerate((wk, wv)):
                for m in range(K4):
                    for k in range(K4):
                        mm = pe.matmul(ps_s[:, i, m * SB:(m + 1) * SB], w[:, k, m * P:(m + 1) * P], oT[:, k, :],
                                       start=(k == 0), stop=(k == K4 - 1))
                mm.then_inc(sem["e_kv_ready"], 1)
            for r, (kind, n, m) in enumerate(rounds):
                if r == 0:
                    pe.wait_ge(sem["e_kd"], 2 + HQ * K4)
                elif kind == "cb":
                    pe.wait_ge(sem["e_bq"], K4)
                elif kind == "vo" and n == 0:
                    pe.wait_ge(sem["e_kd"], 2 + 2 * HQ * K4)
                if r >= 2:
                    pe.wait_ge(sem[f"e_folded{r % 2}"], r // 2)
                for i in range(2):
                    if kind == "a":
                        mm = pe.matmul(ps_o[r % 2][:, i, :], wqT[:, m + i, n * P:(n + 1) * P],
                                       kd[:, m + i, :, :, :].rearrange("p b h s -> p (b h s)"), start=True, stop=True)
                    elif kind == "cb":
                        mm = pe.matmul(ps_o[r % 2][:, i, :], bq[:, m + i, :],
                                       kd[:, m + i, :, :, :].rearrange("p b h s -> p (b h s)"), start=True, stop=True)
                    else:
                        for c in range(2):
                            mm = pe.matmul(ps_o[r % 2][64 * c:64 * c + 64, i, :],
                                           vd[:, 2 * i + c, n, :, :].rearrange("p h s -> p (h s)"),
                                           wo[:, 2 * i + c, :], start=True, stop=True)
                mm.then_inc(sem["e_fold"], 1)

            def scores(b, j):
                pe.wait_ge(sem[f"e_in{j}"], (b - j) * 16 + 32)
                if not early(b, 1):
                    pe.wait_ge(sem["e_biased"], b)
                for t in range(T4):
                    for k in range(K4):
                        mm = pe.matmul(ps_s[:, t // 2, (t % 2) * HS:(t % 2 + 1) * HS], xT[j][:, k, t * P:(t + 1) * P],
                                       a[:, k, b, :, :].rearrange("p m n -> p (m n)"),
                                       start=(k == 0), stop=(k == K4 - 1))
                mm.then_inc(sem["e_scored"], 1)

            def turn(b, j):
                pe.wait_ge(sem["e_probs"], b + 1)
                if not early(b, 1):
                    pe.wait_ge(sem["e_pt"], b)
                for i in range(2):
                    for t in range(T4):
                        mm = pe.transpose(ps_t[:, i, t * P:(t + 1) * P], sc[j][:, t, i * P:(i + 1) * P], ident[:, :])
                mm.then_inc(sem["e_turned"], 1)

            def mix(b, j):
                pe.wait_ge(sem["e_pt"], b + 1)
                if not early(b, 1):
                    pe.wait_ge(sem["e_summed"], b)
                for t in range(T4):
                    for i in range(2):
                        mm = pe.matmul(ps_o[t // 2][:, t % 2, :], pt[:, i, t * P:(t + 1) * P], vo[:, b, i, :],
                                       start=(i == 0), stop=(i == 1))
                mm.then_inc(sem["e_mixed"], 1)

            def step(s, j):
                if inside(s, 1, B):
                    turn(s - 1, 1 - j)
                if inside(s, 0, B):
                    scores(s, j)
                if inside(s, 1, B):
                    mix(s - 1, 1 - j)

            for j in range(2):
                pe.wait_ge(sem[f"e_folded{j}"], len(rounds) // 2)
            loop(pe, B, step, 1)

        def fold_out(e, parity, copy):
            for r, (kind, n, m) in enumerate(rounds):
                if r % 2 != parity:
                    continue
                e.wait_ge(sem["e_fold"], r + 1)
                src = ps_o[parity][:, :, :]
                if kind == "vo":
                    ins = copy(vo[:, n, :, :], src)
                else:
                    dst = a[:, n, :, m:m + 2, :] if kind == "a" else cb[:, :, m:m + 2, :]
                    for i in range(2):
                        ins = copy(dst[:, :, i, :], src[:, i, :].rearrange("p (b n) -> p b n", b=B))
                ins.then_inc(sem[f"e_folded{parity}"], 1)

        @block.vector
        def _(dve):
            dve.memset(kd[:, :, :, :, :].rearrange("p m b h s -> p (m b h s)"), 0.0).then_inc(sem["e_kd"], 1)
            dve.memset(vd[:, :, :, :, :].rearrange("p m b h s -> p (m b h s)"), 0.0).then_inc(sem["e_kd"], 1)
            dve.memset(eps[:, :], EPS).then_inc(sem["e_eps"], 1)
            dve.wait_ge(sem["e_const_in"], const_in)
            dve.tensor_tensor(o[:, :], o[:, :], y[:, :], ALU.add).then_inc(sem["e_o"], 1)
            dve.wait_ge(sem["e_o"], 1)
            dve.tensor_tensor(o[:, :], o[:, :], b2[:, :], ALU.add).then_inc(sem["e_o"], 1)
            for m in range(K4):
                dve.tensor_copy(bq[:, m, :], cols[:, 0, m:m + 1].to_broadcast([P, P])).then_inc(sem["e_bq"], 1)
            dve.wait_ge(sem["e_oT_ready"], 1)
            dve.tensor_copy(oT[:, :, :].rearrange("p k n -> p (k n)"), ps_t[:, 0, :]).then_inc(sem["e_oT"], 1)
            dve.wait_ge(sem["e_kd"], 2)
            for i, dst in enumerate((kd, vd)):
                dve.wait_ge(sem["e_kv_ready"], i + 1)
                for m in range(K4):
                    for hh in range(HQ):
                        r = slice(D * hh, D * (hh + 1))
                        dve.tensor_scalar(dst[r, m, :, hh, :],
                                          ps_s[r, i, m * SB:(m + 1) * SB].rearrange("p (s b) -> p b s", b=B),
                                          cols[r, 1 + i, m:m + 1], None, ALU.add).then_inc(sem["e_kd"], 1)
            fold_out(dve, 0, lambda d, s: dve.tensor_copy(d, s))

            def groups(j):
                return sc[j][:, :, :].rearrange("p t (h s) -> p (t h) s", s=NS)

            def soft_in(b, j):
                dve.wait_ge(sem["e_scored"], b + 1)
                if not early(b, 2):
                    dve.wait_ge(sem["e_turned"], b - 1)
                for u in range(2):
                    ins = dve.tensor_tensor(sc[j][:, 2 * u:2 * u + 2, :],
                                            ps_s[:, u, :].rearrange("p (t n) -> p t n", t=2),
                                            cb[:, b, :, :].rearrange("p m n -> p (m n)").unsqueeze(1)
                                            .to_broadcast([P, 2, HS]), ALU.add)
                ins.then_inc(sem["e_biased"], 1)
                dve.wait_ge(sem["e_biased"], b + 1)
                dve.tensor_reduce(mx[:, :], groups(j), AX.X, ALU.max).then_inc(sem["e_max"], 1)
                dve.wait_ge(sem["e_max"], b + 1)
                dve.tensor_tensor(groups(j), groups(j), mx[:, :].unsqueeze(2).to_broadcast([P, T4 * H, NS]),
                                  ALU.subtract).then_inc(sem["e_shifted"], 1)

            def soft_out(b, j):
                dve.wait_ge(sem["e_exped"], b + 1)
                dve.tensor_reduce(sm[:, :], groups(j), AX.X, ALU.add).then_inc(sem["e_sum"], 1)
                dve.wait_ge(sem["e_sum"], b + 1)
                dve.reciprocal(inv[:, :], sm[:, :]).then_inc(sem["e_inv"], 1)
                dve.wait_ge(sem["e_inv"], b + 1)
                dve.tensor_tensor(groups(j), groups(j), inv[:, :].unsqueeze(2).to_broadcast([P, T4 * H, NS]),
                                  ALU.mult).then_inc(sem["e_probs"], 1)

            def norm_in(b, j):
                dve.wait_ge(sem["e_mixed"], b + 1)
                dve.wait_ge(sem["e_xb"], b + 1)
                for u in range(2):
                    ins = dve.tensor_tensor(h[j][:, 2 * u:2 * u + 2, :], ps_o[u][:, :, :],
                                            h[j][:, 2 * u:2 * u + 2, :], ALU.add)
                ins.then_inc(sem["e_summed"], 1)
                dve.wait_ge(sem["e_summed"], b + 1)
                for t in range(T4):
                    ins = dve.bn_stats(st[j][:, t, 0:6], h[j][:, t, :])
                ins.then_inc(sem["e_bn"], 1)

            def norm_scales(b, j):
                dve.wait_ge(sem["e_bn"], b + 1)
                dve.sem_inc(sem["e_dve_waited"], 1)
                for t in range(T4):
                    ins = dve.bn_aggr(st[j][:, t, 6:8], st[j][:, t, 0:6])
                ins.then_inc(sem["e_var"], 1)

            def norm_out(b, j):
                s_ = st[j]
                dve.wait_ge(sem["e_std"], b + 1)
                dve.reciprocal(s_[:, :, 9:10], s_[:, :, 8:9]).then_inc(sem["e_rstd"], 1)
                dve.wait_ge(sem["e_rstd"], b + 1)
                for t in range(T4):
                    ins = dve.scalar_tensor_tensor(s_[:, t, 10:11], s_[:, t, 6:7], -1.0, s_[:, t, 9:10],
                                                   ALU.mult, ALU.mult)
                ins.then_inc(sem["e_scales"], 1)

            def step(s, j):
                if inside(s, 0, B):
                    soft_in(s, j)
                    soft_out(s, j)
                if inside(s, 1, B):
                    norm_in(s - 1, 1 - j)
                    norm_scales(s - 1, 1 - j)
                    norm_out(s - 1, 1 - j)

            loop(dve, B, step, 1)

        @block.gpsimd
        def _(pool):
            def step(b, j):
                pool.wait_ge(sem[f"e_in{j}"], (b - j) * 16 + 32)
                pool.wait_ge(sem[f"e_stored{j}"], (b - j) * 8 + 16)
                for t in range(T4):
                    ins = pool.tensor_tensor(h[j][:, t, :], x[j][:, t, :], bo[:, :], ALU.add)
                ins.then_inc(sem["e_xb"], 1)

            pool.wait_ge(sem["e_const_in"], const_in)
            loop(pool, B, step, 0)

        @block.scalar
        def _(act):
            fold_out(act, 1, lambda d, s: act.activation(d, s, ACT.Copy))

            def step(s, j):
                b, i = s - 1, 1 - j
                if inside(s, 1, B):
                    act.wait_ge(sem["e_turned"], b + 1)
                    if not early(b, 1):
                        act.wait_ge(sem["e_mixed"], b)
                    act.activation(pt[:, :, :], ps_t[:, :, :], ACT.Copy).then_inc(sem["e_pt"], 1)
                if inside(s, 0, B):
                    act.wait_ge(sem["e_shifted"], s + 1)
                    act.activation(sc[j][:, :, :], sc[j][:, :, :], ACT.Exp, scale=SCALE_F).then_inc(sem["e_exped"], 1)
                if inside(s, 1, B):
                    act.wait_ge(sem["e_var"], b + 1)
                    act.activation(st[i][:, :, 8:9], st[i][:, :, 7:8], ACT.Sqrt, bias=eps[:, :])\
                       .then_inc(sem["e_std"], 1)
                    act.wait_ge(sem["e_scales"], b + 1)
                    for t in range(T4):
                        ins = act.activation(h[i][:, t, :], h[i][:, t, :], ACT.Identity, bias=st[i][:, t, 10:11],
                                             scale=st[i][:, t, 9:10])
                    ins.then_inc(sem["e_normed"], 1)

            act.wait_ge(sem["e_eps"], 1)
            loop(act, B, step, 1)


E_SEMS = ["e_" + n for n in ["sp_waited", "dve_waited", "scored", "xb", "in0", "in1", "normed", "stored0", "stored1",
                             "const_in", "o", "oT_ready", "oT", "kv_ready", "kd", "bq", "folded0", "folded1", "fold",
                             "biased", "probs", "pt", "turned", "summed", "mixed", "eps", "max", "shifted", "exped",
                             "sum", "inv", "bn", "var", "std", "rstd", "scales"]]


def ffn_views(nc, t, x2, x2T, out):
    w = lambda n: t[n].rearrange("(k p) n -> p k n", p=P)
    rows = lambda n: bass.AP(tensor=t[n].tensor, offset=0, ap=[[E, NS], [0, B], [1, E]])
    o1 = nc.dram_tensor("o1", (SB, E), F32).ap()
    hT = nc.dram_tensor("hT", (P, K4, SB), F32).ap()
    y = nc.dram_tensor("y", (NS, B, E), F32).ap()
    bc = lambda n: t[n].partition_broadcast(P)
    return {
        "ident": t["ident"], "d_wq": w("d_Wq"), "d_wkT": w("d_WkT"), "d_wv": w("d_Wv"), "d_wo": w("d_Wo"),
        "sqT": t["sqT"].rearrange("(k p) s -> p k s", p=P), "d_cols": t["d_cols"], "slots": rows("slots"),
        "d_bo": bc("d_bo"), "e_g": rows("e_ln_g"), "e_b": rows("e_ln_b"),
        "x2T": lambda b: x2T[b].rearrange("(k p) s -> p k s", p=P),
        "x2": lambda b: x2[b].rearrange("(t p) e -> p t e", p=P),
        "o1": o1, "hT": hT, "e_bias": t["e_bias"],
        "w1": lambda e: t["e_W1"][e].rearrange("(k p) f -> p k f", p=P),
        "wg": lambda e: t["e_Wg"][e].rearrange("(k p) f -> p k f", p=P),
        "w2": lambda e: t["e_W2"][e].rearrange("(c p) n -> p c n", p=P),
        "y": lambda e: y[e], "y_all": y.rearrange("s b e -> (s b) e"), "e_b2": rows("e_b2"),
        "c_wqT": w("c_WqT"), "c_wk": w("c_Wk"), "c_wv": w("c_Wv"), "c_wo": w("c_Wo"), "c_cols": t["c_cols"],
        "c_bo": bc("c_bo"), "out": lambda b: out[b].rearrange("(t p) e -> p t e", p=P),
    }

def attention_views(nc, t, x1T):
    chunks = lambda ap: ap.rearrange("(k p) n -> p k n", p=P)
    group = lambda n, per: (lambda q: chunks(t[n][q % per]))
    batch = lambda ap, per: (lambda q: chunks(ap[q // per]))
    scratch = lambda name, shape: nc.dram_tensor(name, shape, F32).ap()
    col = lambda ap: (lambda u: ap[u // T4].rearrange("(k p) (t n) -> t p k n", p=P, n=P)[u % T4])
    tok = lambda ap: (lambda u: ap.rearrange("b (t p) e -> (b t) p e", p=P)[u])
    bc = lambda ap: ap.partition_broadcast(P)
    ctx1, ctx2 = scratch("ctx1", (QUADS, P, S)), scratch("ctx2", (PAIRS, P, S))
    x1, x2, x2T = (scratch(n, (B, S, E)) for n in ("x1", "x2", "x2T"))
    whole = lambda ap: ap.rearrange("(b m) p s -> b (m p) s", b=B)
    dr = {
        "ident": t["ident"], "emask": t["emask"], "dist_rev": t["dist_rev"], "dist_fwd": t["dist_fwd"],
        "xT": batch(t["xT"], QUADS // B), "a_bqk": lambda q: t["a_bqk"][q % (QUADS // B)],
        "a_bv": lambda q: bc(t["a_bv"][q % (QUADS // B)]),
        "a_band_q": scratch("band_q", (2, NT, P * WIN)),
        "a_band_k": scratch("band_k", (2, NT, P * WIN)), "a_ctxT": lambda q: ctx1[q],
        "na_wo": chunks(t["attn_Wo"]), "na_bo": bc(t["attn_bo"]), "gamma": bc(t["attn_ln_gamma"]),
        "beta": bc(t["attn_ln_beta"]), "na_cT": col(whole(ctx1)), "na_x": tok(t["x"]), "na_y": tok(x1),
        "na_yT": col(x1T),
        "mask": t["mask"], "x1T": batch(x1T, PAIRS // B), "ctxT": batch(t["ctxT"], PAIRS // B),
        "b_bqk": lambda q: t["b_bqk"][q % (PAIRS // B)], "b_bv": lambda q: bc(t["b_bv"][q % (PAIRS // B)]),
        "b_cxT": lambda q: ctx2[q],
        "nb_wo": chunks(t["xattn_Wo"]), "nb_bo": bc(t["xattn_bo"]), "nb_cT": col(whole(ctx2)), "nb_x": tok(x1),
        "nb_y": tok(x2), "nb_yT": col(x2T),
    }
    for n in "qkv":
        dr["a_w" + n] = group("a_w" + n, QUADS // B)
        dr["b_w" + n] = group("b_w" + n, PAIRS // B)
    return dr, x2, x2T


def program(nc, t, out):
    def run(phase, names, *more):
        sems = {n: nc.alloc_semaphore(n) for n in names}
        phase(nc, dr, sems, *more)
        nc.clear_and_free_semaphores(list(sems.values()))
        nc.all_engine_barrier()

    x1T = nc.dram_tensor("x1T", (B, E, S), F32).ap()
    dr, x2, x2T = attention_views(nc, t, x1T)
    dr.update(ffn_views(nc, t, x2, x2T, out))
    run(self_attention, A_SEMS)
    run(project_norm, norm_sems("na_"), "na_", K4, True)
    run(cross_attention, B_SEMS)
    run(project_norm, norm_sems("nb_"), "nb_", 2 * K4, False)
    run(slot_attention, C_SEMS)
    run(experts, D_SEMS)
    run(slots_to_tokens, E_SEMS)


def kernel(**inputs):
    import numpy as np
    import concourse.bacc as _bacc
    from concourse.bass_utils import run_bass_kernel_spmd as _run
    nc = _bacc.Bacc("TRN2", target_bir_lowering=False, num_devices=1)
    a = {}
    c = np.ascontiguousarray
    i = {k: np.asarray(v) for k, v in inputs.items()}
    a["x"] = i["x"]
    a["xT"] = c(i["x"].transpose(0, 2, 1))
    a["ctxT"] = c(i["ctx_1024"].transpose(0, 2, 1))
    for n in "qkv":
        a[f"a_w{n}"] = c(i[f"L0_attn_W{n}"].reshape(E, E // P, P).transpose(1, 0, 2))
        a[f"b_w{n}"] = c(i[f"L0_xattn_W{n}"].reshape(-1, 2, E, KD).transpose(0, 2, 1, 3).reshape(-1, E, P))
    for z, layer in (("a", "attn"), ("b", "xattn")):
        a[z + "_bqk"] = c(np.stack([i[f"L0_{layer}_b{n}"].reshape(-1, P) for n in "qk"], axis=2))
        a[z + "_bv"] = c(i[f"L0_{layer}_bv"].reshape(-1, P))
    for n in ("attn_Wo", "attn_bo", "attn_ln_gamma", "attn_ln_beta", "xattn_Wo", "xattn_bo"):
        a[n] = i["L0_" + n]
    table = i["L0_attn_dist_emb"]
    for n, rows in (("dist_fwd", table), ("dist_rev", table[::-1])):
        d = np.zeros((1024, D), np.float32)
        d[:1023] = rows
        a[n] = c(np.tile(d.T, (4, 1)))
    block = np.arange(P) // D
    a["emask"] = c(np.stack([block < 2, block % 2 == 0], axis=1).astype(np.float32))
    a["ident"] = np.eye(P, dtype=np.float32)
    mask = np.zeros((P, S), np.float32)
    mask[:, S - P:] = np.where(np.tril(np.ones((P, P), bool)), 0.0, -1e30)
    a["mask"] = mask
    for n in ("d_Wq", "d_Wv", "d_Wo", "c_Wk", "c_Wv", "c_Wo"):
        a[n] = i["L0_ffn_" + n]
    for n in ("d_Wk", "c_Wq"):
        a[n + "T"] = c(i["L0_ffn_" + n].T)
    for z in "dc":
        a[z + "_cols"] = c(np.stack([i[f"L0_ffn_{z}_b{n}"].reshape(4, P) for n in "qkv"]).transpose(2, 0, 1))
        a[z + "_bo"] = i[f"L0_ffn_{z}_bo"]
    a["slots"] = c(i["L0_ffn_slot_query"][0])
    a["sqT"] = c(i["L0_ffn_slot_query"][0].T)
    for n in ("e_ln_g", "e_ln_b", "e_b2", "e_W1", "e_Wg", "e_W2"):
        a[n] = i["L0_ffn_" + n]
    a["e_bias"] = c(np.stack([i["L0_ffn_e_b1"], i["L0_ffn_e_bg"]], axis=1)
                    .reshape(NS, 2, FQ, 4, P).transpose(4, 0, 1, 3, 2).reshape(P, NS, 2, FC))
    t = {n: nc.dram_tensor(f"in_{n}", x.shape, mybir.dt.from_np(x.dtype), kind="ExternalInput").ap() for n, x in a.items()}
    out = nc.dram_tensor("out0", (B, S, E), F32, kind="ExternalOutput").ap()
    program(nc, t, out)
    r = _run(nc, [{f"in_{n}": x for n, x in a.items()}], core_ids=[0])
    return r.results[0]["out0"]
```
